# Optimizing a Trainium2 kernel written in Bass

```python
import numpy as np
import jax
import jax.numpy as jnp

def _softmax(x, axis=-1):
    return jax.nn.softmax(x, axis=axis)

def _gelu(x):
    return jax.nn.gelu(x, approximate=True)

def _silu(x):
    return jax.nn.silu(x)

def _sigmoid(x):
    return jax.nn.sigmoid(x)

def _layernorm(x, axis=-1, eps=1e-05):
    m = jnp.mean(x, axis=axis, keepdims=True)
    v = jnp.var(x, axis=axis, keepdims=True)
    return (x - m) / jnp.sqrt(v + eps)

def _scatter_add(tgt, idx, src, axis=0):
    return tgt.at[idx].add(src)

def _segment_sum(src, seg, n):
    return jax.ops.segment_sum(src, seg, n)
kernel_name = 'mk_conv_attn_hybrid_d4_conv_nchw512_r4_ca5826'

def setup_inputs(seed: int=0):
    np.random.seed(seed)
    _w = jnp.asarray

    def _rec_inputs():
        import jax
        import jax.numpy as jnp
        _gk = jax.random.key(seed)
        x = -0.0002928 + 1 * jax.random.normal(jax.random.fold_in(_gk, 1), (4, 128, 16, 32), jnp.float32)
        return x
    x = _rec_inputs()

    def _L0_conv_setup():
        import jax, jax.numpy as jnp
        import numpy as np
        HEADS = 8
        EPS = 1e-05

        def _layernorm(x, gamma, beta):
            mu = jnp.mean(x, axis=-1, keepdims=True)
            var = jnp.var(x, axis=-1, keepdims=True)
            return (x - mu) * jax.lax.rsqrt(var + EPS) * gamma + beta
        key = jax.random.key(seed)
        ks = jax.random.split(key, 4)
        dim = 128
        x = jax.random.normal(ks[0], (4, dim, 16, 32), dtype=jnp.float32)
        w_qkv = jax.random.normal(ks[1], (dim, 3 * dim), dtype=jnp.float32) * dim ** (-0.5)
        b_qkv = jnp.zeros((3 * dim,), jnp.float32)
        w_out = jax.random.normal(ks[2], (dim, dim), dtype=jnp.float32) * dim ** (-0.5)
        b_out = jnp.zeros((dim,), jnp.float32)
        gamma1 = jnp.ones((dim,), jnp.float32)
        beta1 = jnp.zeros((dim,), jnp.float32)
        gamma2 = jnp.ones((dim,), jnp.float32)
        beta2 = jnp.zeros((dim,), jnp.float32)
        return {'x': x, 'w_qkv': w_qkv, 'b_qkv': b_qkv, 'w_out': w_out, 'b_out': b_out, 'gamma1': gamma1, 'beta1': beta1, 'gamma2': gamma2, 'beta2': beta2}
    _L0_conv_all = _L0_conv_setup()
    _L0_conv_in = {k: v for k, v in _L0_conv_all.items() if k in ('w_qkv', 'b_qkv', 'w_out', 'b_out', 'gamma1', 'beta1', 'gamma2', 'beta2')}
    del _L0_conv_all

    def _L1_conv_setup():
        import jax, jax.numpy as jnp
        import numpy as np
        FREQ_DIM = 32
        TIME_DIM = 32
        HEADS = 8
        TWO_PI = 6.283185307179586

        def get_embeddings(B, H, W, freq_dim, time_dim, dtype):
            nf = freq_dim // 2
            ln_x = jnp.log2(jnp.arange(0, H * nf, dtype=jnp.float32))
            ln_x = ln_x.at[0].set(-2.0)
            ln_x = ln_x.reshape(H, nf).T
            ln_x = ln_x * jnp.arange(1, nf + 1, dtype=jnp.float32)[:, None]
            freq = jnp.stack([jnp.cos(ln_x), jnp.sin(ln_x)], axis=1).reshape(freq_dim, H)
            freq = jnp.broadcast_to(freq[None, :, :, None], (B, freq_dim, H, W))
            nt = time_dim // 2
            k = jnp.arange(0, nt, dtype=jnp.float32) + 0.5
            x = jnp.arange(0, nt * W, dtype=jnp.float32).reshape(W, nt).T
            theta = k[:, None] * x / (W * nt) * TWO_PI
            time = jnp.stack([jnp.cos(theta), jnp.sin(theta)], axis=1).reshape(time_dim, W)
            time = jnp.broadcast_to(time[None, :, None, :], (B, time_dim, H, W))
            return jnp.concatenate([freq, time], axis=1).astype(dtype)
        key = jax.random.key(seed)
        ks = jax.random.split(key, 6)
        B, C, H, W = (2, 128, 16, 32)
        qkC = C + FREQ_DIM + TIME_DIM
        inner = HEADS * 16
        return {'hidden_states': jax.random.normal(ks[0], (B, C, H, W), dtype=jnp.float32), 'Wq': jax.random.normal(ks[1], (qkC, inner), dtype=jnp.float32) * 0.02, 'Wk': jax.random.normal(ks[2], (qkC, inner), dtype=jnp.float32) * 0.02, 'Wv': jax.random.normal(ks[3], (C, inner), dtype=jnp.float32) * 0.02, 'Wout': jax.random.normal(ks[4], (inner, C), dtype=jnp.float32) * 0.02, 'bout': jnp.zeros((C,), dtype=jnp.float32)}
    _L1_conv_all = _L1_conv_setup()
    _L1_conv_in = {k: v for k, v in _L1_conv_all.items() if k in ('Wq', 'Wk', 'Wv', 'Wout', 'bout')}
    del _L1_conv_all

    def _L2_attn_setup():
        import jax, jax.numpy as jnp
        import numpy as np
        EMBED_DIM = 128
        N_HEADS = 8
        HEAD_DIM = EMBED_DIM // N_HEADS
        SEQ = 1024
        BATCH = 2
        key = jax.random.key(seed)
        k1, k2, k3 = jax.random.split(key, 3)
        x = jax.random.normal(k1, (SEQ, BATCH, EMBED_DIM), dtype=jnp.float32)
        lim_in = float(np.sqrt(6.0 / (3 * EMBED_DIM + EMBED_DIM)))
        in_proj_weight = jax.random.uniform(k2, (3 * EMBED_DIM, EMBED_DIM), minval=-lim_in, maxval=lim_in, dtype=jnp.float32)
        in_proj_bias = jnp.zeros((3 * EMBED_DIM,), jnp.float32)
        lim_out = float(np.sqrt(1.0 / EMBED_DIM))
        out_weight = jax.random.uniform(k3, (EMBED_DIM, EMBED_DIM), minval=-lim_out, maxval=lim_out, dtype=jnp.float32)
        out_bias = jnp.zeros((EMBED_DIM,), jnp.float32)
        return {'x': x, 'in_proj_weight': in_proj_weight, 'in_proj_bias': in_proj_bias, 'out_weight': out_weight, 'out_bias': out_bias}
    _L2_attn_all = _L2_attn_setup()
    _L2_attn_in = {k: v for k, v in _L2_attn_all.items() if k in ('in_proj_weight', 'in_proj_bias', 'out_weight', 'out_bias')}
    del _L2_attn_all

    def _L2_ffn_setup():
        import jax, jax.numpy as jnp
        import numpy as np
        STEP_SIZE = 0.1

        def _mlp(y, W1, b1, W2, b2, W3, b3):
            h = jnp.tanh(y @ W1.T + b1)
            h = jnp.tanh(h @ W2.T + b2)
            return h @ W3.T + b3

        def _rk4_step(y, dt, params):
            f = lambda z: _mlp(z, *params)
            k1 = f(y)
            k2 = f(y + dt / 2 * k1)
            k3 = f(y + dt / 2 * k2)
            k4 = f(y + dt * k3)
            return y + dt * (k1 + 2 * k2 + 2 * k3 + k4) / 6
        key = jax.random.key(seed)
        ks = jax.random.split(key, 7)
        B, S, D, H = (64, 16, 128, 512)
        return {'x': jax.random.normal(ks[0], (B, S, D), dtype=jnp.float32), 'W1': jax.random.normal(ks[1], (H, D), dtype=jnp.float32) * (1.0 / np.sqrt(D)), 'b1': jax.random.normal(ks[2], (H,), dtype=jnp.float32) * 0.01, 'W2': jax.random.normal(ks[3], (H, H), dtype=jnp.float32) * (1.0 / np.sqrt(H)), 'b2': jax.random.normal(ks[4], (H,), dtype=jnp.float32) * 0.01, 'W3': jax.random.normal(ks[5], (D, H), dtype=jnp.float32) * (1.0 / np.sqrt(H)), 'b3': jax.random.normal(ks[6], (D,), dtype=jnp.float32) * 0.01}
    _L2_ffn_all = _L2_ffn_setup()
    _L2_ffn_in = {k: v for k, v in _L2_ffn_all.items() if k in ('W1', 'b1', 'W2', 'b2', 'W3', 'b3')}
    del _L2_ffn_all

    def _L3_attn_setup():
        import jax, jax.numpy as jnp
        import numpy as np
        import math
        BS, SEQ, EMBED = (1, 512, 128)
        N_HEADS, FEAT = (8, 16)
        W, DILATION = (32, 4)
        key = jax.random.key(seed)
        ks = jax.random.split(key, 8)
        s = 0.02
        return {'x': jax.random.normal(ks[0], (BS, SEQ, EMBED), dtype=jnp.float32), 'Wq': jax.random.normal(ks[1], (EMBED, N_HEADS * FEAT), dtype=jnp.float32) * s, 'Wk': jax.random.normal(ks[2], (EMBED, N_HEADS * FEAT), dtype=jnp.float32) * s, 'Wv': jax.random.normal(ks[3], (EMBED, N_HEADS * FEAT), dtype=jnp.float32) * s, 'Wff1': jax.random.normal(ks[4], (EMBED, EMBED), dtype=jnp.float32) * s, 'bff1': jnp.zeros((EMBED,), dtype=jnp.float32), 'Wff2': jax.random.normal(ks[5], (EMBED, EMBED), dtype=jnp.float32) * s, 'bff2': jnp.zeros((EMBED,), dtype=jnp.float32)}
    _L3_attn_all = _L3_attn_setup()
    _L3_attn_in = {k: v for k, v in _L3_attn_all.items() if k in ('Wq', 'Wk', 'Wv', 'Wff1', 'bff1', 'Wff2', 'bff2')}
    del _L3_attn_all

    def _L3_ffn_setup():
        import jax, jax.numpy as jnp
        import numpy as np
        GRID_SIZE = 5
        SPLINE_ORDER = 3
        NUM_EXPERTS = 8
        TOP_K = 2
        HIDDEN = 128
        D_FF = 256
        N_BASES = GRID_SIZE + SPLINE_ORDER

        def _grid():
            h = 2.0 / GRID_SIZE
            g = jnp.arange(-SPLINE_ORDER, GRID_SIZE + SPLINE_ORDER + 1, dtype=jnp.float32) * h - 1.0
            return g[None, :]

        def b_splines(x, grid):
            xe = x[..., None]
            bases = ((xe >= grid[:, :-1]) & (xe < grid[:, 1:])).astype(x.dtype)
            for j in range(1, SPLINE_ORDER + 1):
                left = (xe - grid[:, :-(j + 1)]) / (grid[:, j:-1] - grid[:, :-(j + 1)])
                right = (grid[:, j + 1:] - xe) / (grid[:, j + 1:] - grid[:, 1:-j])
                bases = left * bases[..., :-1] + right * bases[..., 1:]
            return bases

        def kan_linear(x, base_w, spline_w, scaler, grid):
            base = jax.nn.silu(x) @ base_w.T
            sb = b_splines(x, grid)
            spline = jnp.einsum('nic,oic->no', sb, spline_w * scaler[..., None])
            return base + spline

        def expert_ffn(x, b1, s1, c1, b2, s2, c2, b3, s3, c3, gh, gf):
            h1 = kan_linear(x, b1, s1, c1, gh)
            h2 = kan_linear(x, b2, s2, c2, gh)
            return kan_linear(h1 * h2, b3, s3, c3, gf)
        key = jax.random.key(seed)
        ks = jax.random.split(key, 8)
        x = jax.random.normal(ks[0], (2, 256, HIDDEN), dtype=jnp.float32)
        gate_w = jax.random.normal(ks[1], (NUM_EXPERTS, HIDDEN), dtype=jnp.float32) * HIDDEN ** (-0.5)
        base_w1 = jax.random.normal(ks[2], (NUM_EXPERTS, D_FF, HIDDEN), dtype=jnp.float32) * HIDDEN ** (-0.5)
        spline_w1 = jax.random.normal(ks[3], (NUM_EXPERTS, D_FF, HIDDEN, N_BASES), dtype=jnp.float32) * 0.02
        scaler_w1 = jnp.ones((NUM_EXPERTS, D_FF, HIDDEN), dtype=jnp.float32)
        base_w2 = jax.random.normal(ks[4], (NUM_EXPERTS, D_FF, HIDDEN), dtype=jnp.float32) * HIDDEN ** (-0.5)
        spline_w2 = jax.random.normal(ks[5], (NUM_EXPERTS, D_FF, HIDDEN, N_BASES), dtype=jnp.float32) * 0.02
        scaler_w2 = jnp.ones((NUM_EXPERTS, D_FF, HIDDEN), dtype=jnp.float32)
        base_w3 = jax.random.normal(ks[6], (NUM_EXPERTS, HIDDEN, D_FF), dtype=jnp.float32) * D_FF ** (-0.5)
        spline_w3 = jax.random.normal(ks[7], (NUM_EXPERTS, HIDDEN, D_FF, N_BASES), dtype=jnp.float32) * 0.02
        scaler_w3 = jnp.ones((NUM_EXPERTS, HIDDEN, D_FF), dtype=jnp.float32)
        return {'x': x, 'gate_w': gate_w, 'base_w1': base_w1, 'spline_w1': spline_w1, 'scaler_w1': scaler_w1, 'base_w2': base_w2, 'spline_w2': spline_w2, 'scaler_w2': scaler_w2, 'base_w3': base_w3, 'spline_w3': spline_w3, 'scaler_w3': scaler_w3}
    _L3_ffn_all = _L3_ffn_setup()
    _L3_ffn_in = {k: v for k, v in _L3_ffn_all.items() if k in ('gate_w', 'base_w1', 'spline_w1', 'scaler_w1', 'base_w2', 'spline_w2', 'scaler_w2', 'base_w3', 'spline_w3', 'scaler_w3')}
    del _L3_ffn_all
    return {'x': x, 'L0_conv_w_qkv': _L0_conv_in['w_qkv'], 'L0_conv_b_qkv': _L0_conv_in['b_qkv'], 'L0_conv_w_out': _L0_conv_in['w_out'], 'L0_conv_b_out': _L0_conv_in['b_out'], 'L0_conv_gamma1': _L0_conv_in['gamma1'], 'L0_conv_beta1': _L0_conv_in['beta1'], 'L0_conv_gamma2': _L0_conv_in['gamma2'], 'L0_conv_beta2': _L0_conv_in['beta2'], 'L1_conv_Wq': _L1_conv_in['Wq'], 'L1_conv_Wk': _L1_conv_in['Wk'], 'L1_conv_Wv': _L1_conv_in['Wv'], 'L1_conv_Wout': _L1_conv_in['Wout'], 'L1_conv_bout': _L1_conv_in['bout'], 'L2_attn_in_proj_weight': _L2_attn_in['in_proj_weight'], 'L2_attn_in_proj_bias': _L2_attn_in['in_proj_bias'], 'L2_attn_out_weight': _L2_attn_in['out_weight'], 'L2_attn_out_bias': _L2_attn_in['out_bias'], 'L2_ffn_W1': _L2_ffn_in['W1'], 'L2_ffn_b1': _L2_ffn_in['b1'], 'L2_ffn_W2': _L2_ffn_in['W2'], 'L2_ffn_b2': _L2_ffn_in['b2'], 'L2_ffn_W3': _L2_ffn_in['W3'], 'L2_ffn_b3': _L2_ffn_in['b3'], 'L3_attn_Wq': _L3_attn_in['Wq'], 'L3_attn_Wk': _L3_attn_in['Wk'], 'L3_attn_Wv': _L3_attn_in['Wv'], 'L3_attn_Wff1': _L3_attn_in['Wff1'], 'L3_attn_bff1': _L3_attn_in['bff1'], 'L3_attn_Wff2': _L3_attn_in['Wff2'], 'L3_attn_bff2': _L3_attn_in['bff2'], 'L3_ffn_gate_w': _L3_ffn_in['gate_w'], 'L3_ffn_base_w1': _L3_ffn_in['base_w1'], 'L3_ffn_spline_w1': _L3_ffn_in['spline_w1'], 'L3_ffn_scaler_w1': _L3_ffn_in['scaler_w1'], 'L3_ffn_base_w2': _L3_ffn_in['base_w2'], 'L3_ffn_spline_w2': _L3_ffn_in['spline_w2'], 'L3_ffn_scaler_w2': _L3_ffn_in['scaler_w2'], 'L3_ffn_base_w3': _L3_ffn_in['base_w3'], 'L3_ffn_spline_w3': _L3_ffn_in['spline_w3'], 'L3_ffn_scaler_w3': _L3_ffn_in['scaler_w3']}

def reference(x, L0_conv_w_qkv, L0_conv_b_qkv, L0_conv_w_out, L0_conv_b_out, L0_conv_gamma1, L0_conv_beta1, L0_conv_gamma2, L0_conv_beta2, L1_conv_Wq, L1_conv_Wk, L1_conv_Wv, L1_conv_Wout, L1_conv_bout, L2_attn_in_proj_weight, L2_attn_in_proj_bias, L2_attn_out_weight, L2_attn_out_bias, L2_ffn_W1, L2_ffn_b1, L2_ffn_W2, L2_ffn_b2, L2_ffn_W3, L2_ffn_b3, L3_attn_Wq, L3_attn_Wk, L3_attn_Wv, L3_attn_Wff1, L3_attn_bff1, L3_attn_Wff2, L3_attn_bff2, L3_ffn_gate_w, L3_ffn_base_w1, L3_ffn_spline_w1, L3_ffn_scaler_w1, L3_ffn_base_w2, L3_ffn_spline_w2, L3_ffn_scaler_w2, L3_ffn_base_w3, L3_ffn_spline_w3, L3_ffn_scaler_w3):
    import jax
    import jax.numpy as jnp

    def _L0_conv_ref(x, w_qkv, b_qkv, w_out, b_out, gamma1, beta1, gamma2, beta2):
        import jax, jax.numpy as jnp
        import numpy as np
        HEADS = 8
        EPS = 1e-05

        def _layernorm(x, gamma, beta):
            mu = jnp.mean(x, axis=-1, keepdims=True)
            var = jnp.var(x, axis=-1, keepdims=True)
            return (x - mu) * jax.lax.rsqrt(var + EPS) * gamma + beta
        b, c, f, t = x.shape
        h = HEADS
        dh = c // h
        scale = dh ** (-0.5)
        xp = jnp.transpose(x, (0, 2, 3, 1))
        xn = _layernorm(xp, gamma1, beta1)
        qkv = xn @ w_qkv + b_qkv
        q, k, v = jnp.split(qkv, 3, axis=-1)

        def to_heads(u):
            return jnp.transpose(u.reshape(b, f * t, h, dh), (0, 2, 1, 3))
        q, k, v = (to_heads(q), to_heads(k), to_heads(v))
        scores = jnp.einsum('bhqd,bhkd->bhqk', q, k) * scale
        attn = jax.nn.softmax(scores, axis=-1)
        o = jnp.einsum('bhqk,bhkd->bhqd', attn, v)
        o = jnp.transpose(o, (0, 2, 1, 3)).reshape(b, f, t, c)
        o = _layernorm(o, gamma2, beta2)
        o = o @ w_out + b_out
        o = o + xn
        return jnp.transpose(o, (0, 3, 1, 2))

    def _L1_conv_ref(hidden_states, Wq, Wk, Wv, Wout, bout):
        import jax, jax.numpy as jnp
        import numpy as np
        FREQ_DIM = 32
        TIME_DIM = 32
        HEADS = 8
        TWO_PI = 6.283185307179586

        def get_embeddings(B, H, W, freq_dim, time_dim, dtype):
            nf = freq_dim // 2
            ln_x = jnp.log2(jnp.arange(0, H * nf, dtype=jnp.float32))
            ln_x = ln_x.at[0].set(-2.0)
            ln_x = ln_x.reshape(H, nf).T
            ln_x = ln_x * jnp.arange(1, nf + 1, dtype=jnp.float32)[:, None]
            freq = jnp.stack([jnp.cos(ln_x), jnp.sin(ln_x)], axis=1).reshape(freq_dim, H)
            freq = jnp.broadcast_to(freq[None, :, :, None], (B, freq_dim, H, W))
            nt = time_dim // 2
            k = jnp.arange(0, nt, dtype=jnp.float32) + 0.5
            x = jnp.arange(0, nt * W, dtype=jnp.float32).reshape(W, nt).T
            theta = k[:, None] * x / (W * nt) * TWO_PI
            time = jnp.stack([jnp.cos(theta), jnp.sin(theta)], axis=1).reshape(time_dim, W)
            time = jnp.broadcast_to(time[None, :, None, :], (B, time_dim, H, W))
            return jnp.concatenate([freq, time], axis=1).astype(dtype)
        B, C, H, W = hidden_states.shape
        emb = get_embeddings(B, H, W, FREQ_DIM, TIME_DIM, hidden_states.dtype)
        qk_hs = jnp.concatenate([hidden_states, emb], axis=1)
        S = H * W
        qk_hs = qk_hs.reshape(B, -1, S).transpose(0, 2, 1)
        v_hs = hidden_states.reshape(B, C, S).transpose(0, 2, 1)
        q = qk_hs @ Wq
        k = qk_hs @ Wk
        v = v_hs @ Wv
        hd_qk = q.shape[-1] // HEADS
        hd_v = v.shape[-1] // HEADS
        q = q.reshape(B, S, HEADS, hd_qk).transpose(0, 2, 1, 3)
        k = k.reshape(B, S, HEADS, hd_qk).transpose(0, 2, 1, 3)
        v = v.reshape(B, S, HEADS, hd_v).transpose(0, 2, 1, 3)
        scale = 1.0 / jnp.sqrt(jnp.asarray(hd_qk, dtype=q.dtype))
        scores = jnp.einsum('bhqd,bhkd->bhqk', q, k) * scale
        attn = jax.nn.softmax(scores, axis=-1)
        o = jnp.einsum('bhqk,bhkd->bhqd', attn, v)
        o = o.transpose(0, 2, 1, 3).reshape(B, S, HEADS * hd_v)
        o = o @ Wout + bout
        o = o.transpose(0, 2, 1).reshape(B, C, H, W)
        return o + hidden_states

    def _L2_attn_ref(x, in_proj_weight, in_proj_bias, out_weight, out_bias):
        import jax, jax.numpy as jnp
        import numpy as np
        EMBED_DIM = 128
        N_HEADS = 8
        HEAD_DIM = EMBED_DIM // N_HEADS
        SEQ = 1024
        BATCH = 2
        S, B, E = x.shape
        H, D = (N_HEADS, HEAD_DIM)
        scaling = 1.0 / D ** 0.5
        qkv = x @ in_proj_weight.T + in_proj_bias
        q, k, v = jnp.split(qkv, 3, axis=-1)

        def to_bh(t):
            return t.reshape(S, B * H, D).transpose(1, 0, 2)
        q = to_bh(q * scaling)
        k = to_bh(k)
        v = to_bh(v)
        scores = jnp.einsum('bqd,bkd->bqk', q, k)
        attn = jax.nn.softmax(scores, axis=-1)
        out = jnp.einsum('bqk,bkd->bqd', attn, v)
        out = out.transpose(1, 0, 2).reshape(S, B, E)
        return out @ out_weight.T + out_bias

    def _L2_ffn_ref(x, W1, b1, W2, b2, W3, b3):
        import jax, jax.numpy as jnp
        import numpy as np
        STEP_SIZE = 0.1

        def _mlp(y, W1, b1, W2, b2, W3, b3):
            h = jnp.tanh(y @ W1.T + b1)
            h = jnp.tanh(h @ W2.T + b2)
            return h @ W3.T + b3

        def _rk4_step(y, dt, params):
            f = lambda z: _mlp(z, *params)
            k1 = f(y)
            k2 = f(y + dt / 2 * k1)
            k3 = f(y + dt / 2 * k2)
            k4 = f(y + dt * k3)
            return y + dt * (k1 + 2 * k2 + 2 * k3 + k4) / 6
        B, S, D = x.shape
        params = (W1, b1, W2, b2, W3, b3)
        span = 1.0 / (S - 1)
        steps = max(1, int(span / STEP_SIZE))
        dt = span / steps

        def interval(y, _):
            for _s in range(steps):
                y = _rk4_step(y, dt, params)
            return (y, y)
        y0 = x[:, 0]
        _, ys = jax.lax.scan(interval, y0, None, length=S - 1)
        return jnp.concatenate([y0[:, None], jnp.moveaxis(ys, 0, 1)], axis=1)

    def _L3_attn_ref(x, Wq, Wk, Wv, Wff1, bff1, Wff2, bff2):
        import jax, jax.numpy as jnp
        import numpy as np
        import math
        BS, SEQ, EMBED = (1, 512, 128)
        N_HEADS, FEAT = (8, 16)
        W, DILATION = (32, 4)
        bs, seq, embed = x.shape
        sqrt_d = math.sqrt(FEAT)

        def proj_heads(W):
            h = jnp.einsum('bse,ef->bsf', x, W)
            return h.reshape(bs, seq, N_HEADS, FEAT).transpose(0, 2, 1, 3)
        q = proj_heads(Wq)
        k = proj_heads(Wk)
        v = proj_heads(Wv)
        pad = W * DILATION
        pad_k = jnp.pad(k, ((0, 0), (0, 0), (pad, pad), (0, 0)))
        pad_v = jnp.pad(v, ((0, 0), (0, 0), (pad, pad), (0, 0)))
        idx = jnp.arange(seq)[:, None] + jnp.arange(0, 2 * W * DILATION + 1, DILATION)[None, :]
        diag_k = pad_k[:, :, idx, :]
        attn = jnp.einsum('bhsf,bhskf->bhsk', q, diag_k)
        attn = jax.nn.softmax(attn, axis=-1) / sqrt_d
        diag_v = pad_v[:, :, idx, :]
        ctx = jnp.einsum('bhsk,bhskf->bhsf', attn, diag_v)
        x_attn = ctx.transpose(0, 2, 1, 3).reshape(bs, seq, embed)
        f = jax.nn.relu(x_attn @ Wff1 + bff1)
        g = jax.nn.relu(f @ Wff2 + bff2)
        return x_attn + g

    def _L3_ffn_ref(x, gate_w, base_w1, spline_w1, scaler_w1, base_w2, spline_w2, scaler_w2, base_w3, spline_w3, scaler_w3):
        import jax, jax.numpy as jnp
        import numpy as np
        GRID_SIZE = 5
        SPLINE_ORDER = 3
        NUM_EXPERTS = 8
        TOP_K = 2
        HIDDEN = 128
        D_FF = 256
        N_BASES = GRID_SIZE + SPLINE_ORDER

        def _grid():
            h = 2.0 / GRID_SIZE
            g = jnp.arange(-SPLINE_ORDER, GRID_SIZE + SPLINE_ORDER + 1, dtype=jnp.float32) * h - 1.0
            return g[None, :]

        def b_splines(x, grid):
            xe = x[..., None]
            bases = ((xe >= grid[:, :-1]) & (xe < grid[:, 1:])).astype(x.dtype)
            for j in range(1, SPLINE_ORDER + 1):
                left = (xe - grid[:, :-(j + 1)]) / (grid[:, j:-1] - grid[:, :-(j + 1)])
                right = (grid[:, j + 1:] - xe) / (grid[:, j + 1:] - grid[:, 1:-j])
                bases = left * bases[..., :-1] + right * bases[..., 1:]
            return bases

        def kan_linear(x, base_w, spline_w, scaler, grid):
            base = jax.nn.silu(x) @ base_w.T
            sb = b_splines(x, grid)
            spline = jnp.einsum('nic,oic->no', sb, spline_w * scaler[..., None])
            return base + spline

        def expert_ffn(x, b1, s1, c1, b2, s2, c2, b3, s3, c3, gh, gf):
            h1 = kan_linear(x, b1, s1, c1, gh)
            h2 = kan_linear(x, b2, s2, c2, gh)
            return kan_linear(h1 * h2, b3, s3, c3, gf)
        B, S, H = x.shape
        gh, gf = (_grid(), _grid())
        xt = x.reshape(-1, H)
        logits = xt @ gate_w.T
        topw, sel = jax.lax.top_k(logits, TOP_K)
        topw = jax.nn.softmax(topw.astype(jnp.float32), axis=-1).astype(x.dtype)
        out = jnp.zeros_like(xt)
        for i in range(NUM_EXPERTS):
            ey = expert_ffn(xt, base_w1[i], spline_w1[i], scaler_w1[i], base_w2[i], spline_w2[i], scaler_w2[i], base_w3[i], spline_w3[i], scaler_w3[i], gh, gf)
            gi = jnp.sum(jnp.where(sel == i, topw, 0.0), axis=-1)
            out = out + gi[:, None] * ey
        return out.reshape(B, S, H)

    def _gn(v, G=32, eps=1e-05):
        B_, C_, H_, W_ = v.shape
        g = v.reshape(B_, G, C_ // G, H_, W_)
        m = jnp.mean(g, axis=(2, 3, 4), keepdims=True)
        s = jnp.var(g, axis=(2, 3, 4), keepdims=True)
        return ((g - m) / jnp.sqrt(s + eps)).reshape(v.shape)

    def _ln_c(v, eps=1e-06):
        m = jnp.mean(v, axis=1, keepdims=True)
        s = jnp.var(v, axis=1, keepdims=True)
        return (v - m) / jnp.sqrt(s + eps)

    def _ln_t(v, eps=1e-05):
        m = jnp.mean(v, axis=-1, keepdims=True)
        s = jnp.var(v, axis=-1, keepdims=True)
        return (v - m) / jnp.sqrt(s + eps)

    def _to_tokens(v):
        B_, C_, H_, W_ = v.shape
        return v.reshape(B_, C_, H_ * W_).transpose(0, 2, 1)

    def _from_tokens(t, like):
        B_, C_, H_, W_ = like.shape
        return t.transpose(0, 2, 1).reshape(B_, C_, H_, W_)
    x = x + _L0_conv_ref(_gn(x), L0_conv_w_qkv, L0_conv_b_qkv, L0_conv_w_out, L0_conv_b_out, L0_conv_gamma1, L0_conv_beta1, L0_conv_gamma2, L0_conv_beta2)
    x = _L1_conv_ref(x, L1_conv_Wq, L1_conv_Wk, L1_conv_Wv, L1_conv_Wout, L1_conv_bout)
    t = _to_tokens(x)
    t = t + _L2_attn_ref(_ln_t(t), L2_attn_in_proj_weight, L2_attn_in_proj_bias, L2_attn_out_weight, L2_attn_out_bias)
    t = t + _L2_ffn_ref(_ln_t(t), L2_ffn_W1, L2_ffn_b1, L2_ffn_W2, L2_ffn_b2, L2_ffn_W3, L2_ffn_b3)
    t = t + _L3_attn_ref(_ln_t(t), L3_attn_Wq, L3_attn_Wk, L3_attn_Wv, L3_attn_Wff1, L3_attn_bff1, L3_attn_Wff2, L3_attn_bff2)
    t = t + _L3_ffn_ref(_ln_t(t), L3_ffn_gate_w, L3_ffn_base_w1, L3_ffn_spline_w1, L3_ffn_scaler_w1, L3_ffn_base_w2, L3_ffn_spline_w2, L3_ffn_scaler_w2, L3_ffn_base_w3, L3_ffn_spline_w3, L3_ffn_scaler_w3)
    x = _from_tokens(t, x)
    return x

_drawn_inputs = setup_inputs


def setup_inputs(seed=0):
    import zlib

    import numpy as np

    out = dict(_drawn_inputs(seed))
    spreads = {'L0_conv_b_qkv': (0.0, 0.1),
     'L0_conv_b_out': (0.0, 0.1),
     'L0_conv_gamma1': (1.0, 0.2),
     'L0_conv_beta1': (0.0, 0.1),
     'L0_conv_gamma2': (1.0, 0.2),
     'L0_conv_beta2': (0.0, 0.1),
     'L1_conv_bout': (0.0, 0.1),
     'L2_attn_in_proj_bias': (0.0, 0.267),
     'L2_attn_out_bias': (0.0, 0.1),
     'L3_attn_bff1': (0.0, 0.8),
     'L3_attn_bff2': (0.0, 0.288),
     'L3_ffn_scaler_w1': (1.0, 0.6),
     'L3_ffn_scaler_w2': (1.0, 0.6),
     'L3_ffn_scaler_w3': (1.0, 0.6)}
    factors = {'L1_conv_Wq': 8.0,
     'L1_conv_Wk': 8.0,
     'L2_ffn_b1': 38.759,
     'L2_ffn_b2': 30.975,
     'L2_ffn_b3': 8.0,
     'L3_attn_Wq': 8.0,
     'L3_attn_Wk': 8.0,
     'L3_attn_Wv': 4.098,
     'L3_attn_Wff1': 8.0,
     'L3_attn_Wff2': 8.0}
    for name, (base, spread) in spreads.items():
        noise = np.random.default_rng([zlib.crc32(name.encode()), seed]).standard_normal(out[name].shape)
        drawn = base * np.exp(spread * noise) if base else spread * noise
        out[name] = jnp.asarray(drawn.astype(out[name].dtype))
    for name, factor in factors.items():
        out[name] = (out[name] * factor).astype(out[name].dtype)
    return out
```

```python
from contextlib import ExitStack

import numpy as np

import concourse.bass as bass
from concourse import mybir

F32 = mybir.dt.float32
BF16 = mybir.dt.bfloat16
F16 = mybir.dt.float16
ALU = mybir.AluOpType
ACT = mybir.ActivationFunctionType
AX = mybir.AxisListType

B = 4
C = 128
S = 512
P = 128
QT = S // P
HEADS = 8
DH = C // HEADS
VW = P + DH
HID = 512
KH = HID // P
NE = 8
FF = 256
NB = 8
NF = NB + 1
DIL = 4
WIN = 32
EMB = 64
STEPS = S - 1
DT = 1.0 / STEPS
HSCALE = 4096.0
NP = 3
EPS = 1e-5
BIG = -1.0e30


class Signals:

    def __init__(self, nc, stage):
        self.nc, self.stage, self.sem, self.per, self.n = nc, stage, {}, {}, {}

    def add(self, **per):
        for name, k in per.items():
            self.sem[name] = self.nc.alloc_semaphore(name=f"{self.stage}_{name}")
            self.per[name], self.n[name] = k, 0

    def up(self, ins, name, by=1):
        ins.then_inc(self.sem[name], by)
        self.n[name] += by

    def seq(self, eng, ins, name, i=None):
        self.up(ins, name)
        self.wait(eng, name, self.n[name], i)

    def wait(self, eng, name, n, i=None):
        if i is None:
            if n > 0:
                eng.wait_ge(self.sem[name], n)
        elif self.per[name]:
            eng.wait_ge(self.sem[name], i * self.per[name] + n)

    def check(self, *names):
        for name in names:
            assert self.n[name] == self.per[name], (name, self.n[name], self.per[name])


def layer_norm_pe(pe, sg, ones, src, sq, mean_ps, var_ps, k, i, src_sig, src_n):
    sg.wait(pe, src_sig, src_n, i)
    sg.up(pe.matmul(mean_ps, ones, src, start=True, stop=True), "ln_mean")
    sg.wait(pe, "ln_sq", k, i)
    sg.up(pe.matmul(var_ps, ones, sq, start=True, stop=True), "ln_var")


def layer_norm_act(act, sg, xc, sq, sd, var_ps, eps, k, i):
    sg.wait(act, "ln_cent", k, i)
    sg.up(act.activation(sq, xc, ACT.Square), "ln_sq")
    sg.wait(act, "ln_var", k, i)
    sg.up(act.activation(sd, var_ps, ACT.Sqrt, bias=eps), "ln_sd")


def layer_norm_dve(dve, sg, src, xc, sd, mean_ps, dst, k, i, gamma=None, beta=None):
    sg.wait(dve, "ln_mean", k, i)
    sg.seq(dve, dve.tensor_tensor(xc, src, mean_ps, ALU.subtract), "ln_cent", i)
    sg.wait(dve, "ln_sd", k, i)
    sg.seq(dve, dve.reciprocal(sd, sd), "dve_step", i)
    if gamma is None:
        sg.seq(dve, dve.tensor_tensor(dst, xc, sd, ALU.mult), "ln_out", i)
    else:
        sg.seq(dve, dve.tensor_tensor(xc, xc, sd, ALU.mult), "dve_step", i)
        sg.seq(dve, dve.tensor_scalar(dst, xc, gamma, beta, ALU.mult, ALU.add), "ln_out", i)


def global_attention(nc, t):
    UNITS = HEADS * QT
    with ExitStack() as ctx:
        def sb(name, shape, dt=F32):
            return ctx.enter_context(nc.sbuf_tensor(name, shape, dt))

        def ps(name):
            return ctx.enter_context(nc.psum_tensor(name, [P, S], F32))

        sg = Signals(nc, "global")
        sg.add(ga_loads=0, x_load=16, gn_mm=2, dve_step=11, dve_gn=3, act_gn=1, gx=1, ln_mean=3, ln_var=3, ln_sq=3,
               ln_sd=3, ln_cent=3, ln_out=3, vones=0, x1_done=1, x2_done=1, ga_z=1)
        for l in (0, 1):
            sg.add(**{f"q_ps{l}": 1, f"k_ps{l}": 1, f"v_ps{l}": 1, f"q_done{l}": 1, f"k_done{l}": 1, f"v_done{l}": 1,
                      f"qm{l}": HEADS, f"score{l}": UNITS, f"nmax{l}": UNITS, f"prob{l}": UNITS, f"recip{l}": UNITS,
                      f"pnorm{l}": UNITS, f"ptrans{l}": UNITS, f"ptcopy{l}": UNITS, f"pv{l}": HEADS,
                      f"o_done{l}": 1, f"out_ps{l}": 1})
        xb, gx, xn, xc, sq, sd, on, x1, x2 = (sb(n, [P, S]) for n in ("xb", "gx", "xn", "xc", "sq", "sd", "on", "x1", "x2b"))
        qT, kT, oT = sb("qT", [P, S]), sb("kT", [P, S]), sb("oT", [P, S])
        qm = [sb(f"qm{n}", [P, S]) for n in range(2)]
        V = sb("V", [P, QT, HEADS * VW])
        Pb = [sb(f"Pb{n}", [P, S]) for n in range(3)]
        PT = [sb(f"PT{n}", [P, QT, S]) for n in range(2)]
        nm, rs, rr = sb("nm", [P, 4]), sb("rs", [P, 4]), sb("rr", [P, 4])
        st6, mv, gms, dev, gvar = sb("st6", [P, 6]), sb("mv", [P, 2]), sb("gms", [P, 2]), sb("dev", [P, 1]), sb("gvar", [P, 1])
        w0, wo0, g4 = sb("w0", [P, 3 * C]), sb("wo0", [P, C]), sb("g4", [P, P])
        cols = sb("cols0", [P, 8])
        bvrow, onerow = sb("bvrow", [1, C]), sb("onerow", [1, P])
        w1 = {n: sb(n, [P, C]) for n in ("w1q", "w1k", "w1v", "w1o")}
        w1qe, w1ke, emb = sb("w1qe", [EMB, C]), sb("w1ke", [EMB, C]), sb("emb_s", [EMB, S])
        pS, pT, pM = [ps("pS0"), ps("pS1")], [ps("pT0"), ps("pT1")], [ps(f"pM{n}") for n in range(3)]
        pO = ps("pO")
        a = t.dram
        col = lambda ap: ap.rearrange("(p o) -> p o", o=1)
        loads = [(t.ident[:], a["c_ident"]), (t.ones[:], a["c_ones"]), (t.hmask[:], a["c_hmask"]), (t.eps[:], a["c_eps"]),
                 (g4[:], a["c_group"]), (emb[:], a["c_emb"]), (onerow[:], a["c_onerow"]),
                 (w0[:], a["L0_conv_w_qkv"]), (wo0[:], a["L0_conv_w_out"]),
                 (cols[:, 0:1], col(a["L0_conv_b_qkv"][0:C])), (cols[:, 1:2], col(a["L0_conv_b_qkv"][C:2 * C])),
                 (bvrow[:], a["L0_conv_b_qkv"][2 * C:3 * C].rearrange("(o n) -> o n", o=1)),
                 (cols[:, 2:3], col(a["L0_conv_b_out"])), (cols[:, 3:4], col(a["L0_conv_gamma1"])),
                 (cols[:, 4:5], col(a["L0_conv_beta1"])), (cols[:, 5:6], col(a["L0_conv_gamma2"])),
                 (cols[:, 6:7], col(a["L0_conv_beta2"])), (cols[:, 7:8], col(a["L1_conv_bout"])),
                 (w1["w1q"][:], a["L1_conv_Wq"][0:C]), (w1["w1k"][:], a["L1_conv_Wk"][0:C]),
                 (w1qe[:], a["L1_conv_Wq"][C:C + EMB]), (w1ke[:], a["L1_conv_Wk"][C:C + EMB]),
                 (w1["w1v"][:], a["L1_conv_Wv"]), (w1["w1o"][:], a["L1_conv_Wout"])]
        LOADED = 16 * len(loads)
        x_dram = a["x"].rearrange("b c h w -> b c (h w)")
        diag = lambda: V[:].rearrange("p t (h x) -> p t h x", x=VW)[:, :, :, 0:DH]
        block = ctx.enter_context(nc.Block())

        @block.sync
        def _(sp):
            with sp.Fori(0, B) as i:
                sg.wait(sp, "x1_done", 0, i)
                sg.up(sp.dma_start(xb[:], x_dram[bass.ds(i, 1)].rearrange("o c s -> (o c) s")), "x_load", 16)

        @block.gpsimd
        def _(pool):
            for dst, src in loads:
                sg.up(pool.dma_start(dst, src), "ga_loads", 16)
            sg.up(pool.memset(V[:], 0.0), "vones")

        def attention_pe(pe, l, i):
            src, sig, n = (xn, "ln_out", 1) if l == 0 else (x1, "x1_done", 1)
            wq, wk, wv = (w0[:, 0:C], w0[:, C:2 * C], w0[:, 2 * C:]) if l == 0 else (w1["w1q"][:], w1["w1k"][:], w1["w1v"][:])
            sg.wait(pe, sig, n, i)
            for dst, w, e, name in ((pM[0], wq, w1qe, "q_ps"), (pM[1], wk, w1ke, "k_ps")):
                if l == 1:
                    pe.matmul(dst[:], e[:], emb[:], start=True, stop=False)
                sg.up(pe.matmul(dst[:], w, src[:], start=(l == 0), stop=True), f"{name}{l}")
            for j in range(QT):
                o = pM[2][:, j * C:(j + 1) * C]
                ins = pe.matmul(o, src[:, j * P:(j + 1) * P], wv, start=True, stop=(l == 1))
                if l == 0:
                    ins = pe.matmul(o, onerow[:], bvrow[:], start=False, stop=True)
            sg.up(ins, f"v_ps{l}")

            def score(u):
                if u == 0:
                    sg.wait(pe, f"k_done{l}", 1, i)
                h, j = u // QT, u % QT
                sg.wait(pe, f"qm{l}", h + 1, i)
                if u >= 2:
                    sg.wait(pe, f"prob{l}", u - 1, i)
                sg.up(pe.matmul(pS[u % 2][:], qm[h % 2][:, j * P:(j + 1) * P], kT[:], start=True, stop=True), f"score{l}")

            def turn(u):
                sg.wait(pe, f"pnorm{l}", u + 1, i)
                if u >= 2:
                    sg.wait(pe, f"ptcopy{l}", u - 1, i)
                for k in range(QT):
                    ins = pe.transpose(pT[u % 2][:, k * P:(k + 1) * P], Pb[u % 3][:, k * P:(k + 1) * P], t.ident[:])
                sg.up(ins, f"ptrans{l}")

            def weigh(h):
                sg.wait(pe, f"ptcopy{l}", QT * (h + 1), i)
                if h == 0:
                    sg.wait(pe, f"v_done{l}", 1, i)
                for k in range(QT):
                    ins = pe.matmul(pO[:], V[:, k, h * P:(h + 1) * P], PT[h % 2][:, k, :],
                                    start=(h == 0 and k == 0), stop=(h == HEADS - 1 and k == QT - 1))
                sg.up(ins, f"pv{l}")

            score(0)
            score(1)
            for u in range(UNITS):
                turn(u)
                if u + 2 < UNITS:
                    score(u + 2)
                if u % QT == 0 and u:
                    weigh(u // QT - 1)
            weigh(HEADS - 1)

        def attention_act(act, l, i):
            sg.wait(act, f"q_ps{l}", 1, i)
            if l == 0:
                sg.up(act.activation(qT[:], pM[0][:], ACT.Identity, bias=cols[:, 0:1]), "q_done0")
            else:
                sg.up(act.activation(qT[:], pM[0][:], ACT.Copy), "q_done1")

            def prob(u):
                sg.wait(act, f"nmax{l}", u + 1, i)
                if u >= 3:
                    sg.wait(act, f"ptrans{l}", u - 2, i)
                sg.up(act.activation(Pb[u % 3][:], pS[u % 2][:], ACT.Exp, bias=nm[:, u % 4:u % 4 + 1],
                                     accum_out=rs[:, u % 4:u % 4 + 1]), f"prob{l}")

            def copy(u):
                h, j = u // QT, u % QT
                sg.wait(act, f"ptrans{l}", u + 1, i)
                if h >= 2:
                    sg.wait(act, f"pv{l}", h - 1, i)
                sg.up(act.activation(PT[h % 2][:, :, j * P:(j + 1) * P],
                                     pT[u % 2][:].rearrange("p (k q) -> p k q", k=QT), ACT.Copy), f"ptcopy{l}")

            for u in range(UNITS):
                prob(u)
                if u:
                    copy(u - 1)
            copy(UNITS - 1)

        def attention_dve(dve, l, i):
            sg.wait(dve, f"k_ps{l}", 1, i)
            if l == 0:
                sg.seq(dve, dve.tensor_scalar(kT[:], pM[1][:], cols[:, 1:2], None, ALU.add), "k_done0", i)
            else:
                sg.seq(dve, dve.tensor_copy(kT[:], pM[1][:]), "k_done1", i)
            sg.wait(dve, f"v_ps{l}", 1, i)
            sg.seq(dve, dve.tensor_copy(diag(), pM[2][:].rearrange("p (t h d) -> p t h d", t=QT, h=HEADS)), f"v_done{l}", i)
            sg.wait(dve, f"q_done{l}", 1, i)

            def mask_q(h):
                sg.seq(dve, dve.tensor_scalar(qm[h % 2][:], qT[:], t.hmask[:, h:h + 1], DH ** -0.5, ALU.mult, ALU.mult),
                       f"qm{l}", i)

            def norm(u):
                k = u % 4
                sg.wait(dve, f"prob{l}", u + 1, i)
                sg.seq(dve, dve.reciprocal(rr[:, k:k + 1], rs[:, k:k + 1]), f"recip{l}", i)
                sg.seq(dve, dve.tensor_scalar(Pb[u % 3][:], Pb[u % 3][:], rr[:, k:k + 1], None, ALU.mult), f"pnorm{l}", i)

            mask_q(0)
            mask_q(1)
            for u in range(UNITS):
                sg.wait(dve, f"score{l}", u + 1, i)
                sg.seq(dve, dve.tensor_reduce(nm[:, u % 4:u % 4 + 1], pS[u % 2][:], AX.X, ALU.max, negate=True), f"nmax{l}", i)
                if u:
                    norm(u - 1)
                if u % QT == QT - 1 and u // QT + 2 < HEADS:
                    mask_q(u // QT + 2)
            norm(UNITS - 1)
            sg.wait(dve, f"pv{l}", HEADS, i)
            sg.seq(dve, dve.tensor_copy(oT[:], pO[:]), f"o_done{l}", i)

        @block.tensor
        def _(pe):
            sg.wait(pe, "ga_loads", LOADED)
            with pe.Fori(0, B) as i:
                sg.wait(pe, "dve_gn", 1, i)
                sg.up(pe.matmul(pM[0][:, 0:2], g4[:], mv[:], start=True, stop=True), "gn_mm")
                sg.wait(pe, "dve_gn", 3, i)
                sg.up(pe.matmul(pM[1][:, 0:1], g4[:], dev[:], start=True, stop=True), "gn_mm")
                layer_norm_pe(pe, sg, t.ones[:], gx[:], sq[:], pM[0][:], pM[1][:], 1, i, "gx", 1)
                attention_pe(pe, 0, i)
                layer_norm_pe(pe, sg, t.ones[:], oT[:], sq[:], pM[0][:], pM[1][:], 2, i, "o_done0", 1)
                sg.wait(pe, "ln_out", 2, i)
                sg.up(pe.matmul(pM[2][:], wo0[:], on[:], start=True, stop=True), "out_ps0")
                attention_pe(pe, 1, i)
                sg.wait(pe, "o_done1", 1, i)
                sg.up(pe.matmul(pM[2][:], w1["w1o"][:], oT[:], start=True, stop=True), "out_ps1")
                layer_norm_pe(pe, sg, t.ones[:], x2[:], sq[:], pM[0][:], pM[1][:], 3, i, "x2_done", 1)

        @block.scalar
        def _(act):
            sg.wait(act, "ga_loads", LOADED)
            with act.Fori(0, B) as i:
                sg.wait(act, "dve_gn", 3, i)
                sg.wait(act, "gn_mm", 2, i)
                sg.up(act.activation(gvar[:], pM[1][:, 0:1], ACT.Sqrt, bias=gms[:, 1:2]), "act_gn")
                layer_norm_act(act, sg, xc[:], sq[:], sd[:], pM[1][:], t.eps[:], 1, i)
                attention_act(act, 0, i)
                layer_norm_act(act, sg, xc[:], sq[:], sd[:], pM[1][:], t.eps[:], 2, i)
                attention_act(act, 1, i)
                layer_norm_act(act, sg, xc[:], sq[:], sd[:], pM[1][:], t.eps[:], 3, i)

        @block.vector
        def _(dve):
            sg.wait(dve, "ga_loads", LOADED)
            sg.wait(dve, "vones", 1)
            with dve.Fori(0, B) as i:
                sg.wait(dve, "x_load", 16, i)
                sg.seq(dve, dve.bn_stats(st6[:], xb[:]), "dve_step", i)
                dve.memset(rr[:, 0:1], 0.0)
                sg.seq(dve, dve.bn_aggr(mv[:], st6[:]), "dve_gn", i)
                sg.wait(dve, "gn_mm", 1, i)
                sg.seq(dve, dve.tensor_scalar(gms[:], pM[0][:, 0:2], EPS, None, ALU.add), "dve_step", i)
                sg.seq(dve, dve.tensor_copy(gms[:, 0:1], pM[0][:, 0:1]), "dve_gn", i)
                sg.seq(dve, dve.tensor_tensor(dev[:], mv[:, 0:1], gms[:, 0:1], ALU.subtract), "dve_step", i)
                sg.seq(dve, dve.tensor_tensor(dev[:], dev[:], dev[:], ALU.mult), "dve_gn", i)
                sg.wait(dve, "act_gn", 1, i)
                sg.seq(dve, dve.reciprocal(gvar[:], gvar[:]), "dve_step", i)
                sg.seq(dve, dve.tensor_scalar(gx[:], xb[:], gms[:, 0:1], gvar[:, 0:1], ALU.subtract, ALU.mult), "gx", i)
                layer_norm_dve(dve, sg, gx[:], xc[:], sd[:], pM[0][:], xn[:], 1, i, cols[:, 3:4], cols[:, 4:5])
                attention_dve(dve, 0, i)
                layer_norm_dve(dve, sg, oT[:], xc[:], sd[:], pM[0][:], on[:], 2, i, cols[:, 5:6], cols[:, 6:7])
                sg.wait(dve, "out_ps0", 1, i)
                sg.seq(dve, dve.scalar_tensor_tensor(out=x1[:], in0=pM[2][:], scalar=cols[:, 2:3], in1=xn[:],
                                                     op0=ALU.add, op1=ALU.add), "dve_step", i)
                sg.seq(dve, dve.tensor_tensor(x1[:], x1[:], xb[:], ALU.add), "x1_done", i)
                attention_dve(dve, 1, i)
                sg.wait(dve, "out_ps1", 1, i)
                sg.seq(dve, dve.scalar_tensor_tensor(out=x2[:], in0=pM[2][:], scalar=cols[:, 7:8], in1=x1[:],
                                                     op0=ALU.add, op1=ALU.add), "x2_done", i)
                layer_norm_dve(dve, sg, x2[:], xc[:], sd[:], pM[0][:], on[:], 3, i)
                one = lambda ap: ap.rearrange("p (o s) -> p o s", o=1)
                sg.seq(dve, dve.tensor_scalar(t.x2[:, bass.ds(i, 1), :], one(x2[:]), 0.0, None, ALU.add), "dve_step", i)
                sg.seq(dve, dve.tensor_scalar(t.z[:, bass.ds(i, 1), :], one(on[:]), 0.0, None, ALU.add), "ga_z", i)

        for name in sg.per:
            if sg.per[name]:
                sg.check(name)
def batch_attention(nc, t):
    with ExitStack() as ctx:
        def sb(name, shape, dt=F32):
            return ctx.enter_context(nc.sbuf_tensor(name, shape, dt))

        def ps(name):
            return ctx.enter_context(nc.psum_tensor(name, [P, S], F32))

        sg = Signals(nc, "batch")
        sg.add(ba_loads=0, zs_done=1, qkv_ps=B, qkv_done=B, ba_step=4 * B + 6, ba_shift=1, ba_exp=1, attn_done=B, ot_ps=1,
               ot_done=1, proj_ps=1, x3_done=1)
        w, wo = sb("ba_w_in", [P, 3 * C]), sb("ba_w_o", [P, C])
        brow, one, bo = sb("b_in", [1, 3 * C]), sb("one_r", [1, P]), sb("b_o", [P, 1])
        zs = sb("zs", [P, B, P])
        qkv = sb("qkv", [P, B, 3 * C])
        prod = sb("prod", [P, B * C])
        sc = sb("sc", [P, B, B, HEADS])
        mx, rs = sb("mx", [P, B, HEADS]), sb("rsum", [P, B, HEADS])
        o, oT = sb("o_t", [P, B, C]), sb("o_c", [P, B, P])
        pq = [ps(f"pq{n}") for n in range(2)]
        pt, pp = ps("pt"), ps("pp")
        a = t.dram
        loads = [(w[:], a["bw_in"]), (wo[:], a["bw_out"]), (brow[:], a["L2_attn_in_proj_bias"].rearrange("(o n) -> o n", o=1)),
                 (one[:], a["c_onerow"]), (bo[:], a["L2_attn_out_bias"].rearrange("(p o) -> p o", o=1))]
        block = ctx.enter_context(nc.Block())

        @block.sync
        def _(sp):
            for dst, src in loads:
                sg.up(sp.dma_start(dst, src), "ba_loads", 16)

        @block.tensor
        def _(pe):
            sg.wait(pe, "ba_loads", 16 * len(loads))
            with pe.Fori(0, QT) as i:
                sg.wait(pe, "zs_done", 1, i)
                for b in range(B):
                    if b >= 2:
                        sg.wait(pe, "qkv_done", b - 1, i)
                    pe.matmul(pq[b % 2][:, 0:3 * C], zs[:, b, :], w[:], start=True, stop=False)
                    sg.up(pe.matmul(pq[b % 2][:, 0:3 * C], one[:], brow[:], start=False, stop=True), "qkv_ps")
                for b in range(B):
                    sg.wait(pe, "attn_done", b + 1, i)
                    ins = pe.transpose(pt[:, b * P:(b + 1) * P], o[:, b, :], t.ident[:])
                sg.up(ins, "ot_ps")
                sg.wait(pe, "ot_done", 1, i)
                sg.up(pe.matmul(pp[:], wo[:], oT[:].rearrange("p b n -> p (b n)"), start=True, stop=True), "proj_ps")

        @block.scalar
        def _(act):
            with act.Fori(0, QT) as i:
                for b in range(B):
                    sg.wait(act, "qkv_ps", b + 1, i)
                    sg.up(act.activation(qkv[:, b, :], pq[b % 2][:, 0:3 * C], ACT.Copy), "qkv_done")
                sg.wait(act, "ba_shift", 1, i)
                sg.up(act.activation(sc[:], sc[:], ACT.Exp, scale=DH ** -0.5), "ba_exp")
                sg.wait(act, "ot_ps", 1, i)
                sg.up(act.activation(oT[:].rearrange("p b n -> p (b n)"), pt[:], ACT.Copy), "ot_done")

        @block.vector
        def _(dve):
            with dve.Fori(0, QT) as i:
                tile = lambda x: x[:, :, bass.ds(i * P, P)]
                sg.seq(dve, dve.tensor_scalar(zs[:], tile(t.z), 0.0, None, ALU.add), "zs_done", i)
                sg.wait(dve, "qkv_done", B, i)
                keys, values = qkv[:, :, C:2 * C], qkv[:, :, 2 * C:3 * C]
                cube = prod[:].rearrange("p (b c) -> p b c", b=B)
                for b in range(B):
                    query = qkv[:, b:b + 1, 0:C].to_broadcast([P, B, C])
                    sg.seq(dve, dve.tensor_tensor(cube, query, keys, ALU.mult), "ba_step", i)
                    sg.seq(dve, dve.tensor_reduce(sc[:, b].rearrange("p k h -> p (k h)"),
                                                  prod[:].rearrange("p (g d) -> p g d", d=DH), AX.X, ALU.add), "ba_step", i)
                bykey = sc[:].rearrange("p b k h -> p b h k")
                sg.seq(dve, dve.tensor_reduce(mx[:], bykey, AX.X, ALU.max), "ba_step", i)
                for b in range(B):
                    ins = dve.tensor_tensor(sc[:, b], sc[:, b], mx[:, b:b + 1, :].to_broadcast([P, B, HEADS]), ALU.subtract)
                    if b < B - 1:
                        sg.seq(dve, ins, "ba_step", i)
                sg.seq(dve, ins, "ba_shift", i)
                sg.wait(dve, "ba_exp", 1, i)
                sg.seq(dve, dve.tensor_reduce(rs[:], bykey, AX.X, ALU.add), "ba_step", i)
                sg.seq(dve, dve.reciprocal(rs[:], rs[:]), "ba_step", i)
                for b in range(B):
                    sg.seq(dve, dve.tensor_tensor(prod[:].rearrange("p (k h d) -> p k h d", k=B, h=HEADS),
                                                  values.rearrange("p k (h d) -> p k h d", d=DH),
                                                  sc[:, b].rearrange("p k (h o) -> p k h o", o=1).to_broadcast([P, B, HEADS, DH]),
                                                  ALU.mult), "ba_step", i)
                    sg.seq(dve, dve.tensor_reduce(o[:, b, :], prod[:].rearrange("p (k c) -> p c k", k=B), AX.X, ALU.add), "ba_step", i)
                    ob = o[:, b, :].rearrange("p (h d) -> p h d", d=DH)
                    sg.seq(dve, dve.tensor_tensor(ob, ob, rs[:, b, :].rearrange("p (h o) -> p h o", o=1).to_broadcast([P, HEADS, DH]),
                                                  ALU.mult), "attn_done", i)
                sg.wait(dve, "proj_ps", 1, i)
                sg.seq(dve, dve.scalar_tensor_tensor(out=tile(t.x3), in0=pp[:].rearrange("p (b n) -> p b n", b=B), scalar=bo[:, 0:1],
                                                     in1=tile(t.x2), op0=ALU.add, op1=ALU.add), "x3_done", i)

        for name in sg.per:
            if sg.per[name]:
                sg.check(name)


def flow(nc, t):
    coef = [(DT / 2, DT / 6), (DT / 2, DT / 3), (DT, DT / 3), (None, DT / 6)]
    NV = KH * B
    HALF = NV // 2
    with ExitStack() as ctx:
        def sb(name, shape, dt=F32):
            return ctx.enter_context(nc.sbuf_tensor(name, shape, dt))

        def ps(name):
            return ctx.enter_context(nc.psum_tensor(name, [P, S], F32))

        sg = Signals(nc, "flow")
        sg.add(fl_loads=0, sel16=0, y_mm=0, y_step=0, y_act=0, w13_ps=0, w13_done=0, v_ps=0, prep=0, part=0, rest=0, b2_moved=0,
               ones_set=0,
               u1=2 * KH, h1=2 * KH, hi1=2 * KH, in1=2 * KH, l2_ps=2 * KH, u2=2 * KH, h2=2 * KH, hi2=2 * KH, in2=2 * KH,
               l13_ps=2 * KH, g13=2 * KH, acc=6, v_shifted=2, hsum=3, hist=1,
               k_ps=0, slope=0, states=0)
        w1, w3n, w2f, w13f, w3 = sb("w1", [P, HID]), sb("w3n", [P, HID]), sb("w2f", [P, KH, HID]), sb("w13f", [P, KH, HID]), sb("w3", [P, KH, C])
        W2, W13 = sb("W2", [P, NP, KH, HID], BF16), sb("W13", [P, NP, KH, HID], BF16)
        b1, b2r, b2s, B2, b3 = sb("b1", [P, KH]), sb("b2r", [KH, P]), sb("b2s", [KH, NP, P], BF16), sb("B2", [NP * KH, P], BF16), sb("b3", [P, 1])
        sel_f, sel = sb("sel_f", [NP * KH, 32]), sb("sel", [NP * KH, 32], BF16)
        yc, ysq, ysd, y0, b3dt = sb("yc", [P, B]), sb("ysq", [P, B]), sb("ysd", [P, B]), sb("y0", [P, B]), sb("b3dt", [P, 1])
        half_b, full_b = sb("half_b", [P, NV]), sb("full_b", [P, NV])
        v_half, v_full, acc = sb("v_half", [P, NV]), sb("v_full", [P, NV]), sb("acc", [P, NV])
        u1, u2, g = sb("u1", [P, NV]), sb("u2", [P, NV]), sb("g", [P, NV])
        h1, h2 = sb("h1", [P, NV]), sb("h2", [P, 4, NV])
        H1, H2 = sb("H1", [P, KH, 2, B], F16), sb("H2", [P, KH, 2, B], F16)
        inner, outer, both = sb("inner", [P, NV]), sb("outer", [P, NV]), sb("both", [P, NV])
        hist = sb("hist_h", [P, KH, S, B])
        slope, Y, ones1 = sb("slope_d", [P, S, B]), sb("Y", [P, B, S]), sb("ones1", [P, S])
        p2, p1, pw = [ps("p2a"), ps("p2b")], [ps("p1a"), ps("p1b")], [ps("pw0"), ps("pw1")]
        py, pv = ps("py"), ps("pv_ps")
        hv = lambda x, q: x[:, HALF * q:HALF * q + HALF]
        mb = lambda x: x.rearrange("p (m b) -> p m b", b=B)
        parts = lambda x: x[:, 0:NV].rearrange("p (m q b) -> p m b q", m=2, q=2)
        a = t.dram
        loads = [(w1[:], a["ff_w1"]), (w3n[:], a["L2_ffn_W3"]), (w2f[:], a["ff_w2"]), (w3[:], a["ff_w3"]), (b1[:], a["ff_b1"]),
                 (b2r[:], a["L2_ffn_b2"].rearrange("(m p) -> m p", p=P)), (b3[:], a["L2_ffn_b3"].rearrange("(p o) -> p o", o=1)),
                 (sel_f[:], a["c_sel"])]
        block = ctx.enter_context(nc.Block())

        @block.sync
        def _(sp):
            for dst, src in loads:
                sg.up(sp.dma_start(dst, src), "fl_loads", 16)
            sg.wait(sp, "part", 9)
            for q in range(NP):
                sg.up(sp.dma_start(B2[KH * q:KH * q + KH, :], b2s[:, q, :]), "b2_moved", 16)

        @block.gpsimd
        def _(pool):
            sg.up(pool.memset(ones1[:], 1.0), "ones_set")
            sg.up(pool.memset(hist[:, :, STEPS:S, :], 0.0), "ones_set")
            sg.wait(pool, "prep", 6)
            sg.up(pool.tensor_tensor(v_half[:], u1[:], half_b[:], ALU.add), "v_shifted")
            sg.up(pool.tensor_tensor(v_full[:], u1[:], full_b[:], ALU.add), "v_shifted")
            sg.n["v_shifted"] = 0
            with pool.Fori(0, STEPS) as s:
                sg.wait(pool, "h2", 6, s)
                sg.seq(pool, pool.tensor_tensor(inner[:], h2[:, 1, :], h2[:, 2, :], ALU.add), "hsum", s)
                sg.wait(pool, "h2", 8, s)
                sg.seq(pool, pool.tensor_tensor(outer[:], h2[:, 0, :], h2[:, 3, :], ALU.add), "hsum", s)
                sg.seq(pool, pool.tensor_tensor(both[:], inner[:], outer[:], ALU.add), "hsum", s)
                sg.up(pool.tensor_tensor(hist[:, :, bass.ds(s, 1), :].rearrange("p m o b -> p m (o b)"), mb(both[:]), mb(inner[:]),
                                         ALU.add), "hist")
                pool.wait_ge(sg.sem["u1"], s * sg.per["u1"] + 2 + 2 * KH)
                sg.up(pool.tensor_tensor(v_half[:], u1[:], half_b[:], ALU.add), "v_shifted")
                sg.up(pool.tensor_tensor(v_full[:], u1[:], full_b[:], ALU.add), "v_shifted")

        def product(pe, s, out, W, H, ready, n, done, seeded):
            def tile(m, k):
                for q in range(NP):
                    first = not seeded and k == 0 and q == 0 and m % 2 == 0
                    ins = pe.matmul(out[m // 2][:, HALF * (m % 2):HALF * (m % 2) + HALF], W[:, q, k, P * m:P * m + P],
                                    H[:, k, :, :].rearrange("p q b -> p (q b)"), start=first, stop=(k == KH - 1 and q == NP - 1),
                                    skip_group_check=True)
                return ins

            sg.wait(pe, ready, n + 1, s)
            for k in (0, 1):
                for m in range(KH):
                    tile(m, k)
            sg.wait(pe, ready, n + 2, s)
            for m in range(KH):
                for k in (2, 3):
                    ins = tile(m, k)
                if m % 2:
                    sg.up(ins, done)

        @block.tensor
        def _(pe):
            sg.wait(pe, "fl_loads", 16 * len(loads))
            sg.up(pe.matmul(py[:, 0:B], t.ones[:], t.x3[:, :, 0], start=True, stop=True), "y_mm")
            sg.wait(pe, "y_act", 1)
            sg.up(pe.matmul(py[:, 0:B], t.ones[:], ysq[:], start=True, stop=True), "y_mm")
            for k in range(KH):
                if k >= 2:
                    sg.wait(pe, "w13_done", k - 1)
                sg.up(pe.matmul(pw[k % 2][:], w3n[:, P * k:P * k + P], w1[:], start=True, stop=True), "w13_ps")
            sg.wait(pe, "y_step", 3)
            for m in range(KH):
                pe.matmul(pv[:, B * m:B * m + B], w1[:, P * m:P * m + P], y0[:], start=True, stop=True)
            for m in range(KH):
                ins = pe.matmul(pv[:, NV + m:NV + m + 1], w1[:, P * m:P * m + P], b3[:], start=True, stop=True)
            sg.up(ins, "v_ps")
            sg.wait(pe, "rest", 8)
            sg.wait(pe, "b2_moved", 16 * NP)
            sg.wait(pe, "sel16", 1)
            with pe.Fori(0, STEPS) as s:
                for e in range(4):
                    sg.wait(pe, "u2", 2 * e, s)
                    for q in range(2):
                        pe.matmul(p2[q][:, 0:NV], B2[:], sel[:, NV * q:NV * q + NV], start=True, stop=False, skip_group_check=True)
                    product(pe, s, p2, W2, H1, "in1", 2 * e, "l2_ps", True)
                    sg.wait(pe, "g13", 2 * e, s)
                    product(pe, s, p1, W13, H2, "in2", 2 * e, "l13_ps", False)
            pe.wait_ge(sg.sem["hist"], STEPS)
            sg.wait(pe, "ones_set", 2)
            BLK = S // 4
            for j in range(4):
                if j >= 2:
                    sg.wait(pe, "slope", j - 1)
                for k in range(KH):
                    ins = pe.matmul(pw[j % 2][:], w3[:, k, :], hist[:, k, BLK * j:BLK * j + BLK, :].rearrange("p s b -> p (s b)"),
                                    start=(k == 0), stop=(k == KH - 1))
                sg.up(ins, "k_ps")

        @block.scalar
        def _(act):
            sg.wait(act, "fl_loads", 16 * len(loads))
            sg.up(act.activation(sel[:], sel_f[:], ACT.Copy), "sel16")
            sg.wait(act, "y_step", 1)
            sg.up(act.activation(ysq[:], yc[:], ACT.Square), "y_act")
            sg.wait(act, "y_mm", 2)
            sg.up(act.activation(ysd[:], py[:, 0:B], ACT.Sqrt, bias=t.eps[:]), "y_act")
            for k in range(KH):
                sg.wait(act, "w13_ps", k + 1)
                sg.up(act.activation(w13f[:, k, :], pw[k % 2][:], ACT.Copy), "w13_done")
            sg.wait(act, "w13_done", KH)
            for q in range(NP):
                for n, (full, split) in enumerate(((b2r[:], b2s[:, q, :]), (w2f[:], W2[:, q]), (w13f[:], W13[:, q]))):
                    if q:
                        sg.wait(act, "rest", 3 * (q - 1) + n + 1)
                    sg.up(act.activation(split, full, ACT.Copy), "part")
            with act.Fori(0, STEPS) as s:
                for e in range(4):
                    for q in range(2):
                        sg.wait(act, "u1", 2 * e + q + 1, s)
                        sg.up(act.activation(hv(h1, q), hv(u1, q), ACT.Tanh), "h1")
                    for q in range(2):
                        sg.wait(act, "u2", 2 * e + q + 1, s)
                        if e == 0 and q == 0:
                            sg.wait(act, "hsum", 0, s)
                        sg.up(act.activation(h2[:, e, HALF * q:HALF * q + HALF], hv(u2, q), ACT.Tanh, scale=1.0 / HSCALE), "h2")

        @block.vector
        def _(dve):
            sg.wait(dve, "y_mm", 1)
            sg.seq(dve, dve.tensor_tensor(yc[:], t.x3[:, :, 0], py[:, 0:B], ALU.subtract), "y_step")
            sg.wait(dve, "y_act", 2)
            sg.seq(dve, dve.reciprocal(ysd[:], ysd[:]), "y_step")
            sg.seq(dve, dve.tensor_tensor(y0[:], yc[:], ysd[:], ALU.mult), "y_step")
            sg.wait(dve, "v_ps", 1)
            wide = lambda x: x.rearrange("p (m o) -> p m o", o=1).to_broadcast([P, KH, B])
            sg.seq(dve, dve.tensor_copy(h1[:, 0:KH], pv[:, NV:NV + KH]), "prep")
            sg.seq(dve, dve.tensor_scalar(mb(half_b[:]), wide(h1[:, 0:KH]), DT / 2, None, ALU.mult), "prep")
            sg.seq(dve, dve.tensor_scalar(mb(full_b[:]), wide(h1[:, 0:KH]), DT, None, ALU.mult), "prep")
            sg.seq(dve, dve.tensor_scalar(b3dt[:], b3[:], DT, None, ALU.mult), "prep")
            sg.seq(dve, dve.tensor_tensor(mb(u1[:]), mb(pv[:, 0:NV]), wide(b1[:]), ALU.add), "prep")
            sg.seq(dve, dve.tensor_copy(u2[:, 0:1], u1[:, 0:1]), "prep")
            for q in range(NP - 1):
                for n, (full, split) in enumerate(((b2r[:], b2s[:, q, :]), (w2f[:], W2[:, q]), (w13f[:], W13[:, q]))):
                    sg.wait(dve, "part", 3 * q + n + 1)
                    sg.seq(dve, dve.tensor_tensor(full, full, split, ALU.subtract), "rest")
            sg.wait(dve, "part", 9)
            for n in range(2):
                sg.seq(dve, dve.tensor_copy(u2[:, n:n + 1], u1[:, n:n + 1]), "rest")
            for q in range(2):
                dve.tensor_copy(hv(u2, q), hv(u1, q)).then_inc(sg.sem["u1"], 1)
            dve.wait_ge(sg.sem["u1"], 2)

            def split(h, H, q, sig, n, s, hi, done):
                sg.wait(dve, sig, n + 1, s)
                Hq = H[:, 2 * q:2 * q + 2, :, :]
                sg.seq(dve, dve.tensor_scalar(Hq[:, :, 0, :], mb(h), HSCALE, None, ALU.mult), hi, s)
                sg.up(dve.scalar_tensor_tensor(out=Hq[:, :, 1, :], in0=mb(h), scalar=HSCALE, in1=Hq[:, :, 0, :],
                                               op0=ALU.mult, op1=ALU.subtract), done)

            with dve.Fori(0, STEPS) as s:
                for e, (next_c, sum_c) in enumerate(coef):
                    n = 2 * e
                    for q in range(2):
                        split(hv(h1, q), H1, q, "h1", n + q, s, "hi1", "in1")
                    for q in range(2):
                        sg.wait(dve, "l2_ps", n + q + 1, s)
                        sg.up(dve.tensor_reduce(mb(hv(u2, q)), parts(p2[q]), AX.X, ALU.add), "u2")
                    for q in range(2):
                        split(h2[:, e, HALF * q:HALF * q + HALF], H2, q, "h2", n + q, s, "hi2", "in2")
                    for q in range(2):
                        sg.wait(dve, "l13_ps", n + q + 1, s)
                        sg.seq(dve, dve.tensor_reduce(mb(hv(g, q)), parts(p1[q]), AX.X, ALU.add), "g13", s)
                        if e == 0:
                            sg.wait(dve, "v_shifted", 2, s)
                        if e < 3:
                            sg.up(dve.scalar_tensor_tensor(out=hv(u1, q), in0=hv(g, q), scalar=next_c / HSCALE,
                                                           in1=hv(v_half if e < 2 else v_full, q), op0=ALU.mult, op1=ALU.add), "u1")
                            if e:
                                sg.wait(dve, "acc", 2 * (e - 1) + q + 1, s)
                            sg.up(dve.scalar_tensor_tensor(out=hv(acc, q), in0=hv(g, q), scalar=sum_c / HSCALE,
                                                           in1=hv(v_full if e == 0 else acc, q), op0=ALU.mult, op1=ALU.add), "acc")
                        else:
                            sg.wait(dve, "acc", 4 + q + 1, s)
                            sg.up(dve.scalar_tensor_tensor(out=hv(u1, q), in0=hv(g, q), scalar=sum_c / HSCALE, in1=hv(acc, q),
                                                           op0=ALU.mult, op1=ALU.add), "u1")
            BLK = S // 4
            for j in range(4):
                sg.wait(dve, "k_ps", j + 1)
                sg.seq(dve, dve.tensor_scalar(slope[:, BLK * j:BLK * j + BLK, :].rearrange("p s b -> p (s b)"), pw[j % 2][:],
                                              DT / 6, b3dt[:, 0:1], ALU.mult, ALU.add), "slope")
            sg.seq(dve, dve.tensor_copy(Y[:, :, 0], y0[:]), "states")
            for b in range(B):
                sg.seq(dve, dve.tensor_tensor_scan(Y[:, b, 1:S], ones1[:, 0:STEPS], slope[:, 0:STEPS, b], y0[:, b:b + 1],
                                                   ALU.mult, ALU.add), "states")
            sg.seq(dve, dve.tensor_tensor(t.x4[:], t.x3[:], Y[:], ALU.add), "states")

        for name in sg.per:
            if sg.per[name]:
                sg.check(name)


def window_attention(nc, t):
    with ExitStack() as ctx:
        def sb(name, shape, dt=F32):
            return ctx.enter_context(nc.sbuf_tensor(name, shape, dt))

        def ps(name):
            return ctx.enter_context(nc.psum_tensor(name, [P, S], F32))

        R = DIL
        sg = Signals(nc, "window")
        sg.add(wa_loads=0, vzero=0, xb_done=1, dve_step=3, ln_mean=2, ln_var=2, ln_sq=2, ln_sd=2, ln_cent=2, ln_out=2,
               wq_ps=1, wk_ps=1, wv_ps=1, wq_done=1, wk_done=1, wv_done=1, wqm=HEADS, wscore=HEADS, wmask=HEADS, wmax=2 * HEADS,
               wprob=HEADS, wpadw=HEADS, wsum=3 * HEADS, wnorm=HEADS, wtrans=HEADS, wcopy=HEADS, wpv=HEADS, wo_done=1,
               f_ps=1, f_done=1, g_ps=1, g_done=1, x5_done=1, logit_ps=1, wa_end=3)
        xb, z, xc, sq, sd = (sb("w" + n, [P, S]) for n in ("xb", "z", "xc", "sq", "sd"))
        qT, kT, xa, f, g, x5, z5 = (sb("w" + n, [P, S]) for n in ("qT", "kT", "xa", "f", "g", "x5", "z5"))
        qm = [sb(f"wqm{n}", [P, S]) for n in range(2)]
        V = sb("wV", [P, R, HEADS * VW])
        sc = [sb(f"wsc{n}", [P, R, P]) for n in range(2)]
        PT = [sb(f"wPT{n}", [P, R, P]) for n in range(2)]
        m, padw, rs = sb("wm", [P, R]), sb("wpadw", [P, R]), sb("wrs", [P, R])
        w = {n: sb("wa_" + n, [P, C]) for n in ("q", "k", "v", "f1", "f2")}
        bias, gate, band, pads = sb("wa_bias", [P, 2]), sb("wa_gate", [P, NE]), sb("wa_band", [P, P]), sb("wa_pads", [P, 2])
        pS, pT, pM = [ps("wpS0"), ps("wpS1")], [ps("wpT0"), ps("wpT1")], [ps(f"wpM{n}") for n in range(3)]
        pO = ps("wpO")
        a = t.dram
        col = lambda ap: ap.rearrange("(p o) -> p o", o=1)
        loads = [(w["q"][:], a["L3_attn_Wq"]), (w["k"][:], a["L3_attn_Wk"]), (w["v"][:], a["L3_attn_Wv"]), (w["f1"][:], a["L3_attn_Wff1"]),
                 (w["f2"][:], a["L3_attn_Wff2"]), (bias[:, 0:1], col(a["L3_attn_bff1"])), (bias[:, 1:2], col(a["L3_attn_bff2"])),
                 (gate[:], a["gate_t"]), (band[:], a["c_band"]), (pads[:], a["c_pads"])]
        res = lambda x, r: x[:, r:S:R]
        one = lambda ap: ap.rearrange("p (o s) -> p o s", o=1)
        block = ctx.enter_context(nc.Block())

        @block.sync
        def _(sp):
            for dst, src in loads:
                sg.up(sp.dma_start(dst, src), "wa_loads", 16)

        @block.gpsimd
        def _(pool):
            sg.up(pool.memset(V[:], 0.0), "vzero")

        @block.tensor
        def _(pe):
            sg.wait(pe, "wa_loads", 16 * len(loads))
            with pe.Fori(0, B) as i:
                layer_norm_pe(pe, sg, t.ones[:], xb[:], sq[:], pM[0][:], pM[1][:], 1, i, "xb_done", 1)
                sg.wait(pe, "ln_out", 1, i)
                sg.up(pe.matmul(pM[0][:], w["q"][:], z[:], start=True, stop=True), "wq_ps")
                sg.up(pe.matmul(pM[1][:], w["k"][:], z[:], start=True, stop=True), "wk_ps")
                for r in range(R):
                    ins = pe.matmul(pM[2][:, r * P:(r + 1) * P], res(z, r), w["v"][:], start=True, stop=True)
                sg.up(ins, "wv_ps")

                def score(h):
                    sg.wait(pe, "wqm", h + 1, i)
                    if h == 0:
                        sg.wait(pe, "wk_done", 1, i)
                    if h >= 2:
                        sg.wait(pe, "wmask", h - 1, i)
                    for r in range(R):
                        ins = pe.matmul(pS[h % 2][:, r * P:(r + 1) * P], res(qm[h % 2], r), res(kT, r), start=True, stop=True)
                    sg.up(ins, "wscore")

                score(0)
                for h in range(HEADS):
                    if h + 1 < HEADS:
                        score(h + 1)
                    sg.wait(pe, "wnorm", h + 1, i)
                    if h >= 2:
                        sg.wait(pe, "wcopy", h - 1, i)
                    for r in range(R):
                        ins = pe.transpose(pT[h % 2][:, r * P:(r + 1) * P], sc[h % 2][:, r, :], t.ident[:])
                    sg.up(ins, "wtrans")
                    if h == 0:
                        sg.wait(pe, "wv_done", 1, i)
                    sg.wait(pe, "wcopy", h + 1, i)
                    for r in range(R):
                        ins = pe.matmul(pO[:, r * P:(r + 1) * P], V[:, r, h * P:(h + 1) * P], PT[h % 2][:, r, :],
                                        start=(h == 0 and r == 0), stop=(h == HEADS - 1), skip_group_check=True)
                    sg.up(ins, "wpv")
                sg.wait(pe, "wo_done", 1, i)
                sg.up(pe.matmul(pM[2][:], w["f1"][:], xa[:], start=True, stop=True), "f_ps")
                sg.wait(pe, "f_done", 1, i)
                sg.up(pe.matmul(pM[0][:], w["f2"][:], f[:], start=True, stop=True), "g_ps")
                layer_norm_pe(pe, sg, t.ones[:], x5[:], sq[:], pM[0][:], pM[1][:], 2, i, "x5_done", 1)
                sg.wait(pe, "ln_out", 2, i)
                for j in range(QT):
                    ins = pe.matmul(pM[2][:, j * NE:(j + 1) * NE], z5[:, j * P:(j + 1) * P], gate[:], start=True, stop=True)
                sg.up(ins, "logit_ps")

        @block.scalar
        def _(act):
            sg.wait(act, "wa_loads", 16 * len(loads))
            with act.Fori(0, B) as i:
                layer_norm_act(act, sg, xc[:], sq[:], sd[:], pM[1][:], t.eps[:], 1, i)
                sg.wait(act, "wq_ps", 1, i)
                sg.up(act.activation(qT[:], pM[0][:], ACT.Copy), "wq_done")
                for h in range(HEADS):
                    sg.wait(act, "wmax", 2 * h + 2, i)
                    sg.up(act.activation(padw[:], m[:], ACT.Exp), "wpadw")
                    for r in range(R):
                        ins = act.activation(sc[h % 2][:, r, :], sc[h % 2][:, r, :], ACT.Exp, bias=m[:, r:r + 1],
                                             accum_out=rs[:, r:r + 1])
                    sg.up(ins, "wprob")
                    sg.wait(act, "wtrans", h + 1, i)
                    if h >= 2:
                        sg.wait(act, "wpv", h - 1, i)
                    sg.up(act.activation(PT[h % 2][:].rearrange("p r q -> p (r q)"), pT[h % 2][:], ACT.Copy), "wcopy")
                sg.wait(act, "f_ps", 1, i)
                sg.up(act.activation(f[:], pM[2][:], ACT.Relu, bias=bias[:, 0:1]), "f_done")
                sg.wait(act, "g_ps", 1, i)
                sg.up(act.activation(g[:], pM[0][:], ACT.Relu, bias=bias[:, 1:2]), "g_done")
                layer_norm_act(act, sg, xc[:], sq[:], sd[:], pM[1][:], t.eps[:], 2, i)

        @block.vector
        def _(dve):
            sg.wait(dve, "wa_loads", 16 * len(loads))
            sg.wait(dve, "vzero", 1)
            with dve.Fori(0, B) as i:
                sg.seq(dve, dve.tensor_scalar(one(xb[:]), t.x4[:, bass.ds(i, 1), :], 0.0, None, ALU.add), "xb_done", i)
                layer_norm_dve(dve, sg, xb[:], xc[:], sd[:], pM[0][:], z[:], 1, i)
                sg.wait(dve, "wk_ps", 1, i)
                sg.seq(dve, dve.tensor_copy(kT[:], pM[1][:]), "wk_done", i)
                sg.wait(dve, "wv_ps", 1, i)
                sg.seq(dve, dve.tensor_copy(V[:].rearrange("p t (h x) -> p t h x", x=VW)[:, :, :, 0:DH],
                                            pM[2][:].rearrange("p (t h d) -> p t h d", t=R, h=HEADS)), "wv_done", i)
                sg.wait(dve, "wq_done", 1, i)
                for h in range(HEADS):
                    sg.seq(dve, dve.tensor_scalar(qm[h % 2][:], qT[:], t.hmask[:, h:h + 1], None, ALU.mult), "wqm", i)
                    sg.wait(dve, "wscore", h + 1, i)
                    if h >= 2:
                        sg.wait(dve, "wtrans", h - 1, i)
                    x = sc[h % 2]
                    sg.seq(dve, dve.tensor_tensor(x[:], pS[h % 2][:].rearrange("p (r k) -> p r k", r=R),
                                                  band[:].rearrange("p (o k) -> p o k", o=1).to_broadcast([P, R, P]), ALU.add), "wmask", i)
                    sg.seq(dve, dve.tensor_reduce(m[:], x[:], AX.X, ALU.max), "wmax", i)
                    sg.seq(dve, dve.tensor_scalar(m[:], m[:], pads[:, 0:1], -1.0, ALU.max, ALU.mult), "wmax", i)
                    sg.wait(dve, "wpadw", h + 1, i)
                    sg.wait(dve, "wprob", h + 1, i)
                    sg.seq(dve, dve.scalar_tensor_tensor(out=rs[:], in0=padw[:], scalar=pads[:, 1:2], in1=rs[:],
                                                         op0=ALU.mult, op1=ALU.add), "wsum", i)
                    sg.seq(dve, dve.tensor_scalar(rs[:], rs[:], float(DH) ** 0.5, None, ALU.mult), "wsum", i)
                    sg.seq(dve, dve.reciprocal(rs[:], rs[:]), "wsum", i)
                    sg.seq(dve, dve.tensor_tensor(x[:], x[:], rs[:].rearrange("p (r o) -> p r o", o=1).to_broadcast([P, R, P]),
                                                  ALU.mult), "wnorm", i)
                sg.wait(dve, "wpv", HEADS, i)
                sg.seq(dve, dve.tensor_copy(xa[:].rearrange("p (a r) -> p r a", r=R), pO[:].rearrange("p (r a) -> p r a", r=R)), "wo_done", i)
                sg.seq(dve, dve.tensor_tensor(x5[:], xb[:], xa[:], ALU.add), "dve_step", i)
                sg.wait(dve, "g_done", 1, i)
                sg.seq(dve, dve.tensor_tensor(x5[:], x5[:], g[:], ALU.add), "x5_done", i)
                layer_norm_dve(dve, sg, x5[:], xc[:], sd[:], pM[0][:], z5[:], 2, i)
                sg.seq(dve, dve.tensor_scalar(t.x5[:, bass.ds(i, 1), :], one(x5[:]), 0.0, None, ALU.add), "wa_end", i)
                sg.seq(dve, dve.tensor_scalar(t.z[:, bass.ds(i, 1), :], one(z5[:]), 0.0, None, ALU.add), "wa_end", i)
                sg.wait(dve, "logit_ps", 1, i)
                sg.seq(dve, dve.tensor_scalar(t.logits[:, bass.ds(i, 1), :, :].rearrange("p o j e -> p o (j e)"),
                                              one(pM[2][:, 0:QT * NE]), 0.0, None, ALU.add), "wa_end", i)

        for name in sg.per:
            if sg.per[name]:
                sg.check(name)


def experts(nc, t, out_dram):
    UT = 2 * B
    TURNS = NE // 2
    LOADS = 16 * 9
    ITEMS = 2 * NB
    XIT = B * NB
    ORDER = [NB] + list(range(NB))
    CHUNKS = [ORDER[0:2], ORDER[2:4], ORDER[4:6], ORDER[6:9]]
    SIXTH = 6.0 ** -0.5
    with ExitStack() as ctx:
        def sb(name, shape, dt=F32):
            return ctx.enter_context(nc.sbuf_tensor(name, shape, dt))

        def ps(name):
            return ctx.enter_context(nc.psum_tensor(name, [P, S], F32))

        sg = Signals(nc, "experts")
        names = ("ex_const gate_step gate_exp xabs xpq xsq xcube xtanh xsilu xfeat w_load0 w_load1 w_scaled l1_ps l2_ps gb_ps gb_done "
                 "h1_done g_done th_done silu_done abs_done pq_done sq_done cube_done feat ge_done out_step out_done final").split()
        sg.add(**{n: 0 for n in names})
        sem = sg.sem
        FX = sb("FX", [P, NF, B * S])
        F2 = sb("F2", [P, NF, 2, S])
        W12 = [sb(f"W12_{n}", [P, 2, NF, FF]) for n in range(2)]
        W3 = [sb(f"W3_{n}", [P, 2, NF, C]) for n in range(2)]
        s12, s3 = sb("s12", [P, 2, FF]), sb("s3", [P, 2, C])
        g, gs = sb("g2", [P, 2, S]), sb("gs", [P, S])
        dist, pn, qn, q2 = ([sb(f"{n}{k}", [P, S]) for k in range(2)] for n in ("dist", "pn", "qn", "q2_"))
        gates, rank, tmp = sb("gates", [P, NE, B * QT]), sb("rank", [P, B * QT, NE]), sb("gtmp", [P, B * QT, NE])
        gmx, ge = sb("gmx", [P, B * QT]), [sb(f"ge{n}", [P, B * QT]) for n in range(2)]
        cen = sb("cen", [P, NB])
        bank = [ps(f"l1_{n}") for n in range(4)]
        out2, pg = [ps("l2_0"), ps("l2_1")], ps("pg")
        a = t.dram
        lg = t.logits[:].rearrange("p b j e -> p (b j) e")
        block = ctx.enter_context(nc.Block())

        def load_expert(sp, e, par):
            pick = lambda n: a[n][bass.ds(e, 1)].rearrange("o p x -> (o p) x")
            for w in range(2):
                sp.dma_start(W12[par][:, w, 0:NB, :].rearrange("p c o -> p (c o)"), pick(f"spline{w + 1}")).then_inc(sem[f"w_load{par}"], 16)
                sp.dma_start(W12[par][:, w, NB, :], pick(f"base{w + 1}")).then_inc(sem[f"w_load{par}"], 16)
                sp.dma_start(s12[:, w, :], pick(f"scaler{w + 1}")).then_inc(sem[f"w_load{par}"], 16)
            sp.dma_start(W3[par][:, :, 0:NB, :].rearrange("p k c o -> p k (c o)"),
                         pick("spline3").rearrange("p (k x) -> p k x", k=2)).then_inc(sem[f"w_load{par}"], 16)
            sp.dma_start(W3[par][:, :, NB, :], pick("base3").rearrange("p (k x) -> p k x", k=2)).then_inc(sem[f"w_load{par}"], 16)
            sp.dma_start(s3[:], pick("scaler3").rearrange("p (k x) -> p k x", k=2)).then_inc(sem[f"w_load{par}"], 16)

        @block.sync
        def _(sp):
            sp.dma_start(cen[:], a["c_centres"]).then_inc(sem["ex_const"], 16)
            load_expert(sp, 0, 0)
            sp.wait_ge(sem["w_scaled"], 3)
            load_expert(sp, 1, 1)
            with sp.Fori(0, TURNS - 1) as i:
                sp.wait_ge(sem["l2_ps"], UT * i + B)
                load_expert(sp, 2 * i + 2, 0)
                sp.wait_ge(sem["l2_ps"], UT * i + 2 * B)
                load_expert(sp, 2 * i + 3, 1)
            sp.wait_ge(sem["out_done"], NE * B)
            sp.dma_start(out_dram, t.x5[:]).then_inc(sem["final"], 16)
            sp.wait_ge(sem["final"], 16)

        @block.gpsimd
        def _(pool):
            def scale(i, par):
                pool.wait_ge(sem[f"w_load{par}"], LOADS * i + LOADS)
                wide = lambda x, n: x.rearrange("p (o n) -> p o n", o=1).to_broadcast([P, NB, n])
                for w in range(2):
                    x = W12[par][:, w, 0:NB, :]
                    pool.tensor_tensor(x, x, wide(s12[:, w, :], FF), ALU.mult).then_inc(sem["w_scaled"], 1)
                for k in range(2):
                    x = W3[par][:, k, 0:NB, :]
                    ins = pool.tensor_tensor(x, x, wide(s3[:, k, :], C), ALU.mult)
                    if k:
                        ins.then_inc(sem["w_scaled"], 1)

            def turn(i, last):
                for m in range(UT):
                    n = UT * i + m
                    if m == 1:
                        scale(i, 1)
                    if m == 5 and not last:
                        scale(i + 1, 0)
                    for k in range(ITEMS):
                        c, o = k // 2, k % 2
                        pool.wait_ge(sem["cube_done"], (ITEMS * UT) * i + ITEMS * m + k + 1)
                        if k == 0:
                            pool.wait_ge(sem["l2_ps"], n)
                        pool.tensor_tensor(F2[:, c, o, :], q2[k % 2][:], dist[k % 2][:], ALU.subtract).then_inc(sem["feat"], 1)

            scale(0, 0)
            for k in range(XIT):
                pool.wait_ge(sem["xcube"], k + 1)
                pool.tensor_tensor(FX[:, k % NB, S * (k // NB):S * (k // NB) + S], q2[k % 2][:], dist[k % 2][:],
                                   ALU.subtract).then_inc(sem["xfeat"], 1)
            with pool.Fori(0, TURNS - 1) as i:
                turn(i, False)
            turn(TURNS - 1, True)

        @block.tensor
        def _(pe):
            def first(par, b, group):
                o, w = group // 2, group % 2
                for f in range(NF):
                    ins = pe.matmul(bank[group][:], W12[par][:, w, f, P * o:P * o + P], FX[:, f, S * b:S * b + S],
                                    start=(f == 0), stop=(f == NF - 1))
                ins.then_inc(sem["l1_ps"], 1)

            def turn(i, last):
                for m in range(UT):
                    n = UT * i + m
                    par, b = m // B, m % B
                    for j in range(4):
                        if m + 1 < UT or not last:
                            if j == 0:
                                if m + 1 == B:
                                    pe.wait_ge(sem["w_scaled"], 6 * i + 6)
                                if m + 1 == UT:
                                    pe.wait_ge(sem["w_scaled"], 6 * i + 9)
                            if j % 2 == 0:
                                pe.wait_ge(sem["g_done"], 2 * n + j // 2 + 1)
                            first((m + 1) // B % 2, (m + 1) % B, j)
                        for f in CHUNKS[j]:
                            if f == NB:
                                pe.wait_ge(sem["silu_done"], n + 1)
                                if m % B == 0:
                                    pe.wait_ge(sem["ge_done"], 2 * i + par + 1)
                                pe.wait_ge(sem["gb_done"], n)
                                for q in range(QT):
                                    ins = pe.matmul(pg[:, P * q:P * q + P],
                                                    ge[par][:, QT * b + q:QT * b + q + 1].to_broadcast([P, P]), t.ident[:],
                                                    start=True, stop=True)
                                ins.then_inc(sem["gb_ps"], 1)
                            else:
                                pe.wait_ge(sem["feat"], (ITEMS * UT) * i + ITEMS * m + 2 * f + 2)
                            for k in range(2):
                                ins = pe.matmul(out2[m % 2][:], W3[par][:, k, f, :], F2[:, f, k, :],
                                                start=(f == NB and k == 0), stop=(f == NB - 1 and k == 1))
                    ins.then_inc(sem["l2_ps"], 1)

            pe.wait_ge(sem["xfeat"], XIT)
            pe.wait_ge(sem["xsilu"], B)
            pe.wait_ge(sem["w_scaled"], 3)
            for group in range(4):
                first(0, 0, group)
            with pe.Fori(0, TURNS - 1) as i:
                turn(i, False)
            turn(TURNS - 1, True)

        @block.scalar
        def _(act):
            act.wait_ge(sem["ex_const"], 16)
            act.wait_ge(sem["gate_step"], 2)
            act.activation(rank[:], rank[:], ACT.Exp).then_inc(sem["gate_exp"], 1)

            def distance(src, c, k):
                act.activation(dist[k % 2][:], src, ACT.Abs, scale=2.5, bias=cen[:, c:c + 1])

            def squares(k, done):
                act.activation(dist[k % 2][:], pn[k % 2][:], ACT.Square, scale=SIXTH).then_inc(sem[done], 1)
                act.activation(q2[k % 2][:], qn[k % 2][:], ACT.Square, scale=2 * SIXTH).then_inc(sem[done], 1)

            for b in range(B):
                if b:
                    act.wait_ge(sem["xsilu"], b)
                act.activation(gs[:], t.z[:, b, :], ACT.Tanh, scale=0.5).then_inc(sem["xtanh"], 1)
            for k in range(XIT + 1):
                if k < XIT:
                    if k >= 2:
                        act.wait_ge(sem["xfeat"], k - 1)
                    act.activation(dist[k % 2][:], t.z[:, k // NB, :], ACT.Abs, scale=2.5, bias=cen[:, k % NB:k % NB + 1]).then_inc(sem["xabs"], 1)
                if k:
                    act.wait_ge(sem["xpq"], 2 * k)
                    squares(k - 1, "xsq")

            def turn(i, last):
                for m in range(UT):
                    n = UT * i + m
                    base = (ITEMS * UT) * i + ITEMS * m
                    for o in range(2):
                        act.wait_ge(sem["l1_ps"], 4 * n + 2 * o + 2)
                        if o == 0:
                            act.wait_ge(sem["silu_done"], n)
                            act.wait_ge(sem["abs_done"], base)
                        act.activation(g[:, o, :], bank[2 * o][:], ACT.Copy).then_inc(sem["h1_done"], 1)
                    act.wait_ge(sem["g_done"], 2 * n + 2)
                    act.wait_ge(sem["out_done"], n)
                    for o in range(2):
                        if o == 0:
                            act.wait_ge(sem["l2_ps"], n)
                        act.activation(F2[:, NB, o, :], g[:, o, :], ACT.Tanh, scale=0.5).then_inc(sem["th_done"], 1)
                    for k in range(ITEMS + 1):
                        if k < ITEMS:
                            if k or m:
                                act.wait_ge(sem["feat"], base + k - 1)
                            act.activation(dist[k % 2][:], g[:, k % 2, :], ACT.Abs, scale=2.5,
                                           bias=cen[:, k // 2:k // 2 + 1]).then_inc(sem["abs_done"], 1)
                        if k:
                            act.wait_ge(sem["pq_done"], 2 * (base + k))
                            squares(k - 1, "sq_done")
                    act.wait_ge(sem["gb_ps"], n + 1)
                    act.activation(gs[:], pg[:], ACT.Copy).then_inc(sem["gb_done"], 1)

            with act.Fori(0, TURNS - 1) as i:
                turn(i, False)
            turn(TURNS - 1, True)

        @block.vector
        def _(dve):
            def step(ins, name="gate_step", done=[0]):
                ins.then_inc(sem[name], 1)
                done[0] += 1
                dve.wait_ge(sem[name], done[0])

            NT = B * QT
            wide = lambda x: x.rearrange("p (n o) -> p n o", o=1).to_broadcast([P, NT, NE])
            step(dve.tensor_reduce(gmx[:], lg, AX.X, ALU.max))
            step(dve.tensor_tensor(rank[:], lg, wide(gmx[:]), ALU.subtract))
            dve.wait_ge(sem["gate_exp"], 1)
            step(dve.tensor_scalar(gates[:].rearrange("p e n -> p n e"), rank[:], 1.0, None, ALU.mult))
            step(dve.memset(rank[:], 0.0))
            for j in range(NE):
                one = lg[:, :, j:j + 1]
                step(dve.tensor_tensor(tmp[:, :, 0:j + 1], one.to_broadcast([P, NT, j + 1]), lg[:, :, 0:j + 1], ALU.is_gt))
                if j + 1 < NE:
                    step(dve.tensor_tensor(tmp[:, :, j + 1:NE], one.to_broadcast([P, NT, NE - 1 - j]), lg[:, :, j + 1:NE], ALU.is_ge))
                step(dve.tensor_tensor(rank[:], rank[:], tmp[:], ALU.add))
            step(dve.tensor_scalar(rank[:], rank[:], 2.0, None, ALU.is_lt))
            gt = gates[:].rearrange("p e n -> p n e")
            step(dve.tensor_tensor(gt, gt, rank[:], ALU.mult))
            step(dve.tensor_reduce(gmx[:], gt, AX.X, ALU.add))
            step(dve.reciprocal(gmx[:], gmx[:]))
            step(dve.tensor_tensor(gt, gt, wide(gmx[:]), ALU.mult))

            for b in range(B):
                dve.wait_ge(sem["xtanh"], b + 1)
                step(dve.tensor_scalar(gs[:], gs[:], 0.5, 0.5, ALU.mult, ALU.add))
                dve.tensor_tensor(FX[:, NB, S * b:S * b + S], gs[:], t.z[:, b, :], ALU.mult).then_inc(sem["xsilu"], 1)

            def hats(k, done):
                dve.tensor_scalar(pn[k % 2][:], dist[k % 2][:], 2.0, -2.0, ALU.min, ALU.add).then_inc(sem[done], 1)
                dve.tensor_scalar(qn[k % 2][:], dist[k % 2][:], 1.0, -1.0, ALU.min, ALU.add).then_inc(sem[done], 1)

            def cubes(k, count, sq, done):
                dve.wait_ge(sem[sq], 2 * count - 1)
                dve.tensor_tensor(dist[k % 2][:], dist[k % 2][:], pn[k % 2][:], ALU.mult)
                dve.wait_ge(sem[sq], 2 * count)
                dve.tensor_tensor(q2[k % 2][:], q2[k % 2][:], qn[k % 2][:], ALU.mult).then_inc(sem[done], 1)

            for k in range(XIT + 1):
                if k < XIT:
                    dve.wait_ge(sem["xabs"], k + 1)
                    if k >= 2:
                        dve.wait_ge(sem["xcube"], k - 1)
                    hats(k, "xpq")
                if k:
                    cubes(k - 1, k, "xsq", "xcube")
            dve.wait_ge(sem["xcube"], XIT)

            def turn(i, last):
                for m in range(UT):
                    n = UT * i + m
                    par, b = m // B, m % B
                    base = (ITEMS * UT) * i + ITEMS * m
                    if b == 0:
                        dve.tensor_scalar(ge[par][:].rearrange("p (o n) -> p o n", o=1), gates[:, bass.ds(2 * i + par, 1), :], 1.0, None,
                                          ALU.mult).then_inc(sem["ge_done"], 1)
                    for o in range(2):
                        dve.wait_ge(sem["h1_done"], 2 * n + o + 1)
                        dve.tensor_tensor(g[:, o, :], g[:, o, :], bank[2 * o + 1][:], ALU.mult).then_inc(sem["g_done"], 1)
                    for o in range(2):
                        x = F2[:, NB, o, :]
                        dve.wait_ge(sem["th_done"], 2 * n + o + 1)
                        dve.tensor_scalar(x, x, 0.5, 0.5, ALU.mult, ALU.add).then_inc(sem["out_step"], 1)
                    for o in range(2):
                        x = F2[:, NB, o, :]
                        dve.wait_ge(sem["out_step"], 3 * n + o + 1)
                        ins = dve.tensor_tensor(x, x, g[:, o, :], ALU.mult)
                    ins.then_inc(sem["silu_done"], 1)
                    for k in range(ITEMS + 1):
                        if k < ITEMS:
                            dve.wait_ge(sem["abs_done"], base + k + 1)
                            if k or m:
                                dve.wait_ge(sem["cube_done"], base + k - 1)
                            hats(k, "pq_done")
                        if k:
                            cubes(k - 1, base + k, "sq_done", "cube_done")
                    dve.wait_ge(sem["gb_done"], n + 1)
                    dve.wait_ge(sem["l2_ps"], n + 1)
                    dve.tensor_tensor(gs[:], gs[:], out2[m % 2][:], ALU.mult).then_inc(sem["out_step"], 1)
                    dve.wait_ge(sem["out_step"], 3 * n + 3)
                    dve.tensor_tensor(t.x5[:, b, :], t.x5[:, b, :], gs[:], ALU.add).then_inc(sem["out_done"], 1)

            with dve.Fori(0, TURNS - 1) as i:
                turn(i, False)
            turn(TURNS - 1, True)


def shape_constants():
    f = np.float32
    head = np.arange(C) // DH
    nf, nt, H, W = 16, 16, 16, 32
    ln = np.log2(np.maximum(np.arange(0, H * nf, dtype=f), f(1)))
    ln[0] = -2.0
    ln = (ln.reshape(H, nf).T * np.arange(1, nf + 1, dtype=f)[:, None]).astype(f)
    freq = np.stack([np.cos(ln), np.sin(ln)], axis=1).reshape(2 * nf, H)
    k = np.arange(0, nt, dtype=f) + f(0.5)
    xs = np.arange(0, nt * W, dtype=f).reshape(W, nt).T
    theta = (k[:, None] * xs / f(W * nt) * f(6.283185307179586)).astype(f)
    time = np.stack([np.cos(theta), np.sin(theta)], axis=1).reshape(2 * nt, W)
    emb = np.concatenate([np.repeat(freq, W, axis=1), np.tile(time, (1, H))], axis=0)
    a = np.arange(P)
    outside = (np.maximum(0, WIN - a) + np.maximum(0, a + WIN - (P - 1))).astype(f)
    sel = np.zeros((NP * KH, 2, 2, 2, B), f)
    for part in range(NP):
        for m in range(KH):
            sel[KH * part + m, m // 2, m % 2, 0, :] = HSCALE
    return {
        "c_ident": np.eye(P, dtype=f),
        "c_ones": np.full((P, P), 1.0 / C, f),
        "c_hmask": (head[:, None] == np.arange(HEADS)[None, :]).astype(f),
        "c_eps": np.full((P, 1), EPS, f),
        "c_group": ((a[:, None] // 4) == (a[None, :] // 4)).astype(f) / f(4),
        "c_emb": emb.astype(f),
        "c_onerow": np.ones((1, P), f),
        "c_band": np.where(np.abs(a[:, None] - a[None, :]) <= WIN, 0.0, BIG).astype(f),
        "c_pads": np.stack([np.where(outside > 0, 0.0, BIG).astype(f), outside], axis=1),
        "c_centres": np.tile((3.5 - np.arange(NB, dtype=f))[None, :], (P, 1)),
        "c_sel": sel.reshape(NP * KH, 32),
    }


def conv_attn_hybrid(nc, dram, out_dram):
    t = Stage()
    t.dram = dram
    with ExitStack() as ctx:
        def sb(name, shape):
            return ctx.enter_context(nc.sbuf_tensor(name, shape, F32))

        t.ident, t.ones, t.hmask, t.eps = sb("ident", [P, P]), sb("ones", [P, P]), sb("hmask", [P, HEADS]), sb("eps", [P, 1])
        stream = sb("stream", [P, B, S])
        t.x2 = t.x3 = t.x4 = t.x5 = stream
        t.z, t.logits = sb("z_all", [P, B, S]), sb("logits_all", [P, B, QT, NE])
        for stage in (global_attention, batch_attention, flow, window_attention):
            with nc.cleanup_on_exit():
                stage(nc, t)
        experts(nc, t, out_dram)


class Stage:
    pass


def laid_out(x):
    a = {n: v for n, v in x.items() if n == "x" or n.startswith(("L0_", "L1_", "L3_attn"))}
    for n in ("in_proj_bias", "out_bias"):
        a["L2_attn_" + n] = x["L2_attn_" + n]
    a["bw_in"], a["bw_out"] = x["L2_attn_in_proj_weight"].T, x["L2_attn_out_weight"].T
    for n in ("W3", "b2", "b3"):
        a["L2_ffn_" + n] = x["L2_ffn_" + n]
    rows = lambda w, n: w.T.reshape(n, P, -1).transpose(1, 0, 2)
    a["ff_w1"], a["ff_w2"], a["ff_w3"] = x["L2_ffn_W1"].T, rows(x["L2_ffn_W2"], KH), rows(x["L2_ffn_W3"], KH)
    a["ff_b1"] = x["L2_ffn_b1"].reshape(KH, P).T
    a["gate_t"] = x["L3_ffn_gate_w"].T
    for n in (1, 2):
        a[f"spline{n}"] = x[f"L3_ffn_spline_w{n}"].transpose(0, 2, 3, 1).reshape(NE, P, -1)
        a[f"base{n}"] = x[f"L3_ffn_base_w{n}"].transpose(0, 2, 1)
        a[f"scaler{n}"] = x[f"L3_ffn_scaler_w{n}"].transpose(0, 2, 1)
    for n in ("spline", "base", "scaler"):
        w = x[f"L3_ffn_{n}_w3"].reshape(NE, C, 2, P, -1)
        a[n + "3"] = w.transpose(0, 3, 2, 4, 1).reshape(NE, P, -1)
    return a


def kernel(**inputs):
    import concourse.bacc as _bacc
    from concourse.bass_utils import run_bass_kernel_spmd as _run

    nc = _bacc.Bacc("TRN2", target_bir_lowering=False, num_devices=1)
    arrays, dram = {}, {}
    for name, v in {**laid_out({n: np.asarray(v) for n, v in inputs.items()}), **shape_constants()}.items():
        v = np.ascontiguousarray(v)
        arrays["in_" + name] = v
        dram[name] = nc.dram_tensor("in_" + name, v.shape, mybir.dt.from_np(v.dtype), kind="ExternalInput").ap()
    out = nc.dram_tensor("out_x", (B, C, S), F32, kind="ExternalOutput").ap()
    conv_attn_hybrid(nc, dram, out.rearrange("b c s -> c b s"))
    r = _run(nc, [arrays], core_ids=[0])
    return r.results[0]["out_x"].reshape(B, C, 16, 32)
```

```python
from contextlib import ExitStack

import numpy as np

import concourse.bass as bass
from concourse import mybir

F32 = mybir.dt.float32
BF16 = mybir.dt.bfloat16
F16 = mybir.dt.float16
ALU = mybir.AluOpType
ACT = mybir.ActivationFunctionType
AX = mybir.AxisListType

B = 4
C = 128
S = 512
P = 128
QT = S // P
HEADS = 8
DH = C // HEADS
VW = P + DH
HID = 512
KH = HID // P
NE = 8
FF = 256
NB = 8
NF = NB + 1
DIL = 4
WIN = 32
EMB = 64
STEPS = S - 1
DT = 1.0 / STEPS
HSCALE = 4096.0
NP = 2
BP = 3
WMAX = 2.0 ** 14
UN = 7
EPS = 1e-5
BIG = -1.0e30


class Signals:

    def __init__(self, nc, stage):
        self.nc, self.stage, self.sem, self.per, self.n = nc, stage, {}, {}, {}

    def add(self, **per):
        for name, k in per.items():
            self.sem[name] = self.nc.alloc_semaphore(name=f"{self.stage}_{name}")
            self.per[name], self.n[name] = k, 0

    def up(self, ins, name, by=1):
        ins.then_inc(self.sem[name], by)
        self.n[name] += by

    def seq(self, eng, ins, name, i=None):
        self.up(ins, name)
        self.wait(eng, name, self.n[name], i)

    def wait(self, eng, name, n, i=None):
        if i is None:
            if n > 0:
                eng.wait_ge(self.sem[name], n)
        elif self.per[name]:
            eng.wait_ge(self.sem[name], i * self.per[name] + n)

    def check(self, *names):
        for name in names:
            assert self.n[name] == self.per[name], (name, self.n[name], self.per[name])


def layer_norm_pe(pe, sg, ones, src, sq, mean_ps, var_ps, k, i, src_sig, src_n):
    sg.wait(pe, src_sig, src_n, i)
    sg.up(pe.matmul(mean_ps, ones, src, start=True, stop=True), "ln_mean")
    sg.wait(pe, "ln_sq", k, i)
    sg.up(pe.matmul(var_ps, ones, sq, start=True, stop=True), "ln_var")


def layer_norm_act(act, sg, xc, sq, sd, var_ps, eps, k, i):
    sg.wait(act, "ln_cent", k, i)
    sg.up(act.activation(sq, xc, ACT.Square), "ln_sq")
    sg.wait(act, "ln_var", k, i)
    sg.up(act.activation(sd, var_ps, ACT.Sqrt, bias=eps), "ln_sd")


def layer_norm_dve(dve, sg, src, xc, sd, mean_ps, dst, k, i, gamma=None, beta=None):
    sg.wait(dve, "ln_mean", k, i)
    sg.seq(dve, dve.tensor_tensor(xc, src, mean_ps, ALU.subtract), "ln_cent", i)
    sg.wait(dve, "ln_sd", k, i)
    sg.seq(dve, dve.reciprocal(sd, sd), "dve_step", i)
    if gamma is None:
        sg.seq(dve, dve.tensor_tensor(dst, xc, sd, ALU.mult), "ln_out", i)
    else:
        sg.seq(dve, dve.tensor_tensor(xc, xc, sd, ALU.mult), "dve_step", i)
        sg.seq(dve, dve.tensor_scalar(dst, xc, gamma, beta, ALU.mult, ALU.add), "ln_out", i)


def global_attention(nc, t):
    UNITS = HEADS * QT
    with ExitStack() as ctx:
        def sb(name, shape, dt=F32):
            return ctx.enter_context(nc.sbuf_tensor(name, shape, dt))

        def ps(name):
            return ctx.enter_context(nc.psum_tensor(name, [P, S], F32))

        sg = Signals(nc, "global")
        sg.add(ga_loads=0, x_load=16, gn_mm=2, dve_step=11, dve_gn=3, act_gn=1, gx=1, ln_mean=3, ln_var=3, ln_sq=3,
               ln_sd=3, ln_cent=3, ln_out=3, vones=0, x1_done=1, x2_done=1, ga_z=1)
        for l in (0, 1):
            sg.add(**{f"q_ps{l}": 1, f"k_ps{l}": 1, f"v_ps{l}": 1, f"q_done{l}": 1, f"k_done{l}": 1, f"v_done{l}": 1,
                      f"qm{l}": HEADS, f"score{l}": UNITS, f"nmax{l}": UNITS, f"prob{l}": UNITS, f"recip{l}": UNITS,
                      f"pnorm{l}": UNITS, f"ptrans{l}": UNITS, f"ptcopy{l}": UNITS, f"pv{l}": HEADS,
                      f"o_done{l}": 1, f"out_ps{l}": 1})
        xb, gx, xn, xc, sq, sd, on, x1, x2 = (sb(n, [P, S]) for n in ("xb", "gx", "xn", "xc", "sq", "sd", "on", "x1", "x2b"))
        qT, kT, oT = sb("qT", [P, S]), sb("kT", [P, S]), sb("oT", [P, S])
        qm = [sb(f"qm{n}", [P, S]) for n in range(2)]
        V = sb("V", [P, QT, HEADS * VW])
        Pb = [sb(f"Pb{n}", [P, S]) for n in range(3)]
        PT = [sb(f"PT{n}", [P, QT, S]) for n in range(2)]
        nm, rs, rr = sb("nm", [P, 4]), sb("rs", [P, 4]), sb("rr", [P, 4])
        st6, mv, gms, dev, gvar = sb("st6", [P, 6]), sb("mv", [P, 2]), sb("gms", [P, 2]), sb("dev", [P, 1]), sb("gvar", [P, 1])
        w0, wo0, g4 = sb("w0", [P, 3 * C]), sb("wo0", [P, C]), sb("g4", [P, P])
        cols = sb("cols0", [P, 8])
        bvrow, onerow = sb("bvrow", [1, C]), sb("onerow", [1, P])
        w1 = {n: sb(n, [P, C]) for n in ("w1q", "w1k", "w1v", "w1o")}
        w1qe, w1ke, emb = sb("w1qe", [EMB, C]), sb("w1ke", [EMB, C]), sb("emb_s", [EMB, S])
        pT, pM, pO = [ps("pT0"), ps("pT1")], [ps(f"pM{n}") for n in range(3)], ps("pO")
        pS = [ps("pS0"), ps("pS1"), pM[0], pM[1]]
        AHEAD = len(pS) - 1
        a = t.dram
        col = lambda ap: ap.rearrange("(p o) -> p o", o=1)
        loads = [(t.ident[:], a["c_ident"]), (t.ones[:], a["c_ones"]), (t.hmask[:], a["c_hmask"]), (t.eps[:], a["c_eps"]),
                 (g4[:], a["c_group"]), (emb[:], a["c_emb"]), (onerow[:], a["c_onerow"]),
                 (w0[:], a["L0_conv_w_qkv"]), (wo0[:], a["L0_conv_w_out"]),
                 (cols[:, 0:1], col(a["L0_conv_b_qkv"][0:C])), (cols[:, 1:2], col(a["L0_conv_b_qkv"][C:2 * C])),
                 (bvrow[:], a["L0_conv_b_qkv"][2 * C:3 * C].rearrange("(o n) -> o n", o=1)),
                 (cols[:, 2:3], col(a["L0_conv_b_out"])), (cols[:, 3:4], col(a["L0_conv_gamma1"])),
                 (cols[:, 4:5], col(a["L0_conv_beta1"])), (cols[:, 5:6], col(a["L0_conv_gamma2"])),
                 (cols[:, 6:7], col(a["L0_conv_beta2"])), (cols[:, 7:8], col(a["L1_conv_bout"])),
                 (w1["w1q"][:], a["L1_conv_Wq"][0:C]), (w1["w1k"][:], a["L1_conv_Wk"][0:C]),
                 (w1qe[:], a["L1_conv_Wq"][C:C + EMB]), (w1ke[:], a["L1_conv_Wk"][C:C + EMB]),
                 (w1["w1v"][:], a["L1_conv_Wv"]), (w1["w1o"][:], a["L1_conv_Wout"])]
        LOADED = 16 * len(loads)
        x_dram = a["x"].rearrange("b c h w -> b c (h w)")
        diag = lambda: V[:].rearrange("p t (h x) -> p t h x", x=VW)[:, :, :, 0:DH]
        block = ctx.enter_context(nc.Block())

        @block.sync
        def _(sp):
            with sp.Fori(0, B) as i:
                sg.wait(sp, "x1_done", 0, i)
                sg.up(sp.dma_start(xb[:], x_dram[bass.ds(i, 1)].rearrange("o c s -> (o c) s")), "x_load", 16)

        @block.gpsimd
        def _(pool):
            for dst, src in loads:
                sg.up(pool.dma_start(dst, src), "ga_loads", 16)
            sg.up(pool.memset(V[:], 0.0), "vones")

        def attention_pe(pe, l, i):
            src, sig, n = (xn, "ln_out", 1) if l == 0 else (x1, "x1_done", 1)
            wq, wk, wv = (w0[:, 0:C], w0[:, C:2 * C], w0[:, 2 * C:]) if l == 0 else (w1["w1q"][:], w1["w1k"][:], w1["w1v"][:])
            sg.wait(pe, sig, n, i)
            for dst, w, e, name in ((pM[0], wq, w1qe, "q_ps"), (pM[1], wk, w1ke, "k_ps")):
                if l == 1:
                    pe.matmul(dst[:], e[:], emb[:], start=True, stop=False)
                sg.up(pe.matmul(dst[:], w, src[:], start=(l == 0), stop=True), f"{name}{l}")
            for j in range(QT):
                o = pM[2][:, j * C:(j + 1) * C]
                ins = pe.matmul(o, src[:, j * P:(j + 1) * P], wv, start=True, stop=(l == 1))
                if l == 0:
                    ins = pe.matmul(o, onerow[:], bvrow[:], start=False, stop=True)
            sg.up(ins, f"v_ps{l}")

            def score(u):
                if u == 0:
                    sg.wait(pe, f"k_done{l}", 1, i)
                h, j = u // QT, u % QT
                sg.wait(pe, f"qm{l}", h + 1, i)
                if u >= len(pS):
                    sg.wait(pe, f"prob{l}", u + 1 - len(pS), i)
                sg.up(pe.matmul(pS[u % len(pS)][:], qm[h % 2][:, j * P:(j + 1) * P], kT[:], start=True, stop=True), f"score{l}")

            def turn(u):
                sg.wait(pe, f"pnorm{l}", u + 1, i)
                if u >= 2:
                    sg.wait(pe, f"ptcopy{l}", u - 1, i)
                for k in range(QT):
                    ins = pe.transpose(pT[u % 2][:, k * P:(k + 1) * P], Pb[u % 3][:, k * P:(k + 1) * P], t.ident[:])
                sg.up(ins, f"ptrans{l}")

            def weigh(h):
                sg.wait(pe, f"ptcopy{l}", QT * (h + 1), i)
                if h == 0:
                    sg.wait(pe, f"v_done{l}", 1, i)
                for k in range(QT):
                    ins = pe.matmul(pO[:], V[:, k, h * P:(h + 1) * P], PT[h % 2][:, k, :],
                                    start=(h == 0 and k == 0), stop=(h == HEADS - 1 and k == QT - 1))
                sg.up(ins, f"pv{l}")

            for u in range(AHEAD):
                score(u)
            for u in range(UNITS):
                turn(u)
                if u + AHEAD < UNITS:
                    score(u + AHEAD)
                if u % QT == 2 and u > QT:
                    weigh(u // QT - 1)
            weigh(HEADS - 1)

        def attention_act(act, l, i):
            sg.wait(act, f"q_ps{l}", 1, i)
            if l == 0:
                sg.up(act.activation(qT[:], pM[0][:], ACT.Identity, bias=cols[:, 0:1]), "q_done0")
            else:
                sg.up(act.activation(qT[:], pM[0][:], ACT.Copy), "q_done1")

            def prob(u):
                sg.wait(act, f"nmax{l}", u + 1, i)
                if u >= 3:
                    sg.wait(act, f"ptrans{l}", u - 2, i)
                sg.up(act.activation(Pb[u % 3][:], pS[u % len(pS)][:], ACT.Exp, bias=nm[:, u % 4:u % 4 + 1],
                                     accum_out=rs[:, u % 4:u % 4 + 1]), f"prob{l}")

            def copy(u):
                h, j = u // QT, u % QT
                sg.wait(act, f"ptrans{l}", u + 1, i)
                if h >= 2:
                    sg.wait(act, f"pv{l}", h - 1, i)
                sg.up(act.activation(PT[h % 2][:, :, j * P:(j + 1) * P],
                                     pT[u % 2][:].rearrange("p (k q) -> p k q", k=QT), ACT.Copy), f"ptcopy{l}")

            for u in range(UNITS):
                prob(u)
                if u >= 2:
                    copy(u - 2)
            copy(UNITS - 2)
            copy(UNITS - 1)

        def attention_dve(dve, l, i):
            sg.wait(dve, f"k_ps{l}", 1, i)
            if l == 0:
                sg.seq(dve, dve.tensor_scalar(kT[:], pM[1][:], cols[:, 1:2], None, ALU.add), "k_done0", i)
            else:
                sg.seq(dve, dve.tensor_copy(kT[:], pM[1][:]), "k_done1", i)
            sg.wait(dve, f"v_ps{l}", 1, i)
            sg.seq(dve, dve.tensor_copy(diag(), pM[2][:].rearrange("p (t h d) -> p t h d", t=QT, h=HEADS)), f"v_done{l}", i)
            sg.wait(dve, f"q_done{l}", 1, i)

            def mask_q(h):
                sg.seq(dve, dve.tensor_scalar(qm[h % 2][:], qT[:], t.hmask[:, h:h + 1], DH ** -0.5, ALU.mult, ALU.mult),
                       f"qm{l}", i)

            def norm(u):
                k = u % 4
                sg.wait(dve, f"prob{l}", u + 1, i)
                sg.seq(dve, dve.reciprocal(rr[:, k:k + 1], rs[:, k:k + 1]), f"recip{l}", i)
                sg.seq(dve, dve.tensor_scalar(Pb[u % 3][:], Pb[u % 3][:], rr[:, k:k + 1], None, ALU.mult), f"pnorm{l}", i)

            mask_q(0)
            mask_q(1)
            for u in range(UNITS):
                sg.wait(dve, f"score{l}", u + 1, i)
                sg.seq(dve, dve.tensor_reduce(nm[:, u % 4:u % 4 + 1], pS[u % len(pS)][:], AX.X, ALU.max, negate=True), f"nmax{l}", i)
                if u:
                    norm(u - 1)
                if u % QT == QT - 1 and u // QT + 2 < HEADS:
                    mask_q(u // QT + 2)
            norm(UNITS - 1)
            sg.wait(dve, f"pv{l}", HEADS, i)
            sg.seq(dve, dve.tensor_copy(oT[:], pO[:]), f"o_done{l}", i)

        @block.tensor
        def _(pe):
            sg.wait(pe, "ga_loads", LOADED)
            with pe.Fori(0, B) as i:
                sg.wait(pe, "dve_gn", 1, i)
                sg.up(pe.matmul(pM[0][:, 0:2], g4[:], mv[:], start=True, stop=True), "gn_mm")
                sg.wait(pe, "dve_gn", 3, i)
                sg.up(pe.matmul(pM[1][:, 0:1], g4[:], dev[:], start=True, stop=True), "gn_mm")
                layer_norm_pe(pe, sg, t.ones[:], gx[:], sq[:], pM[0][:], pM[1][:], 1, i, "gx", 1)
                attention_pe(pe, 0, i)
                layer_norm_pe(pe, sg, t.ones[:], oT[:], sq[:], pM[0][:], pM[1][:], 2, i, "o_done0", 1)
                sg.wait(pe, "ln_out", 2, i)
                sg.up(pe.matmul(pM[2][:], wo0[:], on[:], start=True, stop=True), "out_ps0")
                attention_pe(pe, 1, i)
                sg.wait(pe, "o_done1", 1, i)
                sg.up(pe.matmul(pM[2][:], w1["w1o"][:], oT[:], start=True, stop=True), "out_ps1")
                layer_norm_pe(pe, sg, t.ones[:], x2[:], sq[:], pM[0][:], pM[1][:], 3, i, "x2_done", 1)

        @block.scalar
        def _(act):
            sg.wait(act, "ga_loads", LOADED)
            with act.Fori(0, B) as i:
                sg.wait(act, "dve_gn", 3, i)
                sg.wait(act, "gn_mm", 2, i)
                sg.up(act.activation(gvar[:], pM[1][:, 0:1], ACT.Sqrt, bias=gms[:, 1:2]), "act_gn")
                layer_norm_act(act, sg, xc[:], sq[:], sd[:], pM[1][:], t.eps[:], 1, i)
                attention_act(act, 0, i)
                layer_norm_act(act, sg, xc[:], sq[:], sd[:], pM[1][:], t.eps[:], 2, i)
                attention_act(act, 1, i)
                layer_norm_act(act, sg, xc[:], sq[:], sd[:], pM[1][:], t.eps[:], 3, i)

        @block.vector
        def _(dve):
            sg.wait(dve, "ga_loads", LOADED)
            sg.wait(dve, "vones", 1)
            with dve.Fori(0, B) as i:
                sg.wait(dve, "x_load", 16, i)
                sg.seq(dve, dve.bn_stats(st6[:], xb[:]), "dve_step", i)
                dve.memset(rr[:, 0:1], 0.0)
                sg.seq(dve, dve.bn_aggr(mv[:], st6[:]), "dve_gn", i)
                sg.wait(dve, "gn_mm", 1, i)
                sg.seq(dve, dve.tensor_scalar(gms[:], pM[0][:, 0:2], EPS, None, ALU.add), "dve_step", i)
                sg.seq(dve, dve.tensor_copy(gms[:, 0:1], pM[0][:, 0:1]), "dve_gn", i)
                sg.seq(dve, dve.tensor_tensor(dev[:], mv[:, 0:1], gms[:, 0:1], ALU.subtract), "dve_step", i)
                sg.seq(dve, dve.tensor_tensor(dev[:], dev[:], dev[:], ALU.mult), "dve_gn", i)
                sg.wait(dve, "act_gn", 1, i)
                sg.seq(dve, dve.reciprocal(gvar[:], gvar[:]), "dve_step", i)
                sg.seq(dve, dve.tensor_scalar(gx[:], xb[:], gms[:, 0:1], gvar[:, 0:1], ALU.subtract, ALU.mult), "gx", i)
                layer_norm_dve(dve, sg, gx[:], xc[:], sd[:], pM[0][:], xn[:], 1, i, cols[:, 3:4], cols[:, 4:5])
                attention_dve(dve, 0, i)
                layer_norm_dve(dve, sg, oT[:], xc[:], sd[:], pM[0][:], on[:], 2, i, cols[:, 5:6], cols[:, 6:7])
                sg.wait(dve, "out_ps0", 1, i)
                sg.seq(dve, dve.scalar_tensor_tensor(out=x1[:], in0=pM[2][:], scalar=cols[:, 2:3], in1=xn[:],
                                                     op0=ALU.add, op1=ALU.add), "dve_step", i)
                sg.seq(dve, dve.tensor_tensor(x1[:], x1[:], xb[:], ALU.add), "x1_done", i)
                attention_dve(dve, 1, i)
                sg.wait(dve, "out_ps1", 1, i)
                sg.seq(dve, dve.scalar_tensor_tensor(out=x2[:], in0=pM[2][:], scalar=cols[:, 7:8], in1=x1[:],
                                                     op0=ALU.add, op1=ALU.add), "x2_done", i)
                layer_norm_dve(dve, sg, x2[:], xc[:], sd[:], pM[0][:], on[:], 3, i)
                one = lambda ap: ap.rearrange("p (o s) -> p o s", o=1)
                sg.seq(dve, dve.tensor_scalar(t.x2[:, bass.ds(i, 1), :], one(x2[:]), 0.0, None, ALU.add), "dve_step", i)
                sg.seq(dve, dve.tensor_scalar(t.z[:, bass.ds(i, 1), :], one(on[:]), 0.0, None, ALU.add), "ga_z", i)

        for name in sg.per:
            if sg.per[name]:
                sg.check(name)
def batch_attention(nc, t):
    with ExitStack() as ctx:
        def sb(name, shape, dt=F32):
            return ctx.enter_context(nc.sbuf_tensor(name, shape, dt))

        def ps(name):
            return ctx.enter_context(nc.psum_tensor(name, [P, S], F32))

        sg = Signals(nc, "batch")
        sg.add(ba_loads=0, zs_done=1, qkv_ps=B, qkv_done=B, ba_step=4 * B + 6, ba_shift=1, ba_exp=1, attn_done=B, ot_ps=1,
               ot_done=1, proj_ps=1, x3_done=1)
        w, wo = sb("ba_w_in", [P, 3 * C]), sb("ba_w_o", [P, C])
        brow, one, bo = sb("b_in", [1, 3 * C]), sb("one_r", [1, P]), sb("b_o", [P, 1])
        zs = sb("zs", [P, B, P])
        qkv = sb("qkv", [P, B, 3 * C])
        prod = sb("prod", [P, B * C])
        sc = sb("sc", [P, B, B, HEADS])
        mx, rs = sb("mx", [P, B, HEADS]), sb("rsum", [P, B, HEADS])
        o, oT = sb("o_t", [P, B, C]), sb("o_c", [P, B, P])
        pq = [ps(f"pq{n}") for n in range(2)]
        pt, pp = ps("pt"), ps("pp")
        a = t.dram
        loads = [(w[:], a["bw_in"]), (wo[:], a["bw_out"]), (brow[:], a["L2_attn_in_proj_bias"].rearrange("(o n) -> o n", o=1)),
                 (one[:], a["c_onerow"]), (bo[:], a["L2_attn_out_bias"].rearrange("(p o) -> p o", o=1))]
        block = ctx.enter_context(nc.Block())

        @block.sync
        def _(sp):
            for dst, src in loads:
                sg.up(sp.dma_start(dst, src), "ba_loads", 16)

        @block.tensor
        def _(pe):
            sg.wait(pe, "ba_loads", 16 * len(loads))
            with pe.Fori(0, QT) as i:
                sg.wait(pe, "zs_done", 1, i)
                for b in range(B):
                    if b >= 2:
                        sg.wait(pe, "qkv_done", b - 1, i)
                    pe.matmul(pq[b % 2][:, 0:3 * C], zs[:, b, :], w[:], start=True, stop=False)
                    sg.up(pe.matmul(pq[b % 2][:, 0:3 * C], one[:], brow[:], start=False, stop=True), "qkv_ps")
                for b in range(B):
                    sg.wait(pe, "attn_done", b + 1, i)
                    ins = pe.transpose(pt[:, b * P:(b + 1) * P], o[:, b, :], t.ident[:])
                sg.up(ins, "ot_ps")
                sg.wait(pe, "ot_done", 1, i)
                sg.up(pe.matmul(pp[:], wo[:], oT[:].rearrange("p b n -> p (b n)"), start=True, stop=True), "proj_ps")

        @block.scalar
        def _(act):
            with act.Fori(0, QT) as i:
                for b in range(B):
                    sg.wait(act, "qkv_ps", b + 1, i)
                    sg.up(act.activation(qkv[:, b, :], pq[b % 2][:, 0:3 * C], ACT.Copy), "qkv_done")
                sg.wait(act, "ba_shift", 1, i)
                sg.up(act.activation(sc[:], sc[:], ACT.Exp, scale=DH ** -0.5), "ba_exp")
                sg.wait(act, "ot_ps", 1, i)
                sg.up(act.activation(oT[:].rearrange("p b n -> p (b n)"), pt[:], ACT.Copy), "ot_done")

        @block.vector
        def _(dve):
            with dve.Fori(0, QT) as i:
                tile = lambda x: x[:, :, bass.ds(i * P, P)]
                sg.seq(dve, dve.tensor_scalar(zs[:], tile(t.z), 0.0, None, ALU.add), "zs_done", i)
                sg.wait(dve, "qkv_done", B, i)
                keys, values = qkv[:, :, C:2 * C], qkv[:, :, 2 * C:3 * C]
                cube = prod[:].rearrange("p (b c) -> p b c", b=B)
                for b in range(B):
                    query = qkv[:, b:b + 1, 0:C].to_broadcast([P, B, C])
                    sg.seq(dve, dve.tensor_tensor(cube, query, keys, ALU.mult), "ba_step", i)
                    sg.seq(dve, dve.tensor_reduce(sc[:, b].rearrange("p k h -> p (k h)"),
                                                  prod[:].rearrange("p (g d) -> p g d", d=DH), AX.X, ALU.add), "ba_step", i)
                bykey = sc[:].rearrange("p b k h -> p b h k")
                sg.seq(dve, dve.tensor_reduce(mx[:], bykey, AX.X, ALU.max), "ba_step", i)
                for b in range(B):
                    ins = dve.tensor_tensor(sc[:, b], sc[:, b], mx[:, b:b + 1, :].to_broadcast([P, B, HEADS]), ALU.subtract)
                    if b < B - 1:
                        sg.seq(dve, ins, "ba_step", i)
                sg.seq(dve, ins, "ba_shift", i)
                sg.wait(dve, "ba_exp", 1, i)
                sg.seq(dve, dve.tensor_reduce(rs[:], bykey, AX.X, ALU.add), "ba_step", i)
                sg.seq(dve, dve.reciprocal(rs[:], rs[:]), "ba_step", i)
                for b in range(B):
                    sg.seq(dve, dve.tensor_tensor(prod[:].rearrange("p (k h d) -> p k h d", k=B, h=HEADS),
                                                  values.rearrange("p k (h d) -> p k h d", d=DH),
                                                  sc[:, b].rearrange("p k (h o) -> p k h o", o=1).to_broadcast([P, B, HEADS, DH]),
                                                  ALU.mult), "ba_step", i)
                    sg.seq(dve, dve.tensor_reduce(o[:, b, :], prod[:].rearrange("p (k c) -> p c k", k=B), AX.X, ALU.add), "ba_step", i)
                    ob = o[:, b, :].rearrange("p (h d) -> p h d", d=DH)
                    sg.seq(dve, dve.tensor_tensor(ob, ob, rs[:, b, :].rearrange("p (h o) -> p h o", o=1).to_broadcast([P, HEADS, DH]),
                                                  ALU.mult), "attn_done", i)
                sg.wait(dve, "proj_ps", 1, i)
                sg.seq(dve, dve.scalar_tensor_tensor(out=tile(t.x3), in0=pp[:].rearrange("p (b n) -> p b n", b=B), scalar=bo[:, 0:1],
                                                     in1=tile(t.x2), op0=ALU.add, op1=ALU.add), "x3_done", i)

        for name in sg.per:
            if sg.per[name]:
                sg.check(name)


def flow(nc, t):
    NV = KH * B
    HALF = NV // 2
    with ExitStack() as ctx:
        def sb(name, shape, dt=F32):
            return ctx.enter_context(nc.sbuf_tensor(name, shape, dt))

        def ps(name):
            return ctx.enter_context(nc.psum_tensor(name, [P, S], F32))

        sg = Signals(nc, "flow")
        sg.add(fl_loads=0, sel16=0, y_mm=0, y_step=0, y_act=0, w13_ps=0, w13_done=0, v_ps=0, prep=0, part=0, rest=0, b2_moved=0,
               ones_set=0, wm_ps=0, scales=0, k_ps=0, slope=0, states=0)
        step = dict(u1=2 * KH, h1=2 * KH, hi1=2 * KH, in1=2 * KH, l2_ps=2 * KH, u2=2 * KH, h2=2 * KH, hi2=2 * KH, in2=2 * KH,
                    l13_ps=2 * KH, g13=2 * KH, gsum=3, acc=1, v_shifted=2, hsum=3, hist=1)
        sg.add(**{name: UN * k for name, k in step.items()})

        def wait(eng, name, n, w, i):
            sg.wait(eng, name, w * step[name] + n, i)

        w1, w3n, w2f, w13f, w3 = sb("w1", [P, HID]), sb("w3n", [P, HID]), sb("w2f", [P, KH, HID]), sb("w13f", [P, KH, HID]), sb("w3", [P, KH, C])
        W2, W13 = sb("W2", [P, NP, KH, HID], F16), sb("W13", [P, NP, KH, HID], F16)
        b1, b2r, b2s, B2, b3 = sb("b1", [P, KH]), sb("b2r", [KH, P]), sb("b2s", [KH, BP, P], BF16), sb("B2", [BP * KH, P], BF16), sb("b3", [P, 1])
        sel_f, sel = sb("sel_f", [BP * KH, 32]), sb("sel", [BP * KH, 32], BF16)
        yc, ysq, ysd, y0, b3dt = sb("yc", [P, B]), sb("ysq", [P, B]), sb("ysd", [P, B]), sb("y0", [P, B]), sb("b3dt", [P, 1])
        half_b, full_b = sb("half_b", [P, NV]), sb("full_b", [P, NV])
        v_half, v_full, acc = sb("v_half", [P, NV]), sb("v_full", [P, NV]), sb("acc", [P, NV])
        u1, u2, g = sb("u1", [P, NV]), sb("u2", [P, NV]), sb("g", [P, 4, NV])
        g12, g012, gall = sb("g12", [P, NV]), sb("g012", [P, NV]), sb("gall", [P, NV])
        wmax, wpow, winv, wdiag = sb("wmax", [P, 2]), sb("wpow", [2, 1]), sb("winv", [2, 1]), sb("wdiag", [2, 4])
        wscale, unscale2, coefs = sb("wscale", [P, 2]), sb("unscale2", [P, 1]), sb("coefs", [P, 3])
        h1, h2 = sb("h1", [P, NV]), sb("h2", [P, 4, NV])
        H1, H2 = sb("H1", [P, KH, 2, B], F16), sb("H2", [P, KH, 2, B], F16)
        inner, outer, both = sb("inner", [P, NV]), sb("outer", [P, NV]), sb("both", [P, NV])
        hist = sb("hist_h", [P, KH, S, B])
        slope, Y, ones1 = sb("slope_d", [P, S, B]), sb("Y", [P, B, S]), sb("ones1", [P, S])
        p2, p1, pw = [ps("p2a"), ps("p2b")], [ps("p1a"), ps("p1b")], [ps("pw0"), ps("pw1")]
        py, pv = ps("py"), ps("pv_ps")
        hv = lambda x, q: x[:, HALF * q:HALF * q + HALF]
        mb = lambda x: x.rearrange("p (m b) -> p m b", b=B)
        parts = lambda x: x[:, 0:NV].rearrange("p (m q b) -> p m b q", m=2, q=2)
        splits = [(b2r[:], lambda q: b2s[:, q, :]), (w2f[:], lambda q: W2[:, q]), (w13f[:], lambda q: W13[:, q])]
        a = t.dram
        loads = [(w1[:], a["ff_w1"]), (w3n[:], a["L2_ffn_W3"]), (w2f[:], a["ff_w2"]), (w3[:], a["ff_w3"]), (b1[:], a["ff_b1"]),
                 (b2r[:], a["L2_ffn_b2"].rearrange("(m p) -> m p", p=P)), (b3[:], a["L2_ffn_b3"].rearrange("(p o) -> p o", o=1)),
                 (sel_f[:], a["c_sel"])]
        block = ctx.enter_context(nc.Block())

        @block.sync
        def _(sp):
            for dst, src in loads:
                sg.up(sp.dma_start(dst, src), "fl_loads", 16)
            sg.wait(sp, "part", 7)
            for q in range(BP):
                sg.up(sp.dma_start(B2[KH * q:KH * q + KH, :], b2s[:, q, :]), "b2_moved", 16)

        @block.gpsimd
        def _(pool):
            sg.up(pool.memset(ones1[:], 1.0), "ones_set")
            sg.up(pool.memset(hist[:, :, STEPS:S, :], 0.0), "ones_set")
            sg.wait(pool, "prep", 6)
            sg.up(pool.tensor_tensor(v_half[:], u1[:], half_b[:], ALU.add), "v_shifted")
            sg.up(pool.tensor_tensor(v_full[:], u1[:], full_b[:], ALU.add), "v_shifted")
            sg.n["v_shifted"] = 0
            with pool.Fori(0, STEPS // UN) as i:
                for w in range(UN):
                    wait(pool, "h2", 6, w, i)
                    sg.seq(pool, pool.tensor_tensor(inner[:], h2[:, 1, :], h2[:, 2, :], ALU.add), "hsum", i)
                    wait(pool, "g13", 6, w, i)
                    sg.seq(pool, pool.tensor_tensor(g12[:], g[:, 1, :], g[:, 2, :], ALU.add), "gsum", i)
                    sg.seq(pool, pool.tensor_tensor(g012[:], g12[:], g[:, 0, :], ALU.add), "gsum", i)
                    sg.seq(pool, pool.tensor_tensor(gall[:], g12[:], g012[:], ALU.add), "gsum", i)
                    wait(pool, "h2", 8, w, i)
                    sg.seq(pool, pool.tensor_tensor(outer[:], h2[:, 0, :], h2[:, 3, :], ALU.add), "hsum", i)
                    sg.seq(pool, pool.tensor_tensor(both[:], inner[:], outer[:], ALU.add), "hsum", i)
                    sg.up(pool.tensor_tensor(hist[:, :, bass.ds(UN * i + w, 1), :].rearrange("p m o b -> p m (o b)"), mb(both[:]),
                                             mb(inner[:]), ALU.add), "hist")
                    wait(pool, "u1", 2 + 2 * KH, w, i)
                    sg.up(pool.tensor_tensor(v_half[:], u1[:], half_b[:], ALU.add), "v_shifted")
                    sg.up(pool.tensor_tensor(v_full[:], u1[:], full_b[:], ALU.add), "v_shifted")

        def product(pe, i, w, out, W, H, ready, n, done, seeded):
            def tiles(m, ks):
                for k in ks:
                    for q in range(NP):
                        first = not seeded and k == 0 and q == 0 and m % 2 == 0
                        ins = pe.matmul(out[m // 2][:, HALF * (m % 2):HALF * (m % 2) + HALF], W[:, q, k, P * m:P * m + P],
                                        H[:, k, :, :].rearrange("p q b -> p (q b)"), start=first, stop=(k == KH - 1 and q == NP - 1),
                                        skip_group_check=True)
                return ins

            wait(pe, ready, n + 1, w, i)
            for m in (range(2) if seeded else range(KH)):
                tiles(m, (0, 1))
            wait(pe, ready, n + 2, w, i)
            for m in range(2):
                ins = tiles(m, (2, 3))
            sg.up(ins, done)
            for m in (2, 3):
                ins = tiles(m, range(KH) if seeded else (2, 3))
            sg.up(ins, done)

        @block.tensor
        def _(pe):
            sg.wait(pe, "fl_loads", 16 * len(loads))
            sg.up(pe.matmul(py[:, 0:B], t.ones[:], t.x3[:, :, 0], start=True, stop=True), "y_mm")
            sg.wait(pe, "y_act", 1)
            sg.up(pe.matmul(py[:, 0:B], t.ones[:], ysq[:], start=True, stop=True), "y_mm")
            for k in range(KH):
                if k >= 2:
                    sg.wait(pe, "w13_done", k - 1)
                sg.up(pe.matmul(pw[k % 2][:], w3n[:, P * k:P * k + P], w1[:], start=True, stop=True), "w13_ps")
            sg.wait(pe, "y_step", 3)
            for m in range(KH):
                pe.matmul(pv[:, B * m:B * m + B], w1[:, P * m:P * m + P], y0[:], start=True, stop=True)
            for m in range(KH):
                ins = pe.matmul(pv[:, NV + m:NV + m + 1], w1[:, P * m:P * m + P], b3[:], start=True, stop=True)
            sg.up(ins, "v_ps")
            sg.wait(pe, "scales", 2)
            sg.up(pe.transpose(py[0:2, :P], wmax[:], t.ident[:]), "wm_ps")
            sg.wait(pe, "scales", 8)
            sg.up(pe.matmul(py[:, 0:4], t.ones[0:2, :], wdiag[:], start=True, stop=True), "wm_ps")
            sg.wait(pe, "rest", 6)
            sg.wait(pe, "b2_moved", 16 * BP)
            sg.wait(pe, "sel16", 1)
            with pe.Fori(0, STEPS // UN) as i:
                for w in range(UN):
                    for e in range(4):
                        wait(pe, "u2", 2 * e, w, i)
                        for q in range(2):
                            pe.matmul(p2[q][:, 0:NV], B2[:], sel[:, NV * q:NV * q + NV], start=True, stop=False, skip_group_check=True)
                        product(pe, i, w, p2, W2, H1, "in1", 2 * e, "l2_ps", True)
                        wait(pe, "g13", 2 * e, w, i)
                        product(pe, i, w, p1, W13, H2, "in2", 2 * e, "l13_ps", False)
            pe.wait_ge(sg.sem["hist"], STEPS)
            sg.wait(pe, "ones_set", 2)
            BLK = S // 4
            for j in range(4):
                if j >= 2:
                    sg.wait(pe, "slope", j - 1)
                for k in range(KH):
                    ins = pe.matmul(pw[j % 2][:], w3[:, k, :], hist[:, k, BLK * j:BLK * j + BLK, :].rearrange("p s b -> p (s b)"),
                                    start=(k == 0), stop=(k == KH - 1))
                sg.up(ins, "k_ps")

        @block.scalar
        def _(act):
            sg.wait(act, "fl_loads", 16 * len(loads))
            sg.up(act.activation(sel[:], sel_f[:], ACT.Copy), "sel16")
            sg.wait(act, "y_step", 1)
            sg.up(act.activation(ysq[:], yc[:], ACT.Square), "y_act")
            sg.wait(act, "y_mm", 2)
            sg.up(act.activation(ysd[:], py[:, 0:B], ACT.Sqrt, bias=t.eps[:]), "y_act")
            for k in range(KH):
                sg.wait(act, "w13_ps", k + 1)
                sg.up(act.activation(w13f[:, k, :], pw[k % 2][:], ACT.Copy), "w13_done")
            sg.wait(act, "w13_done", KH)
            for q in range(BP):
                for n, (full, split) in enumerate(splits[:3 if q < NP else 1]):
                    if q:
                        sg.wait(act, "rest", 3 * (q - 1) + n + 1)
                    elif n == 0:
                        sg.wait(act, "scales", 13)
                    sg.up(act.activation(split(q), full, ACT.Copy), "part")
            with act.Fori(0, STEPS // UN) as i:
                for w in range(UN):
                    for e in range(4):
                        for q in range(2):
                            wait(act, "u1", 2 * e + q + 1, w, i)
                            sg.up(act.activation(hv(h1, q), hv(u1, q), ACT.Tanh), "h1")
                        for q in range(2):
                            wait(act, "u2", 2 * e + q + 1, w, i)
                            if e == 0 and q == 0:
                                wait(act, "hsum", 0, w, i)
                            sg.up(act.activation(h2[:, e, HALF * q:HALF * q + HALF], hv(u2, q), ACT.Tanh, scale=unscale2[:, 0:1]), "h2")

        @block.vector
        def _(dve):
            sg.wait(dve, "y_mm", 1)
            sg.seq(dve, dve.tensor_tensor(yc[:], t.x3[:, :, 0], py[:, 0:B], ALU.subtract), "y_step")
            sg.wait(dve, "y_act", 2)
            sg.seq(dve, dve.reciprocal(ysd[:], ysd[:]), "y_step")
            sg.seq(dve, dve.tensor_tensor(y0[:], yc[:], ysd[:], ALU.mult), "y_step")
            sg.wait(dve, "v_ps", 1)
            wide = lambda x: x.rearrange("p (m o) -> p m o", o=1).to_broadcast([P, KH, B])
            sg.seq(dve, dve.tensor_copy(h1[:, 0:KH], pv[:, NV:NV + KH]), "prep")
            sg.seq(dve, dve.tensor_scalar(mb(half_b[:]), wide(h1[:, 0:KH]), DT / 2, None, ALU.mult), "prep")
            sg.seq(dve, dve.tensor_scalar(mb(full_b[:]), wide(h1[:, 0:KH]), DT, None, ALU.mult), "prep")
            sg.seq(dve, dve.tensor_scalar(b3dt[:], b3[:], DT, None, ALU.mult), "prep")
            sg.seq(dve, dve.tensor_tensor(mb(u1[:]), mb(pv[:, 0:NV]), wide(b1[:]), ALU.add), "prep")
            sg.seq(dve, dve.tensor_copy(u2[:, 0:1], u1[:, 0:1]), "prep")
            sg.seq(dve, dve.tensor_reduce(wmax[:, 0:1], w2f[:].rearrange("p k n -> p (k n)"), AX.X, ALU.max, apply_absolute_value=True), "scales")
            sg.wait(dve, "w13_done", KH)
            sg.seq(dve, dve.tensor_reduce(wmax[:, 1:2], w13f[:].rearrange("p k n -> p (k n)"), AX.X, ALU.max, apply_absolute_value=True), "scales")
            sg.wait(dve, "wm_ps", 1)
            sg.seq(dve, dve.tensor_reduce(wpow[:], py[0:2, 0:P], AX.X, ALU.max), "scales")
            sg.seq(dve, dve.tensor_scalar(wpow[:], wpow[:], 2.0 ** -40, None, ALU.max), "scales")
            bits = lambda x: x.bitcast(mybir.dt.int32)
            sg.seq(dve, dve.tensor_scalar(bits(wpow[:]), bits(wpow[:]), 255 << 23, None, ALU.bitwise_and), "scales")
            sg.seq(dve, dve.tensor_scalar(bits(winv[:]), bits(wpow[:]), -1, 254 << 23, ALU.mult, ALU.add), "scales")
            for n, x in enumerate((wpow, winv)):
                sg.seq(dve, dve.tensor_scalar(wdiag[:, 2 * n:2 * n + 2], t.ident[0:2, 0:2], x[:, 0:1], None, ALU.mult), "scales")
            sg.wait(dve, "wm_ps", 2)
            sg.seq(dve, dve.tensor_scalar(wscale[:], py[:, 2:4], C * WMAX, None, ALU.mult), "scales")
            sg.seq(dve, dve.tensor_scalar(unscale2[:], py[:, 0:1], C / WMAX / HSCALE, None, ALU.mult), "scales")
            for n, c in enumerate((DT / 2, DT, DT / 6)):
                sg.seq(dve, dve.tensor_scalar(coefs[:, n:n + 1], py[:, 1:2], C / WMAX / HSCALE * c, None, ALU.mult), "prep")
            for x, n in ((b2r[:], 0), (w2f[:], 0), (w13f[:], 1)):
                sg.seq(dve, dve.tensor_scalar(x, x, wscale[0:x.shape[0], n:n + 1], None, ALU.mult), "scales")
            for q in range(BP - 1):
                for n, (full, split) in enumerate(splits[:3 if q < NP - 1 else 1]):
                    sg.wait(dve, "part", 3 * q + n + 1)
                    sg.seq(dve, dve.tensor_tensor(full, full, split(q), ALU.subtract), "rest")
            sg.wait(dve, "part", 7)
            for n in range(2):
                sg.seq(dve, dve.tensor_copy(u2[:, n:n + 1], u1[:, n:n + 1]), "rest")
            for q in range(2):
                dve.tensor_copy(hv(u2, q), hv(u1, q)).then_inc(sg.sem["u1"], 1)
            dve.wait_ge(sg.sem["u1"], 2)

            def split_h(h, H, q, sig, n, w, i, hi, done):
                wait(dve, sig, n + 1, w, i)
                Hq = H[:, 2 * q:2 * q + 2, :, :]
                sg.seq(dve, dve.tensor_scalar(Hq[:, :, 0, :], mb(h), HSCALE, None, ALU.mult), hi, i)
                sg.up(dve.scalar_tensor_tensor(out=Hq[:, :, 1, :], in0=mb(h), scalar=HSCALE, in1=Hq[:, :, 0, :],
                                               op0=ALU.mult, op1=ALU.subtract), done)

            with dve.Fori(0, STEPS // UN) as i:
                for w in range(UN):
                    for e, next_c in enumerate((0, 0, 1, 2)):
                        n = 2 * e
                        for q in range(2):
                            split_h(hv(h1, q), H1, q, "h1", n + q, w, i, "hi1", "in1")
                        for q in range(2):
                            wait(dve, "l2_ps", n + q + 1, w, i)
                            sg.up(dve.tensor_reduce(mb(hv(u2, q)), parts(p2[q]), AX.X, ALU.add), "u2")
                        for q in range(2):
                            split_h(h2[:, e, HALF * q:HALF * q + HALF], H2, q, "h2", n + q, w, i, "hi2", "in2")
                        if e == 3:
                            wait(dve, "gsum", 3, w, i)
                            sg.seq(dve, dve.scalar_tensor_tensor(out=acc[:], in0=gall[:], scalar=coefs[:, 2:3], in1=v_full[:],
                                                                 op0=ALU.mult, op1=ALU.add), "acc", i)
                        for q in range(2):
                            wait(dve, "l13_ps", n + q + 1, w, i)
                            gq = g[:, e, HALF * q:HALF * q + HALF]
                            sg.seq(dve, dve.tensor_reduce(mb(gq), parts(p1[q]), AX.X, ALU.add), "g13", i)
                            if e == 0:
                                wait(dve, "v_shifted", 2, w, i)
                            base = (v_half, v_half, v_full, acc)[e]
                            sg.up(dve.scalar_tensor_tensor(out=hv(u1, q), in0=gq, scalar=coefs[:, next_c:next_c + 1],
                                                           in1=hv(base, q), op0=ALU.mult, op1=ALU.add), "u1")
            BLK = S // 4
            for j in range(4):
                sg.wait(dve, "k_ps", j + 1)
                sg.seq(dve, dve.tensor_scalar(slope[:, BLK * j:BLK * j + BLK, :].rearrange("p s b -> p (s b)"), pw[j % 2][:],
                                              DT / 6, b3dt[:, 0:1], ALU.mult, ALU.add), "slope")
            sg.seq(dve, dve.tensor_copy(Y[:, :, 0], y0[:]), "states")
            for b in range(B):
                sg.seq(dve, dve.tensor_tensor_scan(Y[:, b, 1:S], ones1[:, 0:STEPS], slope[:, 0:STEPS, b], y0[:, b:b + 1],
                                                   ALU.mult, ALU.add), "states")
            sg.seq(dve, dve.tensor_tensor(t.x4[:], t.x3[:], Y[:], ALU.add), "states")

        for name in sg.per:
            if sg.per[name]:
                sg.check(name)


def window_attention(nc, t):
    with ExitStack() as ctx:
        def sb(name, shape, dt=F32):
            return ctx.enter_context(nc.sbuf_tensor(name, shape, dt))

        def ps(name):
            return ctx.enter_context(nc.psum_tensor(name, [P, S], F32))

        R = DIL
        sg = Signals(nc, "window")
        sg.add(wa_loads=0, vzero=0, xb_done=1, dve_step=3, ln_mean=2, ln_var=2, ln_sq=2, ln_sd=2, ln_cent=2, ln_out=2,
               wq_ps=1, wk_ps=1, wv_ps=1, wq_done=1, wk_done=1, wv_done=1, wqm=HEADS, wscore=HEADS, wmask=HEADS, wmax=2 * HEADS,
               wprob=HEADS, wpadw=HEADS, wsum=3 * HEADS, wnorm=HEADS, wtrans=HEADS, wcopy=HEADS, wpv=HEADS, wo_done=1,
               f_ps=1, f_done=1, g_ps=1, g_done=1, x5_done=1, logit_ps=1, wa_end=3)
        xb, z, xc, sq, sd = (sb("w" + n, [P, S]) for n in ("xb", "z", "xc", "sq", "sd"))
        qT, kT, xa, f, g, x5, z5 = (sb("w" + n, [P, S]) for n in ("qT", "kT", "xa", "f", "g", "x5", "z5"))
        qm = [sb(f"wqm{n}", [P, S]) for n in range(2)]
        V = sb("wV", [P, R, HEADS * VW])
        sc = [sb(f"wsc{n}", [P, R, P]) for n in range(2)]
        PT = [sb(f"wPT{n}", [P, R, P]) for n in range(2)]
        m, padw, rs = ([sb(f"w{name}{n}", [P, R]) for n in range(2)] for name in ("m", "padw", "rs"))
        w = {n: sb("wa_" + n, [P, C]) for n in ("q", "k", "v", "f1", "f2")}
        bias, gate, band, pads = sb("wa_bias", [P, 2]), sb("wa_gate", [P, NE]), sb("wa_band", [P, P]), sb("wa_pads", [P, 2])
        pS, pT, pM = [ps("wpS0"), ps("wpS1")], [ps("wpT0"), ps("wpT1")], [ps(f"wpM{n}") for n in range(3)]
        pO = ps("wpO")
        a = t.dram
        col = lambda ap: ap.rearrange("(p o) -> p o", o=1)
        loads = [(w["q"][:], a["L3_attn_Wq"]), (w["k"][:], a["L3_attn_Wk"]), (w["v"][:], a["L3_attn_Wv"]), (w["f1"][:], a["L3_attn_Wff1"]),
                 (w["f2"][:], a["L3_attn_Wff2"]), (bias[:, 0:1], col(a["L3_attn_bff1"])), (bias[:, 1:2], col(a["L3_attn_bff2"])),
                 (gate[:], a["gate_t"]), (band[:], a["c_band"]), (pads[:], a["c_pads"])]
        res = lambda x, r: x[:, r:S:R]
        one = lambda ap: ap.rearrange("p (o s) -> p o s", o=1)
        block = ctx.enter_context(nc.Block())

        @block.sync
        def _(sp):
            for dst, src in loads:
                sg.up(sp.dma_start(dst, src), "wa_loads", 16)

        @block.gpsimd
        def _(pool):
            sg.up(pool.memset(V[:], 0.0), "vzero")

        @block.tensor
        def _(pe):
            sg.wait(pe, "wa_loads", 16 * len(loads))
            with pe.Fori(0, B) as i:
                layer_norm_pe(pe, sg, t.ones[:], xb[:], sq[:], pM[0][:], pM[1][:], 1, i, "xb_done", 1)
                sg.wait(pe, "ln_out", 1, i)
                sg.up(pe.matmul(pM[0][:], w["q"][:], z[:], start=True, stop=True), "wq_ps")
                sg.up(pe.matmul(pM[1][:], w["k"][:], z[:], start=True, stop=True), "wk_ps")
                for r in range(R):
                    ins = pe.matmul(pM[2][:, r * P:(r + 1) * P], res(z, r), w["v"][:], start=True, stop=True)
                sg.up(ins, "wv_ps")

                def score(h):
                    sg.wait(pe, "wqm", h + 1, i)
                    if h == 0:
                        sg.wait(pe, "wk_done", 1, i)
                    if h >= 2:
                        sg.wait(pe, "wmask", h - 1, i)
                    for r in range(R):
                        ins = pe.matmul(pS[h % 2][:, r * P:(r + 1) * P], res(qm[h % 2], r), res(kT, r), start=True, stop=True)
                    sg.up(ins, "wscore")

                def weigh(h):
                    if h == 0:
                        sg.wait(pe, "wv_done", 1, i)
                    sg.wait(pe, "wcopy", h + 1, i)
                    for r in range(R):
                        ins = pe.matmul(pO[:, r * P:(r + 1) * P], V[:, r, h * P:(h + 1) * P], PT[h % 2][:, r, :],
                                        start=(h == 0 and r == 0), stop=(h == HEADS - 1), skip_group_check=True)
                    sg.up(ins, "wpv")

                score(0)
                score(1)
                for h in range(HEADS):
                    sg.wait(pe, "wnorm", h + 1, i)
                    if h >= 2:
                        sg.wait(pe, "wcopy", h - 1, i)
                    for r in range(R):
                        ins = pe.transpose(pT[h % 2][:, r * P:(r + 1) * P], sc[h % 2][:, r, :], t.ident[:])
                    sg.up(ins, "wtrans")
                    if h + 2 < HEADS:
                        score(h + 2)
                    if h:
                        weigh(h - 1)
                weigh(HEADS - 1)
                sg.wait(pe, "wo_done", 1, i)
                sg.up(pe.matmul(pM[2][:], w["f1"][:], xa[:], start=True, stop=True), "f_ps")
                sg.wait(pe, "f_done", 1, i)
                sg.up(pe.matmul(pM[0][:], w["f2"][:], f[:], start=True, stop=True), "g_ps")
                layer_norm_pe(pe, sg, t.ones[:], x5[:], sq[:], pM[0][:], pM[1][:], 2, i, "x5_done", 1)
                sg.wait(pe, "ln_out", 2, i)
                for j in range(QT):
                    ins = pe.matmul(pM[2][:, j * NE:(j + 1) * NE], z5[:, j * P:(j + 1) * P], gate[:], start=True, stop=True)
                sg.up(ins, "logit_ps")

        @block.scalar
        def _(act):
            sg.wait(act, "wa_loads", 16 * len(loads))
            with act.Fori(0, B) as i:
                layer_norm_act(act, sg, xc[:], sq[:], sd[:], pM[1][:], t.eps[:], 1, i)
                sg.wait(act, "wq_ps", 1, i)
                sg.up(act.activation(qT[:], pM[0][:], ACT.Copy), "wq_done")
                for h in range(HEADS + 1):
                    if h < HEADS:
                        k = h % 2
                        sg.wait(act, "wmax", 2 * h + 2, i)
                        sg.up(act.activation(padw[k][:], m[k][:], ACT.Exp), "wpadw")
                        for r in range(R):
                            ins = act.activation(sc[k][:, r, :], sc[k][:, r, :], ACT.Exp, bias=m[k][:, r:r + 1],
                                                 accum_out=rs[k][:, r:r + 1])
                        sg.up(ins, "wprob")
                    if h:
                        sg.wait(act, "wtrans", h, i)
                        if h >= 3:
                            sg.wait(act, "wpv", h - 2, i)
                        sg.up(act.activation(PT[(h - 1) % 2][:].rearrange("p r q -> p (r q)"), pT[(h - 1) % 2][:], ACT.Copy), "wcopy")
                sg.wait(act, "f_ps", 1, i)
                sg.up(act.activation(f[:], pM[2][:], ACT.Relu, bias=bias[:, 0:1]), "f_done")
                sg.wait(act, "g_ps", 1, i)
                sg.up(act.activation(g[:], pM[0][:], ACT.Relu, bias=bias[:, 1:2]), "g_done")
                layer_norm_act(act, sg, xc[:], sq[:], sd[:], pM[1][:], t.eps[:], 2, i)

        @block.vector
        def _(dve):
            sg.wait(dve, "wa_loads", 16 * len(loads))
            sg.wait(dve, "vzero", 1)
            with dve.Fori(0, B) as i:
                sg.seq(dve, dve.tensor_scalar(one(xb[:]), t.x4[:, bass.ds(i, 1), :], 0.0, None, ALU.add), "xb_done", i)
                layer_norm_dve(dve, sg, xb[:], xc[:], sd[:], pM[0][:], z[:], 1, i)
                sg.wait(dve, "wk_ps", 1, i)
                sg.seq(dve, dve.tensor_copy(kT[:], pM[1][:]), "wk_done", i)
                sg.wait(dve, "wv_ps", 1, i)
                sg.seq(dve, dve.tensor_copy(V[:].rearrange("p t (h x) -> p t h x", x=VW)[:, :, :, 0:DH],
                                            pM[2][:].rearrange("p (t h d) -> p t h d", t=R, h=HEADS)), "wv_done", i)
                sg.wait(dve, "wq_done", 1, i)

                def queries(h):
                    sg.seq(dve, dve.tensor_scalar(qm[h % 2][:], qT[:], t.hmask[:, h:h + 1], None, ALU.mult), "wqm", i)

                def masked(h):
                    k = h % 2
                    sg.wait(dve, "wscore", h + 1, i)
                    if h >= 2:
                        sg.wait(dve, "wtrans", h - 1, i)
                    sg.seq(dve, dve.tensor_tensor(sc[k][:], pS[k][:].rearrange("p (r k) -> p r k", r=R),
                                                  band[:].rearrange("p (o k) -> p o k", o=1).to_broadcast([P, R, P]), ALU.add), "wmask", i)
                    sg.seq(dve, dve.tensor_reduce(m[k][:], sc[k][:], AX.X, ALU.max), "wmax", i)
                    sg.seq(dve, dve.tensor_scalar(m[k][:], m[k][:], pads[:, 0:1], -1.0, ALU.max, ALU.mult), "wmax", i)

                def normalised(h):
                    k = h % 2
                    sg.wait(dve, "wpadw", h + 1, i)
                    sg.wait(dve, "wprob", h + 1, i)
                    sg.seq(dve, dve.scalar_tensor_tensor(out=rs[k][:], in0=padw[k][:], scalar=pads[:, 1:2], in1=rs[k][:],
                                                         op0=ALU.mult, op1=ALU.add), "wsum", i)
                    sg.seq(dve, dve.tensor_scalar(rs[k][:], rs[k][:], float(DH) ** 0.5, None, ALU.mult), "wsum", i)
                    sg.seq(dve, dve.reciprocal(rs[k][:], rs[k][:]), "wsum", i)
                    sg.seq(dve, dve.tensor_tensor(sc[k][:], sc[k][:], rs[k][:].rearrange("p (r o) -> p r o", o=1).to_broadcast([P, R, P]),
                                                  ALU.mult), "wnorm", i)

                queries(0)
                queries(1)
                for h in range(HEADS + 1):
                    if h < HEADS:
                        masked(h)
                    if h:
                        normalised(h - 1)
                    if h + 2 < HEADS:
                        queries(h + 2)
                sg.wait(dve, "wpv", HEADS, i)
                sg.seq(dve, dve.tensor_copy(xa[:].rearrange("p (a r) -> p r a", r=R), pO[:].rearrange("p (r a) -> p r a", r=R)), "wo_done", i)
                sg.seq(dve, dve.tensor_tensor(x5[:], xb[:], xa[:], ALU.add), "dve_step", i)
                sg.wait(dve, "g_done", 1, i)
                sg.seq(dve, dve.tensor_tensor(x5[:], x5[:], g[:], ALU.add), "x5_done", i)
                layer_norm_dve(dve, sg, x5[:], xc[:], sd[:], pM[0][:], z5[:], 2, i)
                sg.seq(dve, dve.tensor_scalar(t.x5[:, bass.ds(i, 1), :], one(x5[:]), 0.0, None, ALU.add), "wa_end", i)
                sg.seq(dve, dve.tensor_scalar(t.z[:, bass.ds(i, 1), :], one(z5[:]), 0.0, None, ALU.add), "wa_end", i)
                sg.wait(dve, "logit_ps", 1, i)
                sg.seq(dve, dve.tensor_scalar(t.logits[:, bass.ds(i, 1), :, :].rearrange("p o j e -> p o (j e)"),
                                              one(pM[2][:, 0:QT * NE]), 0.0, None, ALU.add), "wa_end", i)

        for name in sg.per:
            if sg.per[name]:
                sg.check(name)


def experts(nc, t, out_dram):
    UT = 2 * B
    TURNS = NE // 2
    LOADS = 16 * 9
    ITEMS = 2 * NB
    XIT = B * NB
    ORDER = [NB] + list(range(NB))
    CHUNKS = [ORDER[0:2], ORDER[2:4], ORDER[4:6], ORDER[6:9]]
    SIXTH = 6.0 ** -0.5
    D = 3
    with ExitStack() as ctx:
        def sb(name, shape, dt=F32):
            return ctx.enter_context(nc.sbuf_tensor(name, shape, dt))

        def ps(name):
            return ctx.enter_context(nc.psum_tensor(name, [P, S], F32))

        sg = Signals(nc, "experts")
        names = ("ex_const gate_step gate_exp xabs xpq xsq xcube xtanh xsilu xfeat w_load0 w_load1 w_scaled l1_ps l2_ps l2_feat gb_ps "
                 "gb_done h1_done g_done th_done silu_done silu_used abs_done pq_done sq_done cube_done feat ge_done out_step out_done "
                 "final").split()
        sg.add(**{n: 0 for n in names})
        sem = sg.sem
        FX = sb("FX", [P, NF, B * S])
        F2 = sb("F2", [P, NF, 2, S])
        W12 = [sb(f"W12_{n}", [P, 2, NF, FF]) for n in range(2)]
        W3 = [sb(f"W3_{n}", [P, 2, NF, C]) for n in range(2)]
        s12, s3 = sb("s12", [P, 2, FF]), sb("s3", [P, 2, C])
        g, gs = sb("g2", [P, 2, S]), sb("gs", [P, S])
        dist, pn, qn = ([sb(f"{n}{k}", [P, S]) for k in range(D)] for n in ("dist", "pn", "qn"))
        gates = sb("gates", [P, NE, B * QT])
        rank, tmp = ([x[:, 0:B * QT * NE].rearrange("p (n e) -> p n e", e=NE) for x in pn[0:2]])
        gmx, ge = sb("gmx", [P, B * QT]), [sb(f"ge{n}", [P, B * QT]) for n in range(2)]
        cen = sb("cen", [P, NB])
        bank = [ps(f"l1_{n}") for n in range(4)]
        out2, pg = [ps("l2_0"), ps("l2_1")], ps("pg")
        a = t.dram
        lg = t.logits[:].rearrange("p b j e -> p (b j) e")
        slot = lambda k: F2[:, k // 2, k % 2, :]
        xslot = lambda k: FX[:, k % NB, S * (k // NB):S * (k // NB) + S]
        block = ctx.enter_context(nc.Block())

        def load_expert(sp, e, par):
            pick = lambda n: a[n][bass.ds(e, 1)].rearrange("o p x -> (o p) x")
            for w in range(2):
                sp.dma_start(W12[par][:, w, 0:NB, :].rearrange("p c o -> p (c o)"), pick(f"spline{w + 1}")).then_inc(sem[f"w_load{par}"], 16)
                sp.dma_start(W12[par][:, w, NB, :], pick(f"base{w + 1}")).then_inc(sem[f"w_load{par}"], 16)
                sp.dma_start(s12[:, w, :], pick(f"scaler{w + 1}")).then_inc(sem[f"w_load{par}"], 16)
            sp.dma_start(W3[par][:, :, 0:NB, :].rearrange("p k c o -> p k (c o)"),
                         pick("spline3").rearrange("p (k x) -> p k x", k=2)).then_inc(sem[f"w_load{par}"], 16)
            sp.dma_start(W3[par][:, :, NB, :], pick("base3").rearrange("p (k x) -> p k x", k=2)).then_inc(sem[f"w_load{par}"], 16)
            sp.dma_start(s3[:], pick("scaler3").rearrange("p (k x) -> p k x", k=2)).then_inc(sem[f"w_load{par}"], 16)

        @block.sync
        def _(sp):
            sp.dma_start(cen[:], a["c_centres"]).then_inc(sem["ex_const"], 16)
            load_expert(sp, 0, 0)
            sp.wait_ge(sem["w_scaled"], ITEMS)
            load_expert(sp, 1, 1)
            with sp.Fori(0, TURNS - 1) as i:
                sp.wait_ge(sem["l2_ps"], UT * i + B)
                load_expert(sp, 2 * i + 2, 0)
                sp.wait_ge(sem["l2_ps"], UT * i + 2 * B)
                load_expert(sp, 2 * i + 3, 1)
            sp.wait_ge(sem["out_done"], NE * B)
            sp.dma_start(out_dram, t.x5[:]).then_inc(sem["final"], 16)
            sp.wait_ge(sem["final"], 16)

        @block.gpsimd
        def _(pool):
            def scale(par, k):
                c, o = k // 2, k % 2
                pool.tensor_tensor(W12[par][:, o, c, :], W12[par][:, o, c, :], s12[:, o, :], ALU.mult)
                pool.tensor_tensor(W3[par][:, o, c, :], W3[par][:, o, c, :], s3[:, o, :], ALU.mult).then_inc(sem["w_scaled"], 1)

            def x_items(b):
                for k in range(NB * b, NB * b + NB):
                    pool.wait_ge(sem["xcube"], k + 1)
                    pool.tensor_tensor(xslot(k), xslot(k), dist[k % D][:], ALU.subtract).then_inc(sem["xfeat"], 1)

            def turn(i, last):
                for m in range(UT):
                    base = ITEMS * UT * i + ITEMS * m
                    for k in range(ITEMS):
                        if m == 2:
                            if k == 0:
                                pool.wait_ge(sem["w_load1"], LOADS * i + LOADS)
                            scale(1, k)
                        if m == 6 and not last:
                            if k == 0:
                                pool.wait_ge(sem["w_load0"], LOADS * i + 2 * LOADS)
                            scale(0, k)
                        pool.wait_ge(sem["cube_done"], base + k + 1)
                        pool.tensor_tensor(slot(k), slot(k), dist[k % D][:], ALU.subtract).then_inc(sem["feat"], 1)

            x_items(0)
            pool.wait_ge(sem["w_load0"], LOADS)
            for k in range(ITEMS):
                scale(0, k)
            for b in range(1, B):
                x_items(b)
            with pool.Fori(0, TURNS - 1) as i:
                turn(i, False)
            turn(TURNS - 1, True)

        @block.tensor
        def _(pe):
            def first(par, b, group):
                o, w = group // 2, group % 2
                for f in range(NF):
                    ins = pe.matmul(bank[group][:], W12[par][:, w, f, P * o:P * o + P], FX[:, f, S * b:S * b + S],
                                    start=(f == 0), stop=(f == NF - 1))
                ins.then_inc(sem["l1_ps"], 1)

            def turn(i, last):
                for m in range(UT):
                    n = UT * i + m
                    par, b = m // B, m % B
                    for j in range(4):
                        if m + 1 < UT or not last:
                            if j == 0:
                                if m + 1 < B:
                                    pe.wait_ge(sem["xfeat"], NB * (m + 2))
                                if m + 1 == B:
                                    pe.wait_ge(sem["w_scaled"], 2 * ITEMS * i + 2 * ITEMS)
                                if m + 1 == UT:
                                    pe.wait_ge(sem["w_scaled"], 2 * ITEMS * i + 3 * ITEMS)
                            if j % 2 == 0:
                                pe.wait_ge(sem["g_done"], 2 * n + j // 2 + 1)
                            first((m + 1) // B % 2, (m + 1) % B, j)
                        for f in CHUNKS[j]:
                            if f == NB:
                                pe.wait_ge(sem["silu_done"], n + 1)
                                if m % B == 0:
                                    pe.wait_ge(sem["ge_done"], 2 * i + par + 1)
                                pe.wait_ge(sem["gb_done"], n)
                                for q in range(QT):
                                    ins = pe.matmul(pg[:, P * q:P * q + P],
                                                    ge[par][:, QT * b + q:QT * b + q + 1].to_broadcast([P, P]), t.ident[:],
                                                    start=True, stop=True)
                                ins.then_inc(sem["gb_ps"], 1)
                            else:
                                pe.wait_ge(sem["feat"], ITEMS * UT * i + ITEMS * m + 2 * f + 2)
                            for k in range(2):
                                ins = pe.matmul(out2[m % 2][:], W3[par][:, k, f, :], F2[:, f, k, :],
                                                start=(f == NB and k == 0), stop=(f == NB - 1 and k == 1))
                            if f != NB - 1:
                                ins.then_inc(sem["silu_used" if f == NB else "l2_feat"], 1)
                    ins.then_inc(sem["l2_ps"], 1)

            pe.wait_ge(sem["xfeat"], NB)
            pe.wait_ge(sem["xsilu"], B)
            pe.wait_ge(sem["w_scaled"], ITEMS)
            pe.transpose(pg[:, 0:P], t.ident[:], t.ident[:]).then_inc(sem["l2_feat"], NB - 1)
            for group in range(4):
                first(0, 0, group)
            with pe.Fori(0, TURNS - 1) as i:
                turn(i, False)
            turn(TURNS - 1, True)

        @block.scalar
        def _(act):
            def squares(k, q2, done):
                act.activation(dist[k % D][:], pn[k % D][:], ACT.Square, scale=SIXTH).then_inc(sem[done], 1)
                act.activation(q2, qn[k % D][:], ACT.Square, scale=2 * SIXTH).then_inc(sem[done], 1)

            act.wait_ge(sem["ex_const"], 16)
            for b in range(B):
                if b:
                    act.wait_ge(sem["xsilu"], b)
                act.activation(gs[:], t.z[:, b, :], ACT.Tanh, scale=0.5).then_inc(sem["xtanh"], 1)
            for k in range(XIT + 1):
                if k < XIT:
                    if k >= D:
                        act.wait_ge(sem["xfeat"], k + 1 - D)
                    act.activation(dist[k % D][:], t.z[:, k // NB, :], ACT.Abs, scale=2.5, bias=cen[:, k % NB:k % NB + 1]).then_inc(sem["xabs"], 1)
                if k:
                    act.wait_ge(sem["xpq"], 2 * k)
                    squares(k - 1, xslot(k - 1), "xsq")
            act.wait_ge(sem["gate_step"], B + 2)
            act.activation(rank[:], rank[:], ACT.Exp).then_inc(sem["gate_exp"], 1)
            act.wait_ge(sem["xfeat"], XIT)

            def head(n, base):
                for o in range(2):
                    act.wait_ge(sem["l1_ps"], 4 * n + 2 * o + 2)
                    if o == 0:
                        act.wait_ge(sem["silu_done"], n)
                        act.wait_ge(sem["abs_done"], base)
                    act.activation(g[:, o, :], bank[2 * o][:], ACT.Copy).then_inc(sem["h1_done"], 1)
                for o in range(2):
                    act.wait_ge(sem["g_done"], 2 * n + o + 1)
                    if o == 0:
                        act.wait_ge(sem["silu_used"], n)
                    act.activation(F2[:, NB, o, :], g[:, o, :], ACT.Tanh, scale=0.5).then_inc(sem["th_done"], 1)

            def turn(i, last):
                for m in range(UT):
                    n = UT * i + m
                    base = ITEMS * UT * i + ITEMS * m
                    for k in range(ITEMS + 1):
                        if k < ITEMS:
                            act.wait_ge(sem["feat"], base + max(k + 1 - D, 0))
                            act.activation(dist[k % D][:], g[:, k % 2, :], ACT.Abs, scale=2.5,
                                           bias=cen[:, k // 2:k // 2 + 1]).then_inc(sem["abs_done"], 1)
                        if k:
                            act.wait_ge(sem["pq_done"], 2 * (base + k))
                            if k % 2:
                                c = (k - 1) // 2
                                if c < NB - 1:
                                    act.wait_ge(sem["l2_feat"], (NB - 1) * n + c + 1)
                                else:
                                    act.wait_ge(sem["l2_ps"], n)
                            squares(k - 1, slot(k - 1), "sq_done")
                    act.wait_ge(sem["gb_ps"], n + 1)
                    act.wait_ge(sem["out_done"], n)
                    act.activation(gs[:], pg[:], ACT.Copy).then_inc(sem["gb_done"], 1)
                    if m + 1 < UT or not last:
                        head(n + 1, base + ITEMS)

            head(0, 0)
            with act.Fori(0, TURNS - 1) as i:
                turn(i, False)
            turn(TURNS - 1, True)

        @block.vector
        def _(dve):
            def step(ins, name="gate_step", done=[0]):
                ins.then_inc(sem[name], 1)
                done[0] += 1
                dve.wait_ge(sem[name], done[0])

            def hats(k, done):
                dve.tensor_scalar(pn[k % D][:], dist[k % D][:], 2.0, -2.0, ALU.min, ALU.add).then_inc(sem[done], 1)
                dve.tensor_scalar(qn[k % D][:], dist[k % D][:], 1.0, -1.0, ALU.min, ALU.add).then_inc(sem[done], 1)

            def cubes(k, q2, count, sq, done):
                dve.wait_ge(sem[sq], 2 * count - 1)
                dve.tensor_tensor(dist[k % D][:], dist[k % D][:], pn[k % D][:], ALU.mult)
                dve.wait_ge(sem[sq], 2 * count)
                dve.tensor_tensor(q2, q2, qn[k % D][:], ALU.mult).then_inc(sem[done], 1)

            for b in range(B):
                dve.wait_ge(sem["xtanh"], b + 1)
                step(dve.tensor_scalar(gs[:], gs[:], 0.5, 0.5, ALU.mult, ALU.add))
                dve.tensor_tensor(FX[:, NB, S * b:S * b + S], gs[:], t.z[:, b, :], ALU.mult).then_inc(sem["xsilu"], 1)
            for k in range(XIT + 1):
                if k < XIT:
                    dve.wait_ge(sem["xabs"], k + 1)
                    hats(k, "xpq")
                if k:
                    cubes(k - 1, xslot(k - 1), k, "xsq", "xcube")

            NT = B * QT
            wide = lambda x: x.rearrange("p (n o) -> p n o", o=1).to_broadcast([P, NT, NE])
            step(dve.tensor_reduce(gmx[:], lg, AX.X, ALU.max))
            step(dve.tensor_tensor(rank[:], lg, wide(gmx[:]), ALU.subtract))
            dve.wait_ge(sem["gate_exp"], 1)
            step(dve.tensor_scalar(gates[:].rearrange("p e n -> p n e"), rank[:], 1.0, None, ALU.mult))
            step(dve.memset(rank[:], 0.0))
            for j in range(NE):
                one = lg[:, :, j:j + 1]
                step(dve.tensor_tensor(tmp[:, :, 0:j + 1], one.to_broadcast([P, NT, j + 1]), lg[:, :, 0:j + 1], ALU.is_gt))
                if j + 1 < NE:
                    step(dve.tensor_tensor(tmp[:, :, j + 1:NE], one.to_broadcast([P, NT, NE - 1 - j]), lg[:, :, j + 1:NE], ALU.is_ge))
                step(dve.tensor_tensor(rank[:], rank[:], tmp[:], ALU.add))
            step(dve.tensor_scalar(rank[:], rank[:], 2.0, None, ALU.is_lt))
            gt = gates[:].rearrange("p e n -> p n e")
            step(dve.tensor_tensor(gt, gt, rank[:], ALU.mult))
            step(dve.tensor_reduce(gmx[:], gt, AX.X, ALU.add))
            step(dve.reciprocal(gmx[:], gmx[:]))
            step(dve.tensor_tensor(gt, gt, wide(gmx[:]), ALU.mult))

            def head(n):
                for o in range(2):
                    dve.wait_ge(sem["h1_done"], 2 * n + o + 1)
                    dve.tensor_tensor(g[:, o, :], g[:, o, :], bank[2 * o + 1][:], ALU.mult).then_inc(sem["g_done"], 1)

            def silu(n):
                for o in range(2):
                    x = F2[:, NB, o, :]
                    dve.wait_ge(sem["th_done"], 2 * n + o + 1)
                    dve.tensor_scalar(x, x, 0.5, 0.5, ALU.mult, ALU.add).then_inc(sem["out_step"], 1)
                for o in range(2):
                    x = F2[:, NB, o, :]
                    dve.wait_ge(sem["out_step"], 3 * n + o + 1)
                    ins = dve.tensor_tensor(x, x, g[:, o, :], ALU.mult)
                ins.then_inc(sem["silu_done"], 1)

            def turn(i, last):
                for m in range(UT):
                    n = UT * i + m
                    par, b = m // B, m % B
                    base = ITEMS * UT * i + ITEMS * m
                    if b == 0:
                        dve.tensor_scalar(ge[par][:].rearrange("p (o n) -> p o n", o=1), gates[:, bass.ds(2 * i + par, 1), :], 1.0, None,
                                          ALU.mult).then_inc(sem["ge_done"], 1)
                    for k in range(ITEMS + 1):
                        if k < ITEMS:
                            dve.wait_ge(sem["abs_done"], base + k + 1)
                            hats(k, "pq_done")
                        if k == 0:
                            silu(n)
                        if k:
                            cubes(k - 1, slot(k - 1), base + k, "sq_done", "cube_done")
                    if m + 1 < UT or not last:
                        head(n + 1)
                    dve.wait_ge(sem["gb_done"], n + 1)
                    dve.wait_ge(sem["l2_ps"], n + 1)
                    dve.tensor_tensor(gs[:], gs[:], out2[m % 2][:], ALU.mult).then_inc(sem["out_step"], 1)
                    dve.wait_ge(sem["out_step"], 3 * n + 3)
                    dve.tensor_tensor(t.x5[:, b, :], t.x5[:, b, :], gs[:], ALU.add).then_inc(sem["out_done"], 1)

            head(0)
            with dve.Fori(0, TURNS - 1) as i:
                turn(i, False)
            turn(TURNS - 1, True)


def shape_constants():
    f = np.float32
    head = np.arange(C) // DH
    nf, nt, H, W = 16, 16, 16, 32
    ln = np.log2(np.maximum(np.arange(0, H * nf, dtype=f), f(1)))
    ln[0] = -2.0
    ln = (ln.reshape(H, nf).T * np.arange(1, nf + 1, dtype=f)[:, None]).astype(f)
    freq = np.stack([np.cos(ln), np.sin(ln)], axis=1).reshape(2 * nf, H)
    k = np.arange(0, nt, dtype=f) + f(0.5)
    xs = np.arange(0, nt * W, dtype=f).reshape(W, nt).T
    theta = (k[:, None] * xs / f(W * nt) * f(6.283185307179586)).astype(f)
    time = np.stack([np.cos(theta), np.sin(theta)], axis=1).reshape(2 * nt, W)
    emb = np.concatenate([np.repeat(freq, W, axis=1), np.tile(time, (1, H))], axis=0)
    a = np.arange(P)
    outside = (np.maximum(0, WIN - a) + np.maximum(0, a + WIN - (P - 1))).astype(f)
    sel = np.zeros((BP * KH, 2, 2, 2, B), f)
    for part in range(BP):
        for m in range(KH):
            sel[KH * part + m, m // 2, m % 2, 0, :] = HSCALE
    return {
        "c_ident": np.eye(P, dtype=f),
        "c_ones": np.full((P, P), 1.0 / C, f),
        "c_hmask": (head[:, None] == np.arange(HEADS)[None, :]).astype(f),
        "c_eps": np.full((P, 1), EPS, f),
        "c_group": ((a[:, None] // 4) == (a[None, :] // 4)).astype(f) / f(4),
        "c_emb": emb.astype(f),
        "c_onerow": np.ones((1, P), f),
        "c_band": np.where(np.abs(a[:, None] - a[None, :]) <= WIN, 0.0, BIG).astype(f),
        "c_pads": np.stack([np.where(outside > 0, 0.0, BIG).astype(f), outside], axis=1),
        "c_centres": np.tile((3.5 - np.arange(NB, dtype=f))[None, :], (P, 1)),
        "c_sel": sel.reshape(BP * KH, 32),
    }


def conv_attn_hybrid(nc, dram, out_dram):
    t = Stage()
    t.dram = dram
    with ExitStack() as ctx:
        def sb(name, shape):
            return ctx.enter_context(nc.sbuf_tensor(name, shape, F32))

        t.ident, t.ones, t.hmask, t.eps = sb("ident", [P, P]), sb("ones", [P, P]), sb("hmask", [P, HEADS]), sb("eps", [P, 1])
        stream = sb("stream", [P, B, S])
        t.x2 = t.x3 = t.x4 = t.x5 = stream
        t.z, t.logits = sb("z_all", [P, B, S]), sb("logits_all", [P, B, QT, NE])
        for stage in (global_attention, batch_attention, flow, window_attention):
            with nc.cleanup_on_exit():
                stage(nc, t)
        experts(nc, t, out_dram)


class Stage:
    pass


def laid_out(x):
    a = {n: v for n, v in x.items() if n == "x" or n.startswith(("L0_", "L1_", "L3_attn"))}
    for n in ("in_proj_bias", "out_bias"):
        a["L2_attn_" + n] = x["L2_attn_" + n]
    a["bw_in"], a["bw_out"] = x["L2_attn_in_proj_weight"].T, x["L2_attn_out_weight"].T
    for n in ("W3", "b2", "b3"):
        a["L2_ffn_" + n] = x["L2_ffn_" + n]
    rows = lambda w, n: w.T.reshape(n, P, -1).transpose(1, 0, 2)
    a["ff_w1"], a["ff_w2"], a["ff_w3"] = x["L2_ffn_W1"].T, rows(x["L2_ffn_W2"], KH), rows(x["L2_ffn_W3"], KH)
    a["ff_b1"] = x["L2_ffn_b1"].reshape(KH, P).T
    a["gate_t"] = x["L3_ffn_gate_w"].T
    for n in (1, 2):
        a[f"spline{n}"] = x[f"L3_ffn_spline_w{n}"].transpose(0, 2, 3, 1).reshape(NE, P, -1)
        a[f"base{n}"] = x[f"L3_ffn_base_w{n}"].transpose(0, 2, 1)
        a[f"scaler{n}"] = x[f"L3_ffn_scaler_w{n}"].transpose(0, 2, 1)
    for n in ("spline", "base", "scaler"):
        w = x[f"L3_ffn_{n}_w3"].reshape(NE, C, 2, P, -1)
        a[n + "3"] = w.transpose(0, 3, 2, 4, 1).reshape(NE, P, -1)
    return a


def kernel(**inputs):
    import concourse.bacc as _bacc
    from concourse.bass_utils import run_bass_kernel_spmd as _run

    nc = _bacc.Bacc("TRN2", target_bir_lowering=False, num_devices=1)
    arrays, dram = {}, {}
    for name, v in {**laid_out({n: np.asarray(v) for n, v in inputs.items()}), **shape_constants()}.items():
        v = np.ascontiguousarray(v)
        arrays["in_" + name] = v
        dram[name] = nc.dram_tensor("in_" + name, v.shape, mybir.dt.from_np(v.dtype), kind="ExternalInput").ap()
    out = nc.dram_tensor("out_x", (B, C, S), F32, kind="ExternalOutput").ap()
    conv_attn_hybrid(nc, dram, out.rearrange("b c s -> c b s"))
    r = _run(nc, [arrays], core_ids=[0])
    return r.results[0]["out_x"].reshape(B, C, 16, 32)
```

```python
from contextlib import ExitStack

import numpy as np

import concourse.bass as bass
from concourse import mybir

F32 = mybir.dt.float32
BF16 = mybir.dt.bfloat16
F16 = mybir.dt.float16
ALU = mybir.AluOpType
ACT = mybir.ActivationFunctionType
AX = mybir.AxisListType

B = 4
C = 128
S = 512
P = 128
QT = S // P
HEADS = 8
DH = C // HEADS
VW = P + DH
HID = 512
KH = HID // P
NE = 8
FF = 256
NB = 8
NF = NB + 1
DIL = 4
WIN = 32
EMB = 64
STEPS = S - 1
DT = 1.0 / STEPS
HSCALE = 4096.0
NP = 2
BP = 3
WMAX = 2.0 ** 14
WLOW = 4.0
UN = 7
EPS = 1e-5
BIG = -1.0e30


class Signals:

    def __init__(self, nc, stage):
        self.nc, self.stage, self.sem, self.per, self.n = nc, stage, {}, {}, {}

    def add(self, **per):
        for name, k in per.items():
            self.sem[name] = self.nc.alloc_semaphore(name=f"{self.stage}_{name}")
            self.per[name], self.n[name] = k, 0

    def up(self, ins, name, by=1):
        ins.then_inc(self.sem[name], by)
        self.n[name] += by

    def seq(self, eng, ins, name, i=None):
        self.up(ins, name)
        self.wait(eng, name, self.n[name], i)

    def wait(self, eng, name, n, i=None):
        if i is None:
            if n > 0:
                eng.wait_ge(self.sem[name], n)
        elif self.per[name]:
            eng.wait_ge(self.sem[name], i * self.per[name] + n)

    def check(self, *names):
        for name in names:
            assert self.n[name] == self.per[name], (name, self.n[name], self.per[name])


def layer_norm_pe(pe, sg, ones, src, sq, mean_ps, var_ps, k, i, src_sig, src_n):
    sg.wait(pe, src_sig, src_n, i)
    sg.up(pe.matmul(mean_ps, ones, src, start=True, stop=True), "ln_mean")
    sg.wait(pe, "ln_sq", k, i)
    sg.up(pe.matmul(var_ps, ones, sq, start=True, stop=True), "ln_var")


def layer_norm_act(act, sg, xc, sq, sd, var_ps, eps, k, i):
    sg.wait(act, "ln_cent", k, i)
    sg.up(act.activation(sq, xc, ACT.Square), "ln_sq")
    sg.wait(act, "ln_var", k, i)
    sg.up(act.activation(sd, var_ps, ACT.Sqrt, bias=eps), "ln_sd")


def layer_norm_dve(dve, sg, src, xc, sd, mean_ps, dst, k, i, gamma=None, beta=None):
    sg.wait(dve, "ln_mean", k, i)
    sg.seq(dve, dve.tensor_tensor(xc, src, mean_ps, ALU.subtract), "ln_cent", i)
    sg.wait(dve, "ln_sd", k, i)
    sg.seq(dve, dve.reciprocal(sd, sd), "dve_step", i)
    if gamma is None:
        sg.seq(dve, dve.tensor_tensor(dst, xc, sd, ALU.mult), "ln_out", i)
    else:
        sg.seq(dve, dve.tensor_tensor(xc, xc, sd, ALU.mult), "dve_step", i)
        sg.seq(dve, dve.tensor_scalar(dst, xc, gamma, beta, ALU.mult, ALU.add), "ln_out", i)


def global_attention(nc, t):
    UNITS = HEADS * QT
    with ExitStack() as ctx:
        def sb(name, shape, dt=F32):
            return ctx.enter_context(nc.sbuf_tensor(name, shape, dt))

        def ps(name):
            return ctx.enter_context(nc.psum_tensor(name, [P, S], F32))

        sg = Signals(nc, "global")
        sg.add(ga_loads=0, ga_loads_sp=0, x_load=16, gn_mm=2, dve_step=11, dve_gn=3, act_gn=1, gx=1, ln_mean=3, ln_var=3, ln_sq=3,
               ln_sd=3, ln_cent=3, ln_out=3, vones=0, x1_done=1, x2_done=1, ga_z=1)
        for l in (0, 1):
            sg.add(**{f"q_ps{l}": 1, f"k_ps{l}": 1, f"v_ps{l}": 1, f"q_done{l}": 1, f"k_done{l}": 1, f"v_done{l}": 1,
                      f"qm{l}": HEADS, f"score{l}": UNITS, f"nmax{l}": UNITS, f"prob{l}": UNITS, f"recip{l}": UNITS,
                      f"pnorm{l}": UNITS, f"ptrans{l}": UNITS, f"ptcopy{l}": UNITS, f"pv{l}": HEADS,
                      f"o_done{l}": 1, f"out_ps{l}": 1})
        xb, gx, xn, xc, sq, sd, on, x1, x2 = (sb(n, [P, S]) for n in ("xb", "gx", "xn", "xc", "sq", "sd", "on", "x1", "x2b"))
        qT, kT, oT = sb("qT", [P, S]), sb("kT", [P, S]), sb("oT", [P, S])
        qm = [sb(f"qm{n}", [P, S]) for n in range(2)]
        V = sb("V", [P, QT, HEADS * VW])
        Pb = [sb(f"Pb{n}", [P, S]) for n in range(3)]
        PT = [sb(f"PT{n}", [P, QT, S]) for n in range(2)]
        nm, rs, rr = sb("nm", [P, 4]), sb("rs", [P, 4]), sb("rr", [P, 4])
        st6, mv, gms, dev, gvar = sb("st6", [P, 6]), sb("mv", [P, 2]), sb("gms", [P, 2]), sb("dev", [P, 1]), sb("gvar", [P, 1])
        w0, wo0, g4 = sb("w0", [P, 3 * C]), sb("wo0", [P, C]), sb("g4", [P, P])
        cols = sb("cols0", [P, 8])
        bvrow, onerow = sb("bvrow", [1, C]), sb("onerow", [1, P])
        w1 = {n: sb(n, [P, C]) for n in ("w1q", "w1k", "w1v", "w1o")}
        w1qe, w1ke, emb = sb("w1qe", [EMB, C]), sb("w1ke", [EMB, C]), sb("emb_s", [EMB, S])
        pT, pM, pO = [ps("pT0"), ps("pT1")], [ps(f"pM{n}") for n in range(3)], ps("pO")
        pS = [ps("pS0"), ps("pS1"), pM[0], pM[1]]
        AHEAD = len(pS) - 1
        a = t.dram
        col = lambda ap: ap.rearrange("(p o) -> p o", o=1)
        loads = [(t.ident[:], a["c_ident"]), (t.ones[:], a["c_ones"]), (t.hmask[:], a["c_hmask"]), (t.eps[:], a["c_eps"]),
                 (g4[:], a["c_group"]), (emb[:], a["c_emb"]), (onerow[:], a["c_onerow"]),
                 (w0[:], a["L0_conv_w_qkv"]), (wo0[:], a["L0_conv_w_out"]),
                 (cols[:, 0:1], col(a["L0_conv_b_qkv"][0:C])), (cols[:, 1:2], col(a["L0_conv_b_qkv"][C:2 * C])),
                 (bvrow[:], a["L0_conv_b_qkv"][2 * C:3 * C].rearrange("(o n) -> o n", o=1)),
                 (cols[:, 2:3], col(a["L0_conv_b_out"])), (cols[:, 3:4], col(a["L0_conv_gamma1"])),
                 (cols[:, 4:5], col(a["L0_conv_beta1"])), (cols[:, 5:6], col(a["L0_conv_gamma2"])),
                 (cols[:, 6:7], col(a["L0_conv_beta2"])), (cols[:, 7:8], col(a["L1_conv_bout"])),
                 (w1["w1q"][:], a["L1_conv_Wq"][0:C]), (w1["w1k"][:], a["L1_conv_Wk"][0:C]),
                 (w1qe[:], a["L1_conv_Wq"][C:C + EMB]), (w1ke[:], a["L1_conv_Wk"][C:C + EMB]),
                 (w1["w1v"][:], a["L1_conv_Wv"]), (w1["w1o"][:], a["L1_conv_Wout"])]
        LOADED = 16 * len(loads) // 2
        x_dram = a["x"].rearrange("b c h w -> b c (h w)")
        diag = lambda: V[:].rearrange("p t (h x) -> p t h x", x=VW)[:, :, :, 0:DH]
        block = ctx.enter_context(nc.Block())

        @block.sync
        def _(sp):
            for dst, src in loads[0::2]:
                sg.up(sp.dma_start(dst, src), "ga_loads_sp", 16)
            with sp.Fori(0, B) as i:
                sg.wait(sp, "x1_done", 0, i)
                sg.up(sp.dma_start(xb[:], x_dram[bass.ds(i, 1)].rearrange("o c s -> (o c) s")), "x_load", 16)

        @block.gpsimd
        def _(pool):
            for dst, src in loads[1::2]:
                sg.up(pool.dma_start(dst, src), "ga_loads", 16)
            sg.up(pool.memset(V[:], 0.0), "vones")

        def attention_pe(pe, l, i):
            src, sig, n = (xn, "ln_out", 1) if l == 0 else (x1, "x1_done", 1)
            wq, wk, wv = (w0[:, 0:C], w0[:, C:2 * C], w0[:, 2 * C:]) if l == 0 else (w1["w1q"][:], w1["w1k"][:], w1["w1v"][:])
            sg.wait(pe, sig, n, i)
            for dst, w, e, name in ((pM[0], wq, w1qe, "q_ps"), (pM[1], wk, w1ke, "k_ps")):
                if l == 1:
                    pe.matmul(dst[:], e[:], emb[:], start=True, stop=False)
                sg.up(pe.matmul(dst[:], w, src[:], start=(l == 0), stop=True), f"{name}{l}")
            for j in range(QT):
                o = pM[2][:, j * C:(j + 1) * C]
                ins = pe.matmul(o, src[:, j * P:(j + 1) * P], wv, start=True, stop=(l == 1))
                if l == 0:
                    ins = pe.matmul(o, onerow[:], bvrow[:], start=False, stop=True)
            sg.up(ins, f"v_ps{l}")

            def score(u):
                if u == 0:
                    sg.wait(pe, f"k_done{l}", 1, i)
                h, j = u // QT, u % QT
                sg.wait(pe, f"qm{l}", h + 1, i)
                if u >= len(pS):
                    sg.wait(pe, f"prob{l}", u + 1 - len(pS), i)
                sg.up(pe.matmul(pS[u % len(pS)][:], qm[h % 2][:, j * P:(j + 1) * P], kT[:], start=True, stop=True), f"score{l}")

            def turn(u):
                sg.wait(pe, f"pnorm{l}", u + 1, i)
                if u >= 2:
                    sg.wait(pe, f"ptcopy{l}", u - 1, i)
                for k in range(QT):
                    ins = pe.transpose(pT[u % 2][:, k * P:(k + 1) * P], Pb[u % 3][:, k * P:(k + 1) * P], t.ident[:])
                sg.up(ins, f"ptrans{l}")

            def weigh(h):
                sg.wait(pe, f"ptcopy{l}", QT * (h + 1), i)
                if h == 0:
                    sg.wait(pe, f"v_done{l}", 1, i)
                for k in range(QT):
                    ins = pe.matmul(pO[:], V[:, k, h * P:(h + 1) * P], PT[h % 2][:, k, :],
                                    start=(h == 0 and k == 0), stop=(h == HEADS - 1 and k == QT - 1))
                sg.up(ins, f"pv{l}")

            for u in range(AHEAD):
                score(u)
            for u in range(UNITS):
                turn(u)
                if u + AHEAD < UNITS:
                    score(u + AHEAD)
                if u % QT == 2 and u > QT:
                    weigh(u // QT - 1)
            weigh(HEADS - 1)

        def attention_act(act, l, i):
            sg.wait(act, f"q_ps{l}", 1, i)
            if l == 0:
                sg.up(act.activation(qT[:], pM[0][:], ACT.Identity, bias=cols[:, 0:1]), "q_done0")
            else:
                sg.up(act.activation(qT[:], pM[0][:], ACT.Copy), "q_done1")

            def prob(u):
                sg.wait(act, f"nmax{l}", u + 1, i)
                if u >= 3:
                    sg.wait(act, f"ptrans{l}", u - 2, i)
                sg.up(act.activation(Pb[u % 3][:], pS[u % len(pS)][:], ACT.Exp, bias=nm[:, u % 4:u % 4 + 1],
                                     accum_out=rs[:, u % 4:u % 4 + 1]), f"prob{l}")

            def copy(u):
                h, j = u // QT, u % QT
                sg.wait(act, f"ptrans{l}", u + 1, i)
                if h >= 2:
                    sg.wait(act, f"pv{l}", h - 1, i)
                sg.up(act.activation(PT[h % 2][:, :, j * P:(j + 1) * P],
                                     pT[u % 2][:].rearrange("p (k q) -> p k q", k=QT), ACT.Copy), f"ptcopy{l}")

            for u in range(UNITS):
                prob(u)
                if u >= 2:
                    copy(u - 2)
            copy(UNITS - 2)
            copy(UNITS - 1)

        def attention_dve(dve, l, i):
            sg.wait(dve, f"k_ps{l}", 1, i)
            if l == 0:
                sg.seq(dve, dve.tensor_scalar(kT[:], pM[1][:], cols[:, 1:2], None, ALU.add), "k_done0", i)
            else:
                sg.seq(dve, dve.tensor_copy(kT[:], pM[1][:]), "k_done1", i)
            sg.wait(dve, f"v_ps{l}", 1, i)
            sg.seq(dve, dve.tensor_copy(diag(), pM[2][:].rearrange("p (t h d) -> p t h d", t=QT, h=HEADS)), f"v_done{l}", i)
            sg.wait(dve, f"q_done{l}", 1, i)

            def mask_q(h):
                sg.seq(dve, dve.tensor_scalar(qm[h % 2][:], qT[:], t.hmask[:, h:h + 1], DH ** -0.5, ALU.mult, ALU.mult),
                       f"qm{l}", i)

            def norm(u):
                k = u % 4
                sg.wait(dve, f"prob{l}", u + 1, i)
                sg.seq(dve, dve.reciprocal(rr[:, k:k + 1], rs[:, k:k + 1]), f"recip{l}", i)
                sg.seq(dve, dve.tensor_scalar(Pb[u % 3][:], Pb[u % 3][:], rr[:, k:k + 1], None, ALU.mult), f"pnorm{l}", i)

            mask_q(0)
            mask_q(1)
            for u in range(UNITS):
                sg.wait(dve, f"score{l}", u + 1, i)
                sg.seq(dve, dve.tensor_reduce(nm[:, u % 4:u % 4 + 1], pS[u % len(pS)][:], AX.X, ALU.max, negate=True), f"nmax{l}", i)
                if u:
                    norm(u - 1)
                if u % QT == QT - 1 and u // QT + 2 < HEADS:
                    mask_q(u // QT + 2)
            norm(UNITS - 1)
            sg.wait(dve, f"pv{l}", HEADS, i)
            sg.seq(dve, dve.tensor_copy(oT[:], pO[:]), f"o_done{l}", i)

        @block.tensor
        def _(pe):
            sg.wait(pe, "ga_loads", LOADED)
            sg.wait(pe, "ga_loads_sp", LOADED)
            with pe.Fori(0, B) as i:
                sg.wait(pe, "dve_gn", 1, i)
                sg.up(pe.matmul(pM[0][:, 0:2], g4[:], mv[:], start=True, stop=True), "gn_mm")
                sg.wait(pe, "dve_gn", 3, i)
                sg.up(pe.matmul(pM[1][:, 0:1], g4[:], dev[:], start=True, stop=True), "gn_mm")
                layer_norm_pe(pe, sg, t.ones[:], gx[:], sq[:], pM[0][:], pM[1][:], 1, i, "gx", 1)
                attention_pe(pe, 0, i)
                layer_norm_pe(pe, sg, t.ones[:], oT[:], sq[:], pM[0][:], pM[1][:], 2, i, "o_done0", 1)
                sg.wait(pe, "ln_out", 2, i)
                sg.up(pe.matmul(pM[2][:], wo0[:], on[:], start=True, stop=True), "out_ps0")
                attention_pe(pe, 1, i)
                sg.wait(pe, "o_done1", 1, i)
                sg.up(pe.matmul(pM[2][:], w1["w1o"][:], oT[:], start=True, stop=True), "out_ps1")
                layer_norm_pe(pe, sg, t.ones[:], x2[:], sq[:], pM[0][:], pM[1][:], 3, i, "x2_done", 1)

        @block.scalar
        def _(act):
            sg.wait(act, "ga_loads", LOADED)
            sg.wait(act, "ga_loads_sp", LOADED)
            with act.Fori(0, B) as i:
                sg.wait(act, "dve_gn", 3, i)
                sg.wait(act, "gn_mm", 2, i)
                sg.up(act.activation(gvar[:], pM[1][:, 0:1], ACT.Sqrt, bias=gms[:, 1:2]), "act_gn")
                layer_norm_act(act, sg, xc[:], sq[:], sd[:], pM[1][:], t.eps[:], 1, i)
                attention_act(act, 0, i)
                layer_norm_act(act, sg, xc[:], sq[:], sd[:], pM[1][:], t.eps[:], 2, i)
                attention_act(act, 1, i)
                layer_norm_act(act, sg, xc[:], sq[:], sd[:], pM[1][:], t.eps[:], 3, i)

        @block.vector
        def _(dve):
            sg.wait(dve, "ga_loads", LOADED)
            sg.wait(dve, "ga_loads_sp", LOADED)
            sg.wait(dve, "vones", 1)
            with dve.Fori(0, B) as i:
                sg.wait(dve, "x_load", 16, i)
                sg.seq(dve, dve.bn_stats(st6[:], xb[:]), "dve_step", i)
                dve.memset(rr[:, 0:1], 0.0)
                sg.seq(dve, dve.bn_aggr(mv[:], st6[:]), "dve_gn", i)
                sg.wait(dve, "gn_mm", 1, i)
                sg.seq(dve, dve.tensor_scalar(gms[:], pM[0][:, 0:2], EPS, None, ALU.add), "dve_step", i)
                sg.seq(dve, dve.tensor_copy(gms[:, 0:1], pM[0][:, 0:1]), "dve_gn", i)
                sg.seq(dve, dve.tensor_tensor(dev[:], mv[:, 0:1], gms[:, 0:1], ALU.subtract), "dve_step", i)
                sg.seq(dve, dve.tensor_tensor(dev[:], dev[:], dev[:], ALU.mult), "dve_gn", i)
                sg.wait(dve, "act_gn", 1, i)
                sg.seq(dve, dve.reciprocal(gvar[:], gvar[:]), "dve_step", i)
                sg.seq(dve, dve.tensor_scalar(gx[:], xb[:], gms[:, 0:1], gvar[:, 0:1], ALU.subtract, ALU.mult), "gx", i)
                layer_norm_dve(dve, sg, gx[:], xc[:], sd[:], pM[0][:], xn[:], 1, i, cols[:, 3:4], cols[:, 4:5])
                attention_dve(dve, 0, i)
                layer_norm_dve(dve, sg, oT[:], xc[:], sd[:], pM[0][:], on[:], 2, i, cols[:, 5:6], cols[:, 6:7])
                sg.wait(dve, "out_ps0", 1, i)
                sg.seq(dve, dve.scalar_tensor_tensor(out=x1[:], in0=pM[2][:], scalar=cols[:, 2:3], in1=xn[:],
                                                     op0=ALU.add, op1=ALU.add), "dve_step", i)
                sg.seq(dve, dve.tensor_tensor(x1[:], x1[:], xb[:], ALU.add), "x1_done", i)
                attention_dve(dve, 1, i)
                sg.wait(dve, "out_ps1", 1, i)
                sg.seq(dve, dve.scalar_tensor_tensor(out=x2[:], in0=pM[2][:], scalar=cols[:, 7:8], in1=x1[:],
                                                     op0=ALU.add, op1=ALU.add), "x2_done", i)
                layer_norm_dve(dve, sg, x2[:], xc[:], sd[:], pM[0][:], on[:], 3, i)
                one = lambda ap: ap.rearrange("p (o s) -> p o s", o=1)
                sg.seq(dve, dve.tensor_scalar(t.x2[:, bass.ds(i, 1), :], one(x2[:]), 0.0, None, ALU.add), "dve_step", i)
                sg.seq(dve, dve.tensor_scalar(t.z[:, bass.ds(i, 1), :], one(on[:]), 0.0, None, ALU.add), "ga_z", i)

        for name in sg.per:
            if sg.per[name]:
                sg.check(name)
def batch_attention(nc, t):
    with ExitStack() as ctx:
        def sb(name, shape, dt=F32):
            return ctx.enter_context(nc.sbuf_tensor(name, shape, dt))

        def ps(name):
            return ctx.enter_context(nc.psum_tensor(name, [P, S], F32))

        sg = Signals(nc, "batch")
        sg.add(ba_loads=0, zs_done=1, qkv_ps=B, qkv_done=B, ba_step=4 * B + 6, ba_shift=1, ba_exp=1, attn_done=B, ot_ps=1,
               ot_done=1, proj_ps=1, x3_done=1)
        w, wo = sb("ba_w_in", [P, 3 * C]), sb("ba_w_o", [P, C])
        brow, one, bo = sb("b_in", [1, 3 * C]), sb("one_r", [1, P]), sb("b_o", [P, 1])
        zs = sb("zs", [P, B, P])
        qkv = sb("qkv", [P, B, 3 * C])
        prod = sb("prod", [P, B * C])
        sc = sb("sc", [P, B, B, HEADS])
        mx, rs = sb("mx", [P, B, HEADS]), sb("rsum", [P, B, HEADS])
        o, oT = sb("o_t", [P, B, C]), sb("o_c", [P, B, P])
        pq = [ps(f"pq{n}") for n in range(2)]
        pt, pp = ps("pt"), ps("pp")
        a = t.dram
        loads = [(w[:], a["bw_in"]), (wo[:], a["bw_out"]), (brow[:], a["L2_attn_in_proj_bias"].rearrange("(o n) -> o n", o=1)),
                 (one[:], a["c_onerow"]), (bo[:], a["L2_attn_out_bias"].rearrange("(p o) -> p o", o=1))]
        block = ctx.enter_context(nc.Block())

        @block.sync
        def _(sp):
            for dst, src in loads:
                sg.up(sp.dma_start(dst, src), "ba_loads", 16)

        @block.tensor
        def _(pe):
            sg.wait(pe, "ba_loads", 16 * len(loads))
            with pe.Fori(0, QT) as i:
                sg.wait(pe, "zs_done", 1, i)
                for b in range(B):
                    if b >= 2:
                        sg.wait(pe, "qkv_done", b - 1, i)
                    pe.matmul(pq[b % 2][:, 0:3 * C], zs[:, b, :], w[:], start=True, stop=False)
                    sg.up(pe.matmul(pq[b % 2][:, 0:3 * C], one[:], brow[:], start=False, stop=True), "qkv_ps")
                for b in range(B):
                    sg.wait(pe, "attn_done", b + 1, i)
                    ins = pe.transpose(pt[:, b * P:(b + 1) * P], o[:, b, :], t.ident[:])
                sg.up(ins, "ot_ps")
                sg.wait(pe, "ot_done", 1, i)
                sg.up(pe.matmul(pp[:], wo[:], oT[:].rearrange("p b n -> p (b n)"), start=True, stop=True), "proj_ps")

        @block.scalar
        def _(act):
            with act.Fori(0, QT) as i:
                for b in range(B):
                    sg.wait(act, "qkv_ps", b + 1, i)
                    sg.up(act.activation(qkv[:, b, :], pq[b % 2][:, 0:3 * C], ACT.Copy), "qkv_done")
                sg.wait(act, "ba_shift", 1, i)
                sg.up(act.activation(sc[:], sc[:], ACT.Exp, scale=DH ** -0.5), "ba_exp")
                sg.wait(act, "ot_ps", 1, i)
                sg.up(act.activation(oT[:].rearrange("p b n -> p (b n)"), pt[:], ACT.Copy), "ot_done")

        @block.vector
        def _(dve):
            with dve.Fori(0, QT) as i:
                tile = lambda x: x[:, :, bass.ds(i * P, P)]
                sg.seq(dve, dve.tensor_scalar(zs[:], tile(t.z), 0.0, None, ALU.add), "zs_done", i)
                sg.wait(dve, "qkv_done", B, i)
                keys, values = qkv[:, :, C:2 * C], qkv[:, :, 2 * C:3 * C]
                cube = prod[:].rearrange("p (b c) -> p b c", b=B)
                for b in range(B):
                    query = qkv[:, b:b + 1, 0:C].to_broadcast([P, B, C])
                    sg.seq(dve, dve.tensor_tensor(cube, query, keys, ALU.mult), "ba_step", i)
                    sg.seq(dve, dve.tensor_reduce(sc[:, b].rearrange("p k h -> p (k h)"),
                                                  prod[:].rearrange("p (g d) -> p g d", d=DH), AX.X, ALU.add), "ba_step", i)
                bykey = sc[:].rearrange("p b k h -> p b h k")
                sg.seq(dve, dve.tensor_reduce(mx[:], bykey, AX.X, ALU.max), "ba_step", i)
                for b in range(B):
                    ins = dve.tensor_tensor(sc[:, b], sc[:, b], mx[:, b:b + 1, :].to_broadcast([P, B, HEADS]), ALU.subtract)
                    if b < B - 1:
                        sg.seq(dve, ins, "ba_step", i)
                sg.seq(dve, ins, "ba_shift", i)
                sg.wait(dve, "ba_exp", 1, i)
                sg.seq(dve, dve.tensor_reduce(rs[:], bykey, AX.X, ALU.add), "ba_step", i)
                sg.seq(dve, dve.reciprocal(rs[:], rs[:]), "ba_step", i)
                for b in range(B):
                    sg.seq(dve, dve.tensor_tensor(prod[:].rearrange("p (k h d) -> p k h d", k=B, h=HEADS),
                                                  values.rearrange("p k (h d) -> p k h d", d=DH),
                                                  sc[:, b].rearrange("p k (h o) -> p k h o", o=1).to_broadcast([P, B, HEADS, DH]),
                                                  ALU.mult), "ba_step", i)
                    sg.seq(dve, dve.tensor_reduce(o[:, b, :], prod[:].rearrange("p (k c) -> p c k", k=B), AX.X, ALU.add), "ba_step", i)
                    ob = o[:, b, :].rearrange("p (h d) -> p h d", d=DH)
                    sg.seq(dve, dve.tensor_tensor(ob, ob, rs[:, b, :].rearrange("p (h o) -> p h o", o=1).to_broadcast([P, HEADS, DH]),
                                                  ALU.mult), "attn_done", i)
                sg.wait(dve, "proj_ps", 1, i)
                sg.seq(dve, dve.scalar_tensor_tensor(out=tile(t.x3), in0=pp[:].rearrange("p (b n) -> p b n", b=B), scalar=bo[:, 0:1],
                                                     in1=tile(t.x2), op0=ALU.add, op1=ALU.add), "x3_done", i)

        for name in sg.per:
            if sg.per[name]:
                sg.check(name)


def flow(nc, t):
    NV = KH * B
    GROUPS = [(0, 1), (2,), (3,)]
    G = len(GROUPS)
    BLOCKS2 = [(0, 0), (1, 0), (2, 0), (1, 1), (0, 1), (2, 1), (1, 2), (0, 2), (2, 2)]
    BLOCKS13 = [(0, 0), (0, 1), (1, 0), (2, 0), (2, 1), (1, 1), (1, 2), (2, 2), (0, 2)]
    with ExitStack() as ctx:
        def sb(name, shape, dt=F32):
            return ctx.enter_context(nc.sbuf_tensor(name, shape, dt))

        def ps(name):
            return ctx.enter_context(nc.psum_tensor(name, [P, S], F32))

        sg = Signals(nc, "flow")
        sg.add(fl_loads=0, sel16=0, y_mm=0, y_step=0, y_act=0, w13_ps=0, w13_done=0, v_ps=0, prep=0, part=0, rest=0, b2_moved=0,
               ones_set=0, wm_ps=0, scales=0, large_set=0, k_ps=0, slope=0, states=0)
        step = dict(u1=4 * G, h1=4 * G, hi1=4 * G, in1=4 * G, l2_ps=4 * G, u2=4 * G, h2=4 * G, hi2=4 * G, in2=4 * G,
                    l13_ps=4 * G, g13=4 * G, gsum=3, acc=1, v_shifted=2, hsum=3, hist=1)
        sg.add(**{name: UN * k for name, k in step.items()})

        def wait(eng, name, n, w, i):
            sg.wait(eng, name, w * step[name] + n, i)

        w1, w3n, w2f, w13f, w3 = sb("w1", [P, HID]), sb("w3n", [P, HID]), sb("w2f", [P, KH, HID]), sb("w13f", [P, KH, HID]), sb("w3", [P, KH, C])
        W2, W13 = sb("W2", [P, NP, KH, HID], F16), sb("W13", [P, NP, KH, HID], F16)
        b1, b2r, b2s, B2, b3 = sb("b1", [P, KH]), sb("b2r", [KH, P]), sb("b2s", [KH, BP, P], BF16), sb("B2", [BP * KH, P], BF16), sb("b3", [P, 1])
        sel_f, sel = sb("sel_f", [BP * KH, 32]), sb("sel", [BP * KH, 32], BF16)
        yc, ysq, ysd, y0, b3dt = sb("yc", [P, B]), sb("ysq", [P, B]), sb("ysd", [P, B]), sb("y0", [P, B]), sb("b3dt", [P, 1])
        half_b, full_b = sb("half_b", [P, NV]), sb("full_b", [P, NV])
        v_half, v_full, acc = sb("v_half", [P, NV]), sb("v_full", [P, NV]), sb("acc", [P, NV])
        u1, u2, g = sb("u1", [P, NV]), sb("u2", [P, NV]), sb("g", [P, 4, NV])
        g12, g012, gall = sb("g12", [P, NV]), sb("g012", [P, NV]), sb("gall", [P, NV])
        wmax, wpow, winv, wdiag = sb("wmax", [P, 2]), sb("wpow", [2, 1]), sb("winv", [2, 1]), sb("wdiag", [2, 4])
        wscale, unscale2, coefs = sb("wscale", [P, 2]), sb("unscale2", [P, 1]), sb("coefs", [P, 3])
        wtop, large = sb("wtop", [P, 1]), sb("large", [P, 1], mybir.dt.int32)
        COEFS = [c * WLOW / WMAX / HSCALE for c in (DT / 2, DT, DT / 6)]
        h1, h2 = sb("h1", [P, NV]), sb("h2", [P, 4, NV])
        H1, H2 = sb("H1", [P, KH, 2, B], F16), sb("H2", [P, KH, 2, B], F16)
        inner, outer, both = sb("inner", [P, NV]), sb("outer", [P, NV]), sb("both", [P, NV])
        hist = sb("hist_h", [P, KH, S, B])
        slope, Y, ones1 = sb("slope_d", [P, S, B]), sb("Y", [P, B, S]), sb("ones1", [P, S])
        p2, p1, py, pv = [ps(f"p2_{n}") for n in range(G)], [ps(f"p1_{n}") for n in range(G)], ps("py"), ps("pv_ps")
        pw = p1[0:2]
        cols = lambda x, q: x[:, B * GROUPS[q][0]:B * GROUPS[q][-1] + B]
        mb = lambda x: x.rearrange("p (m b) -> p m b", b=B)
        parts = lambda x, q: x[:, 0:2 * B * len(GROUPS[q])].rearrange("p (m q b) -> p m b q", q=2, b=B)
        splits = [(b2r[:], lambda q: b2s[:, q, :]), (w2f[:], lambda q: W2[:, q]), (w13f[:], lambda q: W13[:, q])]
        a = t.dram
        loads = [(w1[:], a["ff_w1"]), (w3n[:], a["L2_ffn_W3"]), (w2f[:], a["ff_w2"]), (w3[:], a["ff_w3"]), (b1[:], a["ff_b1"]),
                 (b2r[:], a["L2_ffn_b2"].rearrange("(m p) -> m p", p=P)), (b3[:], a["L2_ffn_b3"].rearrange("(p o) -> p o", o=1)),
                 (sel_f[:], a["c_sel"])]
        block = ctx.enter_context(nc.Block())

        @block.sync
        def _(sp):
            for dst, src in loads:
                sg.up(sp.dma_start(dst, src), "fl_loads", 16)
            sg.wait(sp, "part", 7)
            for q in range(BP):
                sg.up(sp.dma_start(B2[KH * q:KH * q + KH, :], b2s[:, q, :]), "b2_moved", 16)

        @block.gpsimd
        def _(pool):
            sg.up(pool.memset(ones1[:], 1.0), "ones_set")
            sg.up(pool.memset(hist[:, :, STEPS:S, :], 0.0), "ones_set")
            sg.wait(pool, "prep", 6)
            sg.up(pool.tensor_tensor(v_half[:], u1[:], half_b[:], ALU.add), "v_shifted")
            sg.up(pool.tensor_tensor(v_full[:], u1[:], full_b[:], ALU.add), "v_shifted")
            sg.n["v_shifted"] = 0
            with pool.Fori(0, STEPS // UN) as i:
                for w in range(UN):
                    wait(pool, "h2", 3 * G, w, i)
                    sg.seq(pool, pool.tensor_tensor(inner[:], h2[:, 1, :], h2[:, 2, :], ALU.add), "hsum", i)
                    wait(pool, "g13", 3 * G, w, i)
                    sg.seq(pool, pool.tensor_tensor(g12[:], g[:, 1, :], g[:, 2, :], ALU.add), "gsum", i)
                    sg.seq(pool, pool.tensor_tensor(g012[:], g12[:], g[:, 0, :], ALU.add), "gsum", i)
                    sg.seq(pool, pool.tensor_tensor(gall[:], g12[:], g012[:], ALU.add), "gsum", i)
                    wait(pool, "h2", 4 * G, w, i)
                    sg.seq(pool, pool.tensor_tensor(outer[:], h2[:, 0, :], h2[:, 3, :], ALU.add), "hsum", i)
                    sg.seq(pool, pool.tensor_tensor(both[:], inner[:], outer[:], ALU.add), "hsum", i)
                    sg.up(pool.tensor_tensor(hist[:, :, bass.ds(UN * i + w, 1), :].rearrange("p m o b -> p m (o b)"), mb(both[:]),
                                             mb(inner[:]), ALU.add), "hist")
                    wait(pool, "u1", G + 4 * G, w, i)
                    sg.up(pool.tensor_tensor(v_half[:], u1[:], half_b[:], ALU.add), "v_shifted")
                    sg.up(pool.tensor_tensor(v_full[:], u1[:], full_b[:], ALU.add), "v_shifted")

        def product(pe, i, w, out, W, H, ready, n, done, blocks, seeded):
            arrived, left = -1, [G] * G
            for r, c in blocks:
                if r > arrived:
                    wait(pe, ready, n + r + 1, w, i)
                    arrived = r
                for m in GROUPS[c]:
                    at = 2 * B * (m - GROUPS[c][0])
                    for k in GROUPS[r]:
                        for q in range(NP):
                            first = left[c] == G and m == GROUPS[c][0] and k == GROUPS[r][0] and q == 0
                            ins = pe.matmul(out[c][:, at:at + 2 * B], W[:, q, k, P * m:P * m + P], H[:, k, :, :].rearrange("p q b -> p (q b)"),
                                            start=first and not seeded, stop=(left[c] == 1 and k == GROUPS[r][-1] and q == NP - 1),
                                            skip_group_check=True)
                left[c] -= 1
                if left[c] == 0:
                    sg.up(ins, done)

        @block.tensor
        def _(pe):
            sg.wait(pe, "fl_loads", 16 * len(loads))
            sg.up(pe.matmul(py[:, 0:B], t.ones[:], t.x3[:, :, 0], start=True, stop=True), "y_mm")
            sg.wait(pe, "y_act", 1)
            sg.up(pe.matmul(py[:, 0:B], t.ones[:], ysq[:], start=True, stop=True), "y_mm")
            for k in range(KH):
                if k >= 2:
                    sg.wait(pe, "w13_done", k - 1)
                sg.up(pe.matmul(pw[k % 2][:], w3n[:, P * k:P * k + P], w1[:], start=True, stop=True), "w13_ps")
            sg.wait(pe, "y_step", 3)
            for m in range(KH):
                pe.matmul(pv[:, B * m:B * m + B], w1[:, P * m:P * m + P], y0[:], start=True, stop=True)
            for m in range(KH):
                ins = pe.matmul(pv[:, NV + m:NV + m + 1], w1[:, P * m:P * m + P], b3[:], start=True, stop=True)
            sg.up(ins, "v_ps")
            sg.wait(pe, "scales", 2)
            sg.up(pe.transpose(py[0:2, :P], wmax[:], t.ident[:]), "wm_ps")
            sg.wait(pe, "scales", 8)
            sg.up(pe.matmul(py[:, 0:4], t.ones[0:2, :], wdiag[:], start=True, stop=True), "wm_ps")
            sg.wait(pe, "rest", 6)
            sg.wait(pe, "b2_moved", 16 * BP)
            sg.wait(pe, "sel16", 1)
            with pe.Fori(0, STEPS // UN) as i:
                for w in range(UN):
                    for e in range(4):
                        wait(pe, "u2", G * e, w, i)
                        for q in range(G):
                            pe.matmul(p2[q][:, 0:2 * B * len(GROUPS[q])], B2[:],
                                      sel[:, 2 * B * GROUPS[q][0]:2 * B * (GROUPS[q][-1] + 1)], start=True, stop=False, skip_group_check=True)
                        product(pe, i, w, p2, W2, H1, "in1", G * e, "l2_ps", BLOCKS2, True)
                        wait(pe, "g13", G * e, w, i)
                        product(pe, i, w, p1, W13, H2, "in2", G * e, "l13_ps", BLOCKS13, False)
            pe.wait_ge(sg.sem["hist"], STEPS)
            pe.wait_ge(sg.sem["g13"], STEPS * step["g13"])
            sg.wait(pe, "ones_set", 2)
            BLK = S // 4
            for j in range(4):
                if j >= 2:
                    sg.wait(pe, "slope", j - 1)
                for k in range(KH):
                    ins = pe.matmul(pw[j % 2][:], w3[:, k, :], hist[:, k, BLK * j:BLK * j + BLK, :].rearrange("p s b -> p (s b)"),
                                    start=(k == 0), stop=(k == KH - 1))
                sg.up(ins, "k_ps")

        @block.scalar
        def _(act):
            sg.wait(act, "fl_loads", 16 * len(loads))
            sg.up(act.activation(sel[:], sel_f[:], ACT.Copy), "sel16")
            sg.wait(act, "y_step", 1)
            sg.up(act.activation(ysq[:], yc[:], ACT.Square), "y_act")
            sg.wait(act, "y_mm", 2)
            sg.up(act.activation(ysd[:], py[:, 0:B], ACT.Sqrt, bias=t.eps[:]), "y_act")
            for k in range(KH):
                sg.wait(act, "w13_ps", k + 1)
                sg.up(act.activation(w13f[:, k, :], pw[k % 2][:], ACT.Copy), "w13_done")
            sg.wait(act, "w13_done", KH)
            for q in range(BP):
                for n, (full, split) in enumerate(splits[:3 if q < NP else 1]):
                    if q:
                        sg.wait(act, "rest", 3 * (q - 1) + n + 1)
                    elif n == 0:
                        sg.wait(act, "scales", 13)
                    sg.up(act.activation(split(q), full, ACT.Copy), "part")
            def steps(scale):
                with act.Fori(0, STEPS // UN) as i:
                    for w in range(UN):
                        for e in range(4):
                            for q in range(G):
                                wait(act, "u1", G * e + q + 1, w, i)
                                sg.up(act.activation(cols(h1, q), cols(u1, q), ACT.Tanh), "h1")
                            for q in range(G):
                                if e == 0 and q == 0:
                                    wait(act, "hsum", 0, w, i)
                                wait(act, "u2", G * e + q + 1, w, i)
                                sg.up(act.activation(cols(h2[:, e, :], q), cols(u2, q), ACT.Tanh, scale=scale), "h2")

            sg.wait(act, "large_set", 1)
            is_large = act.value_load(large[0:1, 0:1], min_val=0, max_val=1)
            counted = dict(sg.n)
            with act.If(is_large == 0):
                steps(WLOW / WMAX / HSCALE)
            sg.n.update(counted)
            with act.Else():
                steps(unscale2[:, 0:1])

        @block.vector
        def _(dve):
            sg.wait(dve, "y_mm", 1)
            sg.seq(dve, dve.tensor_tensor(yc[:], t.x3[:, :, 0], py[:, 0:B], ALU.subtract), "y_step")
            sg.wait(dve, "y_act", 2)
            sg.seq(dve, dve.reciprocal(ysd[:], ysd[:]), "y_step")
            sg.seq(dve, dve.tensor_tensor(y0[:], yc[:], ysd[:], ALU.mult), "y_step")
            sg.wait(dve, "v_ps", 1)
            wide = lambda x: x.rearrange("p (m o) -> p m o", o=1).to_broadcast([P, KH, B])
            sg.seq(dve, dve.tensor_copy(h1[:, 0:KH], pv[:, NV:NV + KH]), "prep")
            sg.seq(dve, dve.tensor_scalar(mb(half_b[:]), wide(h1[:, 0:KH]), DT / 2, None, ALU.mult), "prep")
            sg.seq(dve, dve.tensor_scalar(mb(full_b[:]), wide(h1[:, 0:KH]), DT, None, ALU.mult), "prep")
            sg.seq(dve, dve.tensor_scalar(b3dt[:], b3[:], DT, None, ALU.mult), "prep")
            sg.seq(dve, dve.tensor_tensor(mb(u1[:]), mb(pv[:, 0:NV]), wide(b1[:]), ALU.add), "prep")
            sg.seq(dve, dve.tensor_copy(u2[:, 0:1], u1[:, 0:1]), "prep")
            sg.seq(dve, dve.tensor_reduce(wmax[:, 0:1], w2f[:].rearrange("p k n -> p (k n)"), AX.X, ALU.max, apply_absolute_value=True), "scales")
            sg.wait(dve, "w13_done", KH)
            sg.seq(dve, dve.tensor_reduce(wmax[:, 1:2], w13f[:].rearrange("p k n -> p (k n)"), AX.X, ALU.max, apply_absolute_value=True), "scales")
            sg.wait(dve, "wm_ps", 1)
            sg.seq(dve, dve.tensor_reduce(wpow[:], py[0:2, 0:P], AX.X, ALU.max), "scales")
            sg.seq(dve, dve.tensor_scalar(wpow[:], wpow[:], WLOW, None, ALU.max), "scales")
            bits = lambda x: x.bitcast(mybir.dt.int32)
            sg.seq(dve, dve.tensor_scalar(bits(wpow[:]), bits(wpow[:]), 255 << 23, None, ALU.bitwise_and), "scales")
            sg.seq(dve, dve.tensor_scalar(bits(winv[:]), bits(wpow[:]), -1, 254 << 23, ALU.mult, ALU.add), "scales")
            for n, x in enumerate((wpow, winv)):
                sg.seq(dve, dve.tensor_scalar(wdiag[:, 2 * n:2 * n + 2], t.ident[0:2, 0:2], x[:, 0:1], None, ALU.mult), "scales")
            sg.wait(dve, "wm_ps", 2)
            sg.seq(dve, dve.tensor_reduce(wtop[:], py[:, 0:2], AX.X, ALU.max), "prep")
            sg.seq(dve, dve.tensor_scalar(large[:], wtop[:], WLOW / C, None, ALU.is_gt), "large_set")
            sg.seq(dve, dve.tensor_scalar(wscale[:], py[:, 2:4], C * WMAX, None, ALU.mult), "scales")
            sg.seq(dve, dve.tensor_scalar(unscale2[:], py[:, 0:1], C / WMAX / HSCALE, None, ALU.mult), "scales")
            for n, c in enumerate((DT / 2, DT, DT / 6)):
                sg.seq(dve, dve.tensor_scalar(coefs[:, n:n + 1], py[:, 1:2], C / WMAX / HSCALE * c, None, ALU.mult), "prep")
            for x, n in ((b2r[:], 0), (w2f[:], 0), (w13f[:], 1)):
                sg.seq(dve, dve.tensor_scalar(x, x, wscale[0:x.shape[0], n:n + 1], None, ALU.mult), "scales")
            for q in range(BP - 1):
                for n, (full, split) in enumerate(splits[:3 if q < NP - 1 else 1]):
                    sg.wait(dve, "part", 3 * q + n + 1)
                    sg.seq(dve, dve.tensor_tensor(full, full, split(q), ALU.subtract), "rest")
            sg.wait(dve, "part", 7)
            for n in range(2):
                sg.seq(dve, dve.tensor_copy(u2[:, n:n + 1], u1[:, n:n + 1]), "rest")
            for q in range(G):
                dve.tensor_copy(cols(u2, q), cols(u1, q)).then_inc(sg.sem["u1"], 1)
            dve.wait_ge(sg.sem["u1"], G)

            def split_h(h, H, layer, n, w, i):
                def high(q):
                    wait(dve, f"h{layer}", n + q + 1, w, i)
                    Hq = H[:, GROUPS[q][0]:GROUPS[q][-1] + 1, 0, :]
                    sg.up(dve.tensor_scalar(Hq, mb(cols(h, q)), HSCALE, None, ALU.mult), f"hi{layer}")

                def low(q):
                    wait(dve, f"hi{layer}", n + q + 1, w, i)
                    Hq = H[:, GROUPS[q][0]:GROUPS[q][-1] + 1, :, :]
                    sg.up(dve.scalar_tensor_tensor(out=Hq[:, :, 1, :], in0=mb(cols(h, q)), scalar=HSCALE, in1=Hq[:, :, 0, :],
                                                   op0=ALU.mult, op1=ALU.subtract), f"in{layer}")

                high(0)
                if layer == 1:
                    high(1)
                    low(0)
                    high(2)
                else:
                    low(0)
                    high(1)
                    high(2)
                low(1)
                low(2)

            def steps(factor):
                with dve.Fori(0, STEPS // UN) as i:
                    for w in range(UN):
                        for e, next_c in enumerate((0, 0, 1, 2)):
                            n = G * e
                            base = (v_half, v_half, v_full, acc)[e]

                            def slope_v(q):
                                wait(dve, "l13_ps", n + q + 1, w, i)
                                sg.up(dve.tensor_reduce(mb(cols(g[:, e, :], q)), parts(p1[q], q), AX.X, ALU.add), "g13")

                            def next_v(q):
                                wait(dve, "g13", n + q + 1, w, i)
                                sg.up(dve.scalar_tensor_tensor(out=cols(u1, q), in0=cols(g[:, e, :], q), scalar=factor[next_c],
                                                               in1=cols(base, q), op0=ALU.mult, op1=ALU.add), "u1")

                            split_h(h1, H1, 1, n, w, i)
                            if e == 3:
                                wait(dve, "gsum", 3, w, i)
                                sg.seq(dve, dve.scalar_tensor_tensor(out=acc[:], in0=gall[:], scalar=factor[2], in1=v_full[:],
                                                                     op0=ALU.mult, op1=ALU.add), "acc", i)
                            for q in range(G):
                                wait(dve, "l2_ps", n + q + 1, w, i)
                                sg.up(dve.tensor_reduce(mb(cols(u2, q)), parts(p2[q], q), AX.X, ALU.add), "u2")
                            split_h(h2[:, e, :], H2, 2, n, w, i)
                            if e == 0:
                                wait(dve, "v_shifted", 2, w, i)
                            slope_v(0)
                            slope_v(1)
                            next_v(0)
                            slope_v(2)
                            next_v(1)
                            next_v(2)

            is_large = dve.value_load(large[0:1, 0:1], min_val=0, max_val=1)
            counted = dict(sg.n)
            with dve.If(is_large == 0):
                steps(COEFS)
            sg.n.update(counted)
            with dve.Else():
                steps([coefs[:, n:n + 1] for n in range(3)])
            BLK = S // 4
            for j in range(4):
                sg.wait(dve, "k_ps", j + 1)
                sg.seq(dve, dve.tensor_scalar(slope[:, BLK * j:BLK * j + BLK, :].rearrange("p s b -> p (s b)"), pw[j % 2][:],
                                              DT / 6, b3dt[:, 0:1], ALU.mult, ALU.add), "slope")
            sg.seq(dve, dve.tensor_copy(Y[:, :, 0], y0[:]), "states")
            for b in range(B):
                sg.seq(dve, dve.tensor_tensor_scan(Y[:, b, 1:S], ones1[:, 0:STEPS], slope[:, 0:STEPS, b], y0[:, b:b + 1],
                                                   ALU.mult, ALU.add), "states")
            sg.seq(dve, dve.tensor_tensor(t.x4[:], t.x3[:], Y[:], ALU.add), "states")

        for name in sg.per:
            if sg.per[name]:
                sg.check(name)


class ExpertBuffers:

    LOADS = 16 * 9

    def __init__(self, sb, name, scalers=None):
        self.first, self.second = sb(f"W12_{name}", [P, 2, NF, FF]), sb(f"W3_{name}", [P, 2, NF, C])
        self.scalers = scalers or (sb("s12", [P, 2, FF]), sb("s3", [P, 2, C]))

    def load(self, sp, dram, e, loaded):
        first, second, (s12, s3) = self.first, self.second, self.scalers
        pick = lambda n: dram[n][bass.ds(e, 1)].rearrange("o p x -> (o p) x")
        for w in range(2):
            sp.dma_start(first[:, w, 0:NB, :].rearrange("p c o -> p (c o)"), pick(f"spline{w + 1}")).then_inc(loaded, 16)
            sp.dma_start(first[:, w, NB, :], pick(f"base{w + 1}")).then_inc(loaded, 16)
            sp.dma_start(s12[:, w, :], pick(f"scaler{w + 1}")).then_inc(loaded, 16)
        sp.dma_start(second[:, :, 0:NB, :].rearrange("p k c o -> p k (c o)"), pick("spline3").rearrange("p (k x) -> p k x", k=2)).then_inc(loaded, 16)
        sp.dma_start(second[:, :, NB, :], pick("base3").rearrange("p (k x) -> p k x", k=2)).then_inc(loaded, 16)
        sp.dma_start(s3[:], pick("scaler3").rearrange("p (k x) -> p k x", k=2)).then_inc(loaded, 16)

    def scale(self, pool, k, scaled):
        first, second, (s12, s3) = self.first, self.second, self.scalers
        c, o = k // 2, k % 2
        pool.tensor_tensor(first[:, o, c, :], first[:, o, c, :], s12[:, o, :], ALU.mult)
        pool.tensor_tensor(second[:, o, c, :], second[:, o, c, :], s3[:, o, :], ALU.mult).then_inc(scaled, 1)


def window_attention(nc, t):
    with ExitStack() as ctx:
        def sb(name, shape, dt=F32):
            return ctx.enter_context(nc.sbuf_tensor(name, shape, dt))

        def ps(name):
            return ctx.enter_context(nc.psum_tensor(name, [P, S], F32))

        R = DIL
        sg = Signals(nc, "window")
        sg.add(wa_loads=0, vzero=0, w_load=0, w_scaled=0, xb_done=1, dve_step=3, ln_mean=2, ln_var=2, ln_sq=2, ln_sd=2, ln_cent=2, ln_out=2,
               wq_ps=1, wk_ps=1, wv_ps=1, wq_done=1, wk_done=1, wv_done=1, wqm=HEADS, wscore=HEADS, wmask=HEADS, wmax=2 * HEADS,
               wprob=HEADS, wpadw=HEADS, wsum=3 * HEADS, wnorm=HEADS, wtrans=HEADS, wcopy=HEADS, wpv=HEADS, wo_done=1,
               f_ps=1, f_done=1, g_ps=1, g_done=1, x5_done=1, logit_ps=1, wa_end=3)
        xb, z, xc, sq, sd = (sb("w" + n, [P, S]) for n in ("xb", "z", "xc", "sq", "sd"))
        qT, kT, xa, f, g, x5, z5 = (sb("w" + n, [P, S]) for n in ("qT", "kT", "xa", "f", "g", "x5", "z5"))
        qm = [sb(f"wqm{n}", [P, S]) for n in range(2)]
        V = sb("wV", [P, R, HEADS * VW])
        sc = [sb(f"wsc{n}", [P, R, P]) for n in range(2)]
        PT = [sb(f"wPT{n}", [P, R, P]) for n in range(2)]
        m, padw, rs = ([sb(f"w{name}{n}", [P, R]) for n in range(2)] for name in ("m", "padw", "rs"))
        w = {n: sb("wa_" + n, [P, C]) for n in ("q", "k", "v", "f1", "f2")}
        bias, gate, band, pads = sb("wa_bias", [P, 2]), sb("wa_gate", [P, NE]), sb("wa_band", [P, P]), sb("wa_pads", [P, 2])
        pS, pT, pM = [ps("wpS0"), ps("wpS1")], [ps("wpT0"), ps("wpT1")], [ps(f"wpM{n}") for n in range(3)]
        pO = ps("wpO")
        a = t.dram
        col = lambda ap: ap.rearrange("(p o) -> p o", o=1)
        loads = [(w["q"][:], a["L3_attn_Wq"]), (w["k"][:], a["L3_attn_Wk"]), (w["v"][:], a["L3_attn_Wv"]), (w["f1"][:], a["L3_attn_Wff1"]),
                 (w["f2"][:], a["L3_attn_Wff2"]), (bias[:, 0:1], col(a["L3_attn_bff1"])), (bias[:, 1:2], col(a["L3_attn_bff2"])),
                 (gate[:], a["gate_t"]), (band[:], a["c_band"]), (pads[:], a["c_pads"])]
        res = lambda x, r: x[:, r:S:R]
        one = lambda ap: ap.rearrange("p (o s) -> p o s", o=1)
        block = ctx.enter_context(nc.Block())

        @block.sync
        def _(sp):
            for dst, src in loads:
                sg.up(sp.dma_start(dst, src), "wa_loads", 16)
            t.expert0.load(sp, a, 0, sg.sem["w_load"])

        @block.gpsimd
        def _(pool):
            sg.up(pool.memset(V[:], 0.0), "vzero")
            pool.wait_ge(sg.sem["w_load"], t.expert0.LOADS)
            for k in range(2 * NB):
                t.expert0.scale(pool, k, sg.sem["w_scaled"])

        @block.tensor
        def _(pe):
            sg.wait(pe, "wa_loads", 16 * len(loads))
            with pe.Fori(0, B) as i:
                layer_norm_pe(pe, sg, t.ones[:], xb[:], sq[:], pM[0][:], pM[1][:], 1, i, "xb_done", 1)
                sg.wait(pe, "ln_out", 1, i)
                sg.up(pe.matmul(pM[0][:], w["q"][:], z[:], start=True, stop=True), "wq_ps")
                sg.up(pe.matmul(pM[1][:], w["k"][:], z[:], start=True, stop=True), "wk_ps")
                for r in range(R):
                    ins = pe.matmul(pM[2][:, r * P:(r + 1) * P], res(z, r), w["v"][:], start=True, stop=True)
                sg.up(ins, "wv_ps")

                def score(h):
                    sg.wait(pe, "wqm", h + 1, i)
                    if h == 0:
                        sg.wait(pe, "wk_done", 1, i)
                    if h >= 2:
                        sg.wait(pe, "wmask", h - 1, i)
                    for r in range(R):
                        ins = pe.matmul(pS[h % 2][:, r * P:(r + 1) * P], res(qm[h % 2], r), res(kT, r), start=True, stop=True)
                    sg.up(ins, "wscore")

                def weigh(h):
                    if h == 0:
                        sg.wait(pe, "wv_done", 1, i)
                    sg.wait(pe, "wcopy", h + 1, i)
                    for r in range(R):
                        ins = pe.matmul(pO[:, r * P:(r + 1) * P], V[:, r, h * P:(h + 1) * P], PT[h % 2][:, r, :],
                                        start=(h == 0 and r == 0), stop=(h == HEADS - 1), skip_group_check=True)
                    sg.up(ins, "wpv")

                score(0)
                score(1)
                for h in range(HEADS):
                    sg.wait(pe, "wnorm", h + 1, i)
                    if h >= 2:
                        sg.wait(pe, "wcopy", h - 1, i)
                    for r in range(R):
                        ins = pe.transpose(pT[h % 2][:, r * P:(r + 1) * P], sc[h % 2][:, r, :], t.ident[:])
                    sg.up(ins, "wtrans")
                    if h + 2 < HEADS:
                        score(h + 2)
                    if h:
                        weigh(h - 1)
                weigh(HEADS - 1)
                sg.wait(pe, "wo_done", 1, i)
                sg.up(pe.matmul(pM[2][:], w["f1"][:], xa[:], start=True, stop=True), "f_ps")
                sg.wait(pe, "f_done", 1, i)
                sg.up(pe.matmul(pM[0][:], w["f2"][:], f[:], start=True, stop=True), "g_ps")
                layer_norm_pe(pe, sg, t.ones[:], x5[:], sq[:], pM[0][:], pM[1][:], 2, i, "x5_done", 1)
                sg.wait(pe, "ln_out", 2, i)
                for j in range(QT):
                    ins = pe.matmul(pM[2][:, j * NE:(j + 1) * NE], z5[:, j * P:(j + 1) * P], gate[:], start=True, stop=True)
                sg.up(ins, "logit_ps")

        @block.scalar
        def _(act):
            sg.wait(act, "wa_loads", 16 * len(loads))
            with act.Fori(0, B) as i:
                layer_norm_act(act, sg, xc[:], sq[:], sd[:], pM[1][:], t.eps[:], 1, i)
                sg.wait(act, "wq_ps", 1, i)
                sg.up(act.activation(qT[:], pM[0][:], ACT.Copy), "wq_done")
                for h in range(HEADS + 1):
                    if h < HEADS:
                        k = h % 2
                        sg.wait(act, "wmax", 2 * h + 2, i)
                        sg.up(act.activation(padw[k][:], m[k][:], ACT.Exp), "wpadw")
                        for r in range(R):
                            ins = act.activation(sc[k][:, r, :], sc[k][:, r, :], ACT.Exp, bias=m[k][:, r:r + 1],
                                                 accum_out=rs[k][:, r:r + 1])
                        sg.up(ins, "wprob")
                    if h:
                        sg.wait(act, "wtrans", h, i)
                        if h >= 3:
                            sg.wait(act, "wpv", h - 2, i)
                        sg.up(act.activation(PT[(h - 1) % 2][:].rearrange("p r q -> p (r q)"), pT[(h - 1) % 2][:], ACT.Copy), "wcopy")
                sg.wait(act, "f_ps", 1, i)
                sg.up(act.activation(f[:], pM[2][:], ACT.Relu, bias=bias[:, 0:1]), "f_done")
                sg.wait(act, "g_ps", 1, i)
                sg.up(act.activation(g[:], pM[0][:], ACT.Relu, bias=bias[:, 1:2]), "g_done")
                layer_norm_act(act, sg, xc[:], sq[:], sd[:], pM[1][:], t.eps[:], 2, i)

        @block.vector
        def _(dve):
            sg.wait(dve, "wa_loads", 16 * len(loads))
            sg.wait(dve, "vzero", 1)
            with dve.Fori(0, B) as i:
                sg.seq(dve, dve.tensor_scalar(one(xb[:]), t.x4[:, bass.ds(i, 1), :], 0.0, None, ALU.add), "xb_done", i)
                layer_norm_dve(dve, sg, xb[:], xc[:], sd[:], pM[0][:], z[:], 1, i)
                sg.wait(dve, "wk_ps", 1, i)
                sg.seq(dve, dve.tensor_copy(kT[:], pM[1][:]), "wk_done", i)
                sg.wait(dve, "wv_ps", 1, i)
                sg.seq(dve, dve.tensor_copy(V[:].rearrange("p t (h x) -> p t h x", x=VW)[:, :, :, 0:DH],
                                            pM[2][:].rearrange("p (t h d) -> p t h d", t=R, h=HEADS)), "wv_done", i)
                sg.wait(dve, "wq_done", 1, i)

                def queries(h):
                    sg.seq(dve, dve.tensor_scalar(qm[h % 2][:], qT[:], t.hmask[:, h:h + 1], None, ALU.mult), "wqm", i)

                def masked(h):
                    k = h % 2
                    sg.wait(dve, "wscore", h + 1, i)
                    if h >= 2:
                        sg.wait(dve, "wtrans", h - 1, i)
                    sg.seq(dve, dve.tensor_tensor(sc[k][:], pS[k][:].rearrange("p (r k) -> p r k", r=R),
                                                  band[:].rearrange("p (o k) -> p o k", o=1).to_broadcast([P, R, P]), ALU.add), "wmask", i)
                    sg.seq(dve, dve.tensor_reduce(m[k][:], sc[k][:], AX.X, ALU.max), "wmax", i)
                    sg.seq(dve, dve.tensor_scalar(m[k][:], m[k][:], pads[:, 0:1], -1.0, ALU.max, ALU.mult), "wmax", i)

                def normalised(h):
                    k = h % 2
                    sg.wait(dve, "wpadw", h + 1, i)
                    sg.wait(dve, "wprob", h + 1, i)
                    sg.seq(dve, dve.scalar_tensor_tensor(out=rs[k][:], in0=padw[k][:], scalar=pads[:, 1:2], in1=rs[k][:],
                                                         op0=ALU.mult, op1=ALU.add), "wsum", i)
                    sg.seq(dve, dve.tensor_scalar(rs[k][:], rs[k][:], float(DH) ** 0.5, None, ALU.mult), "wsum", i)
                    sg.seq(dve, dve.reciprocal(rs[k][:], rs[k][:]), "wsum", i)
                    sg.seq(dve, dve.tensor_tensor(sc[k][:], sc[k][:], rs[k][:].rearrange("p (r o) -> p r o", o=1).to_broadcast([P, R, P]),
                                                  ALU.mult), "wnorm", i)

                queries(0)
                queries(1)
                for h in range(HEADS + 1):
                    if h < HEADS:
                        masked(h)
                    if h:
                        normalised(h - 1)
                    if h + 2 < HEADS:
                        queries(h + 2)
                sg.wait(dve, "wpv", HEADS, i)
                sg.seq(dve, dve.tensor_copy(xa[:].rearrange("p (a r) -> p r a", r=R), pO[:].rearrange("p (r a) -> p r a", r=R)), "wo_done", i)
                sg.seq(dve, dve.tensor_tensor(x5[:], xb[:], xa[:], ALU.add), "dve_step", i)
                sg.wait(dve, "g_done", 1, i)
                sg.seq(dve, dve.tensor_tensor(x5[:], x5[:], g[:], ALU.add), "x5_done", i)
                layer_norm_dve(dve, sg, x5[:], xc[:], sd[:], pM[0][:], z5[:], 2, i)
                sg.seq(dve, dve.tensor_scalar(t.x5[:, bass.ds(i, 1), :], one(x5[:]), 0.0, None, ALU.add), "wa_end", i)
                sg.seq(dve, dve.tensor_scalar(t.z[:, bass.ds(i, 1), :], one(z5[:]), 0.0, None, ALU.add), "wa_end", i)
                sg.wait(dve, "logit_ps", 1, i)
                sg.seq(dve, dve.tensor_scalar(t.logits[:, bass.ds(i, 1), :, :].rearrange("p o j e -> p o (j e)"),
                                              one(pM[2][:, 0:QT * NE]), 0.0, None, ALU.add), "wa_end", i)

        for name in sg.per:
            if sg.per[name]:
                sg.check(name)


def experts(nc, t, out_dram):
    UT = 2 * B
    TURNS = NE // 2
    LOADS = ExpertBuffers.LOADS
    ITEMS = 2 * NB
    XIT = B * NB
    ORDER = [NB] + list(range(NB))
    CHUNKS = [ORDER[0:2], ORDER[2:4], ORDER[4:6], ORDER[6:9]]
    SIXTH = 6.0 ** -0.5
    D = 3
    with ExitStack() as ctx:
        def sb(name, shape, dt=F32):
            return ctx.enter_context(nc.sbuf_tensor(name, shape, dt))

        def ps(name):
            return ctx.enter_context(nc.psum_tensor(name, [P, S], F32))

        sg = Signals(nc, "experts")
        names = ("ex_const gate_step gate_exp xabs xpq xsq xcube xtanh xsilu xfeat w_load0 w_load1 w_scaled l1_ps l2_ps l2_feat gb_ps "
                 "gb_done h1_done g_done th_done silu_done silu_used abs_done pq_done sq_done cube_done feat ge_done out_step out_done "
                 "final").split()
        sg.add(**{n: 0 for n in names})
        sem = sg.sem
        FX = sb("FX", [P, NF, B * S])
        F2 = sb("F2", [P, NF, 2, S])
        W = [t.expert0, ExpertBuffers(sb, "odd", t.expert0.scalers)]
        W12, W3 = [w.first for w in W], [w.second for w in W]
        g, gs = sb("g2", [P, 2, S]), sb("gs", [P, S])
        dist, pn, qn = ([sb(f"{n}{k}", [P, S]) for k in range(D)] for n in ("dist", "pn", "qn"))
        gates = sb("gates", [P, NE, B * QT])
        rank, tmp = ([x[:, 0:B * QT * NE].rearrange("p (n e) -> p n e", e=NE) for x in pn[0:2]])
        gmx, ge = sb("gmx", [P, B * QT]), [sb(f"ge{n}", [P, B * QT]) for n in range(2)]
        cen = sb("cen", [P, NB])
        bank = [ps(f"l1_{n}") for n in range(4)]
        out2, pg = [ps("l2_0"), ps("l2_1")], ps("pg")
        a = t.dram
        lg = t.logits[:].rearrange("p b j e -> p (b j) e")
        slot = lambda k: F2[:, k // 2, k % 2, :]
        xslot = lambda k: FX[:, k % NB, S * (k // NB):S * (k // NB) + S]
        block = ctx.enter_context(nc.Block())

        @block.sync
        def _(sp):
            sp.dma_start(cen[:], a["c_centres"]).then_inc(sem["ex_const"], 16)
            W[1].load(sp, a, 1, sem["w_load1"])
            with sp.Fori(0, TURNS - 1) as i:
                sp.wait_ge(sem["l2_ps"], UT * i + B)
                W[0].load(sp, a, 2 * i + 2, sem["w_load0"])
                sp.wait_ge(sem["l2_ps"], UT * i + 2 * B)
                W[1].load(sp, a, 2 * i + 3, sem["w_load1"])
            sp.wait_ge(sem["out_done"], NE * B)
            sp.dma_start(out_dram, t.x5[:]).then_inc(sem["final"], 16)
            sp.wait_ge(sem["final"], 16)

        @block.gpsimd
        def _(pool):
            def x_items(b):
                for k in range(NB * b, NB * b + NB):
                    pool.wait_ge(sem["xcube"], k + 1)
                    pool.tensor_tensor(xslot(k), xslot(k), dist[k % D][:], ALU.subtract).then_inc(sem["xfeat"], 1)

            def turn(i, last):
                for m in range(UT):
                    base = ITEMS * UT * i + ITEMS * m
                    for k in range(ITEMS):
                        if m == 2:
                            if k == 0:
                                pool.wait_ge(sem["w_load1"], LOADS * i + LOADS)
                            W[1].scale(pool, k, sem["w_scaled"])
                        if m == 6 and not last:
                            if k == 0:
                                pool.wait_ge(sem["w_load0"], LOADS * i + LOADS)
                            W[0].scale(pool, k, sem["w_scaled"])
                        pool.wait_ge(sem["cube_done"], base + k + 1)
                        pool.tensor_tensor(slot(k), slot(k), dist[k % D][:], ALU.subtract).then_inc(sem["feat"], 1)

            for b in range(B):
                x_items(b)
            with pool.Fori(0, TURNS - 1) as i:
                turn(i, False)
            turn(TURNS - 1, True)

        @block.tensor
        def _(pe):
            def first(par, b, group):
                o, w = group // 2, group % 2
                for f in range(NF):
                    ins = pe.matmul(bank[group][:], W12[par][:, w, f, P * o:P * o + P], FX[:, f, S * b:S * b + S],
                                    start=(f == 0), stop=(f == NF - 1))
                ins.then_inc(sem["l1_ps"], 1)

            def turn(i, last):
                for m in range(UT):
                    n = UT * i + m
                    par, b = m // B, m % B
                    for j in range(4):
                        if m + 1 < UT or not last:
                            if j == 0:
                                if m + 1 < B:
                                    pe.wait_ge(sem["xfeat"], NB * (m + 2))
                                if m + 1 == B:
                                    pe.wait_ge(sem["w_scaled"], 2 * ITEMS * i + ITEMS)
                                if m + 1 == UT:
                                    pe.wait_ge(sem["w_scaled"], 2 * ITEMS * i + 2 * ITEMS)
                            if j % 2 == 0:
                                pe.wait_ge(sem["g_done"], 2 * n + j // 2 + 1)
                            first((m + 1) // B % 2, (m + 1) % B, j)
                        for f in CHUNKS[j]:
                            if f == NB:
                                pe.wait_ge(sem["silu_done"], n + 1)
                                if m % B == 0:
                                    pe.wait_ge(sem["ge_done"], 2 * i + par + 1)
                                pe.wait_ge(sem["gb_done"], n)
                                for q in range(QT):
                                    ins = pe.matmul(pg[:, P * q:P * q + P],
                                                    ge[par][:, QT * b + q:QT * b + q + 1].to_broadcast([P, P]), t.ident[:],
                                                    start=True, stop=True)
                                ins.then_inc(sem["gb_ps"], 1)
                            else:
                                pe.wait_ge(sem["feat"], ITEMS * UT * i + ITEMS * m + 2 * f + 2)
                            for k in range(2):
                                ins = pe.matmul(out2[m % 2][:], W3[par][:, k, f, :], F2[:, f, k, :],
                                                start=(f == NB and k == 0), stop=(f == NB - 1 and k == 1))
                            if f != NB - 1:
                                ins.then_inc(sem["silu_used" if f == NB else "l2_feat"], 1)
                    ins.then_inc(sem["l2_ps"], 1)

            pe.wait_ge(sem["xfeat"], NB)
            pe.wait_ge(sem["xsilu"], B)
            pe.transpose(pg[:, 0:P], t.ident[:], t.ident[:]).then_inc(sem["l2_feat"], NB - 1)
            for group in range(4):
                first(0, 0, group)
            with pe.Fori(0, TURNS - 1) as i:
                turn(i, False)
            turn(TURNS - 1, True)

        @block.scalar
        def _(act):
            def squares(k, q2, done):
                act.activation(dist[k % D][:], pn[k % D][:], ACT.Square, scale=SIXTH).then_inc(sem[done], 1)
                act.activation(q2, qn[k % D][:], ACT.Square, scale=2 * SIXTH).then_inc(sem[done], 1)

            act.wait_ge(sem["ex_const"], 16)
            for b in range(B):
                if b:
                    act.wait_ge(sem["xsilu"], b)
                act.activation(gs[:], t.z[:, b, :], ACT.Tanh, scale=0.5).then_inc(sem["xtanh"], 1)
            for k in range(XIT + 1):
                if k < XIT:
                    if k >= D:
                        act.wait_ge(sem["xfeat"], k + 1 - D)
                    act.activation(dist[k % D][:], t.z[:, k // NB, :], ACT.Abs, scale=2.5, bias=cen[:, k % NB:k % NB + 1]).then_inc(sem["xabs"], 1)
                if k:
                    act.wait_ge(sem["xpq"], 2 * k)
                    squares(k - 1, xslot(k - 1), "xsq")
            act.wait_ge(sem["gate_step"], B + 2)
            act.activation(rank[:], rank[:], ACT.Exp).then_inc(sem["gate_exp"], 1)
            act.wait_ge(sem["xfeat"], XIT)

            def head(n, base):
                for o in range(2):
                    act.wait_ge(sem["l1_ps"], 4 * n + 2 * o + 2)
                    if o == 0:
                        act.wait_ge(sem["silu_done"], n)
                        act.wait_ge(sem["abs_done"], base)
                    act.activation(g[:, o, :], bank[2 * o][:], ACT.Copy).then_inc(sem["h1_done"], 1)
                for o in range(2):
                    act.wait_ge(sem["g_done"], 2 * n + o + 1)
                    if o == 0:
                        act.wait_ge(sem["silu_used"], n)
                    act.activation(F2[:, NB, o, :], g[:, o, :], ACT.Tanh, scale=0.5).then_inc(sem["th_done"], 1)

            def turn(i, last):
                for m in range(UT):
                    n = UT * i + m
                    base = ITEMS * UT * i + ITEMS * m
                    for k in range(ITEMS + 1):
                        if k < ITEMS:
                            act.wait_ge(sem["feat"], base + max(k + 1 - D, 0))
                            act.activation(dist[k % D][:], g[:, k % 2, :], ACT.Abs, scale=2.5,
                                           bias=cen[:, k // 2:k // 2 + 1]).then_inc(sem["abs_done"], 1)
                        if k:
                            act.wait_ge(sem["pq_done"], 2 * (base + k))
                            if k % 2:
                                c = (k - 1) // 2
                                if c < NB - 1:
                                    act.wait_ge(sem["l2_feat"], (NB - 1) * n + c + 1)
                                else:
                                    act.wait_ge(sem["l2_ps"], n)
                            squares(k - 1, slot(k - 1), "sq_done")
                    act.wait_ge(sem["gb_ps"], n + 1)
                    act.wait_ge(sem["out_done"], n)
                    act.activation(gs[:], pg[:], ACT.Copy).then_inc(sem["gb_done"], 1)
                    if m + 1 < UT or not last:
                        head(n + 1, base + ITEMS)

            head(0, 0)
            with act.Fori(0, TURNS - 1) as i:
                turn(i, False)
            turn(TURNS - 1, True)

        @block.vector
        def _(dve):
            def step(ins, name="gate_step", done=[0]):
                ins.then_inc(sem[name], 1)
                done[0] += 1
                dve.wait_ge(sem[name], done[0])

            def hats(k, done):
                dve.tensor_scalar(pn[k % D][:], dist[k % D][:], 2.0, -2.0, ALU.min, ALU.add).then_inc(sem[done], 1)
                dve.tensor_scalar(qn[k % D][:], dist[k % D][:], 1.0, -1.0, ALU.min, ALU.add).then_inc(sem[done], 1)

            def cubes(k, q2, count, sq, done):
                dve.wait_ge(sem[sq], 2 * count - 1)
                dve.tensor_tensor(dist[k % D][:], dist[k % D][:], pn[k % D][:], ALU.mult)
                dve.wait_ge(sem[sq], 2 * count)
                dve.tensor_tensor(q2, q2, qn[k % D][:], ALU.mult).then_inc(sem[done], 1)

            for b in range(B):
                dve.wait_ge(sem["xtanh"], b + 1)
                step(dve.tensor_scalar(gs[:], gs[:], 0.5, 0.5, ALU.mult, ALU.add))
                dve.tensor_tensor(FX[:, NB, S * b:S * b + S], gs[:], t.z[:, b, :], ALU.mult).then_inc(sem["xsilu"], 1)
            for k in range(XIT + 1):
                if k < XIT:
                    dve.wait_ge(sem["xabs"], k + 1)
                    hats(k, "xpq")
                if k:
                    cubes(k - 1, xslot(k - 1), k, "xsq", "xcube")

            NT = B * QT
            wide = lambda x: x.rearrange("p (n o) -> p n o", o=1).to_broadcast([P, NT, NE])
            step(dve.tensor_reduce(gmx[:], lg, AX.X, ALU.max))
            step(dve.tensor_tensor(rank[:], lg, wide(gmx[:]), ALU.subtract))
            dve.wait_ge(sem["gate_exp"], 1)
            step(dve.tensor_scalar(gates[:].rearrange("p e n -> p n e"), rank[:], 1.0, None, ALU.mult))
            step(dve.memset(rank[:], 0.0))
            for j in range(NE):
                one = lg[:, :, j:j + 1]
                step(dve.tensor_tensor(tmp[:, :, 0:j + 1], one.to_broadcast([P, NT, j + 1]), lg[:, :, 0:j + 1], ALU.is_gt))
                if j + 1 < NE:
                    step(dve.tensor_tensor(tmp[:, :, j + 1:NE], one.to_broadcast([P, NT, NE - 1 - j]), lg[:, :, j + 1:NE], ALU.is_ge))
                step(dve.tensor_tensor(rank[:], rank[:], tmp[:], ALU.add))
            step(dve.tensor_scalar(rank[:], rank[:], 2.0, None, ALU.is_lt))
            gt = gates[:].rearrange("p e n -> p n e")
            step(dve.tensor_tensor(gt, gt, rank[:], ALU.mult))
            step(dve.tensor_reduce(gmx[:], gt, AX.X, ALU.add))
            step(dve.reciprocal(gmx[:], gmx[:]))
            step(dve.tensor_tensor(gt, gt, wide(gmx[:]), ALU.mult))

            def head(n):
                for o in range(2):
                    dve.wait_ge(sem["h1_done"], 2 * n + o + 1)
                    dve.tensor_tensor(g[:, o, :], g[:, o, :], bank[2 * o + 1][:], ALU.mult).then_inc(sem["g_done"], 1)

            def silu(n):
                for o in range(2):
                    x = F2[:, NB, o, :]
                    dve.wait_ge(sem["th_done"], 2 * n + o + 1)
                    dve.tensor_scalar(x, x, 0.5, 0.5, ALU.mult, ALU.add).then_inc(sem["out_step"], 1)
                for o in range(2):
                    x = F2[:, NB, o, :]
                    dve.wait_ge(sem["out_step"], 3 * n + o + 1)
                    ins = dve.tensor_tensor(x, x, g[:, o, :], ALU.mult)
                ins.then_inc(sem["silu_done"], 1)

            def turn(i, last):
                for m in range(UT):
                    n = UT * i + m
                    par, b = m // B, m % B
                    base = ITEMS * UT * i + ITEMS * m
                    if b == 0:
                        dve.tensor_scalar(ge[par][:].rearrange("p (o n) -> p o n", o=1), gates[:, bass.ds(2 * i + par, 1), :], 1.0, None,
                                          ALU.mult).then_inc(sem["ge_done"], 1)
                    for k in range(ITEMS + 1):
                        if k < ITEMS:
                            dve.wait_ge(sem["abs_done"], base + k + 1)
                            hats(k, "pq_done")
                        if k == 0:
                            silu(n)
                        if k:
                            cubes(k - 1, slot(k - 1), base + k, "sq_done", "cube_done")
                    if m + 1 < UT or not last:
                        head(n + 1)
                    dve.wait_ge(sem["gb_done"], n + 1)
                    dve.wait_ge(sem["l2_ps"], n + 1)
                    dve.tensor_tensor(gs[:], gs[:], out2[m % 2][:], ALU.mult).then_inc(sem["out_step"], 1)
                    dve.wait_ge(sem["out_step"], 3 * n + 3)
                    dve.tensor_tensor(t.x5[:, b, :], t.x5[:, b, :], gs[:], ALU.add).then_inc(sem["out_done"], 1)

            head(0)
            with dve.Fori(0, TURNS - 1) as i:
                turn(i, False)
            turn(TURNS - 1, True)


def shape_constants():
    f = np.float32
    head = np.arange(C) // DH
    nf, nt, H, W = 16, 16, 16, 32
    ln = np.log2(np.maximum(np.arange(0, H * nf, dtype=f), f(1)))
    ln[0] = -2.0
    ln = (ln.reshape(H, nf).T * np.arange(1, nf + 1, dtype=f)[:, None]).astype(f)
    freq = np.stack([np.cos(ln), np.sin(ln)], axis=1).reshape(2 * nf, H)
    k = np.arange(0, nt, dtype=f) + f(0.5)
    xs = np.arange(0, nt * W, dtype=f).reshape(W, nt).T
    theta = (k[:, None] * xs / f(W * nt) * f(6.283185307179586)).astype(f)
    time = np.stack([np.cos(theta), np.sin(theta)], axis=1).reshape(2 * nt, W)
    emb = np.concatenate([np.repeat(freq, W, axis=1), np.tile(time, (1, H))], axis=0)
    a = np.arange(P)
    outside = (np.maximum(0, WIN - a) + np.maximum(0, a + WIN - (P - 1))).astype(f)
    sel = np.zeros((BP * KH, 2, 2, 2, B), f)
    for part in range(BP):
        for m in range(KH):
            sel[KH * part + m, m // 2, m % 2, 0, :] = HSCALE
    return {
        "c_ident": np.eye(P, dtype=f),
        "c_ones": np.full((P, P), 1.0 / C, f),
        "c_hmask": (head[:, None] == np.arange(HEADS)[None, :]).astype(f),
        "c_eps": np.full((P, 1), EPS, f),
        "c_group": ((a[:, None] // 4) == (a[None, :] // 4)).astype(f) / f(4),
        "c_emb": emb.astype(f),
        "c_onerow": np.ones((1, P), f),
        "c_band": np.where(np.abs(a[:, None] - a[None, :]) <= WIN, 0.0, BIG).astype(f),
        "c_pads": np.stack([np.where(outside > 0, 0.0, BIG).astype(f), outside], axis=1),
        "c_centres": np.tile((3.5 - np.arange(NB, dtype=f))[None, :], (P, 1)),
        "c_sel": sel.reshape(BP * KH, 32),
    }


class Stage:
    pass


def conv_attn_hybrid(nc, dram, out_dram):
    t = Stage()
    t.dram = dram
    with ExitStack() as ctx:
        def sb(name, shape):
            return ctx.enter_context(nc.sbuf_tensor(name, shape, F32))

        t.ident, t.ones, t.hmask, t.eps = sb("ident", [P, P]), sb("ones", [P, P]), sb("hmask", [P, HEADS]), sb("eps", [P, 1])
        stream = sb("stream", [P, B, S])
        t.x2 = t.x3 = t.x4 = t.x5 = stream
        t.z, t.logits = sb("z_all", [P, B, S]), sb("logits_all", [P, B, QT, NE])
        t.expert0 = ExpertBuffers(sb, "even")
        for stage in (global_attention, batch_attention, flow, window_attention):
            with nc.cleanup_on_exit():
                stage(nc, t)
        experts(nc, t, out_dram)


def laid_out(x):
    a = {n: v for n, v in x.items() if n == "x" or n.startswith(("L0_", "L1_", "L3_attn"))}
    for n in ("in_proj_bias", "out_bias"):
        a["L2_attn_" + n] = x["L2_attn_" + n]
    a["bw_in"], a["bw_out"] = x["L2_attn_in_proj_weight"].T, x["L2_attn_out_weight"].T
    for n in ("W3", "b2", "b3"):
        a["L2_ffn_" + n] = x["L2_ffn_" + n]
    rows = lambda w, n: w.T.reshape(n, P, -1).transpose(1, 0, 2)
    a["ff_w1"], a["ff_w2"], a["ff_w3"] = x["L2_ffn_W1"].T, rows(x["L2_ffn_W2"], KH), rows(x["L2_ffn_W3"], KH)
    a["ff_b1"] = x["L2_ffn_b1"].reshape(KH, P).T
    a["gate_t"] = x["L3_ffn_gate_w"].T
    for n in (1, 2):
        a[f"spline{n}"] = x[f"L3_ffn_spline_w{n}"].transpose(0, 2, 3, 1).reshape(NE, P, -1)
        a[f"base{n}"] = x[f"L3_ffn_base_w{n}"].transpose(0, 2, 1)
        a[f"scaler{n}"] = x[f"L3_ffn_scaler_w{n}"].transpose(0, 2, 1)
    for n in ("spline", "base", "scaler"):
        w = x[f"L3_ffn_{n}_w3"].reshape(NE, C, 2, P, -1)
        a[n + "3"] = w.transpose(0, 3, 2, 4, 1).reshape(NE, P, -1)
    return a


def kernel(**inputs):
    import concourse.bacc as _bacc
    from concourse.bass_utils import run_bass_kernel_spmd as _run

    nc = _bacc.Bacc("TRN2", target_bir_lowering=False, num_devices=1)
    arrays, dram = {}, {}
    for name, v in {**laid_out({n: np.asarray(v) for n, v in inputs.items()}), **shape_constants()}.items():
        v = np.ascontiguousarray(v)
        arrays["in_" + name] = v
        dram[name] = nc.dram_tensor("in_" + name, v.shape, mybir.dt.from_np(v.dtype), kind="ExternalInput").ap()
    out = nc.dram_tensor("out_x", (B, C, S), F32, kind="ExternalOutput").ap()
    conv_attn_hybrid(nc, dram, out.rearrange("b c s -> c b s"))
    r = _run(nc, [arrays], core_ids=[0])
    return r.results[0]["out_x"].reshape(B, C, 16, 32)
```
